# Optimizing a Trainium2 kernel written in Bass

```python
import numpy as np
import jax
import jax.numpy as jnp

def _softmax(x, axis=-1):
    return jax.nn.softmax(x, axis=axis)

def _gelu(x):
    return jax.nn.gelu(x, approximate=True)

def _silu(x):
    return jax.nn.silu(x)

def _sigmoid(x):
    return jax.nn.sigmoid(x)

def _layernorm(x, axis=-1, eps=1e-05):
    m = jnp.mean(x, axis=axis, keepdims=True)
    v = jnp.var(x, axis=axis, keepdims=True)
    return (x - m) / jnp.sqrt(v + eps)

def _scatter_add(tgt, idx, src, axis=0):
    return tgt.at[idx].add(src)

def _segment_sum(src, seg, n):
    return jax.ops.segment_sum(src, seg, n)
kernel_name = 'mk_cond_resid_d4_seqx_r4_8c1319'

def setup_inputs(seed: int=0):
    np.random.seed(seed)
    _w = jnp.asarray

    def _rec_inputs():
        import jax
        import jax.numpy as jnp
        _rk = jax.random.key(seed)
        x = 8.748e-05 + 1 * jax.random.normal(jax.random.fold_in(_rk, 1), (4, 512, 512), jnp.float32)
        _lenS = 512 - jax.random.randint(jax.random.fold_in(_rk, 7), (4,), 0, max(1, 512 // 4) + 1, jnp.int32)
        _lenS2 = 512 - jax.random.randint(jax.random.fold_in(_rk, 8), (4,), 0, max(1, 512 // 4) + 1, jnp.int32)
        fside_BxSx1_0 = -0.00499425 + 1.0058 * jax.random.normal(jax.random.fold_in(_rk, 11), (4, 512, 1), jnp.float32)
        cond_2048 = 0.00513981 + 1.0024 * jax.random.normal(jax.random.fold_in(_rk, 12), (4, 512), jnp.float32)
        return (x, fside_BxSx1_0, cond_2048)
    x, fside_BxSx1_0, cond_2048 = _rec_inputs()

    def _L0_cond_setup():
        import jax, jax.numpy as jnp
        import numpy as np
        G, N, K = (16, 512, 5120)
        key = jax.random.key(seed)
        k1, k2, k3 = jax.random.split(key, 3)
        return {'emb_s': jax.random.normal(k1, (G, N, 1), dtype=jnp.float32), 'emb_t': jax.random.normal(k2, (G, 1, N), dtype=jnp.float32), 'attention_weights': jax.random.normal(k3, (G, N, N), dtype=jnp.float32), 'k': K}
    _L0_cond_all = _L0_cond_setup()
    _L0_cond_in = {k: v for k, v in _L0_cond_all.items() if k in ()}
    del _L0_cond_all

    def _L1_cond_setup():
        import jax, jax.numpy as jnp
        import numpy as np
        HEADS = 16
        EPS = 1e-06

        def _rms_norm(x, g):
            xf = x.astype(jnp.float32)
            y = xf * jax.lax.rsqrt(jnp.mean(xf * xf, axis=-1, keepdims=True) + EPS)
            return y.astype(x.dtype) * g
        key = jax.random.key(seed)
        ks = jax.random.split(key, 6)
        b, n, dim, emb_dim = (4, 512, 512, 512)
        d_head = dim // HEADS
        return {'x': jax.random.normal(ks[0], (b, n, dim), jnp.float32), 'emb': jax.random.normal(ks[1], (b, 1, emb_dim), jnp.float32), 'W_emb': jax.random.normal(ks[2], (emb_dim, 2 * dim), jnp.float32) * emb_dim ** (-0.5), 'b_emb': jnp.zeros((2 * dim,), jnp.float32), 'g_norm': jnp.ones((dim,), jnp.float32), 'W_qkv': jax.random.normal(ks[3], (dim, 3 * dim), jnp.float32) * dim ** (-0.5), 'g_q': jnp.ones((d_head,), jnp.float32), 'g_k': jnp.ones((d_head,), jnp.float32), 'W_out': jax.random.normal(ks[4], (dim, dim), jnp.float32) * dim ** (-0.5)}
    _L1_cond_all = _L1_cond_setup()
    _L1_cond_in = {k: v for k, v in _L1_cond_all.items() if k in ('W_emb', 'b_emb', 'g_norm', 'W_qkv', 'g_q', 'g_k', 'W_out')}
    del _L1_cond_all

    def _L2_cond_setup():
        import jax, jax.numpy as jnp
        import numpy as np
        B, T, D = (16, 128, 512)
        key = jax.random.key(seed)
        k0, k1, k2, k3 = jax.random.split(key, 4)
        scale = 1.0 / np.sqrt(D)
        return {'initial_state': jax.random.normal(k0, (B, D), jnp.float32), 'inputs': jax.random.normal(k1, (B, T, D), jnp.float32), 'W_ih': jax.random.normal(k2, (D, 3 * D), jnp.float32) * scale, 'W_hh': jax.random.normal(k3, (D, 3 * D), jnp.float32) * scale, 'b_ih': jnp.zeros((3 * D,), jnp.float32), 'b_hh': jnp.zeros((3 * D,), jnp.float32)}
    _L2_cond_all = _L2_cond_setup()
    _L2_cond_in = {k: v for k, v in _L2_cond_all.items() if k in ('W_ih', 'W_hh', 'b_ih', 'b_hh')}
    del _L2_cond_all

    def _L3_cond_setup():
        import jax, jax.numpy as jnp
        import numpy as np
        DIM = 512
        H = 16
        DH = 128
        INNER = H * DH
        MLP = 4 * DIM
        B, T = (2, 512)
        EPS = 1e-06

        def _ln(x):
            mu = jnp.mean(x, axis=-1, keepdims=True)
            var = jnp.var(x, axis=-1, keepdims=True)
            return (x - mu) * jax.lax.rsqrt(var + EPS)
        key = jax.random.key(seed)
        ks = jax.random.split(key, 12)
        s = 0.02
        return {'x': jax.random.normal(ks[0], (B, T, DIM), jnp.float32), 'timestep_embed': jax.random.normal(ks[1], (B, DIM), jnp.float32), 'ada_w': jax.random.normal(ks[2], (DIM, 6 * DIM), jnp.float32) * s, 'ada_b': jnp.zeros((6 * DIM,), jnp.float32), 'qkv_w': jax.random.normal(ks[3], (DIM, 3 * INNER), jnp.float32) * s, 'qkv_b': jnp.zeros((3 * INNER,), jnp.float32), 'out_w': jax.random.normal(ks[4], (INNER, DIM), jnp.float32) * s, 'out_b': jnp.zeros((DIM,), jnp.float32), 'ffn_w1': jax.random.normal(ks[5], (DIM, MLP), jnp.float32) * s, 'ffn_b1': jnp.zeros((MLP,), jnp.float32), 'ffn_w2': jax.random.normal(ks[6], (MLP, DIM), jnp.float32) * s, 'ffn_b2': jnp.zeros((DIM,), jnp.float32)}
    _L3_cond_all = _L3_cond_setup()
    _L3_cond_in = {k: v for k, v in _L3_cond_all.items() if k in ('ada_w', 'ada_b', 'qkv_w', 'qkv_b', 'out_w', 'out_b', 'ffn_w1', 'ffn_b1', 'ffn_w2', 'ffn_b2')}
    del _L3_cond_all
    return {'x': x, 'fside_BxSx1_0': fside_BxSx1_0, 'cond_2048': cond_2048, 'L1_cond_W_emb': _L1_cond_in['W_emb'], 'L1_cond_b_emb': _L1_cond_in['b_emb'], 'L1_cond_g_norm': _L1_cond_in['g_norm'], 'L1_cond_W_qkv': _L1_cond_in['W_qkv'], 'L1_cond_g_q': _L1_cond_in['g_q'], 'L1_cond_g_k': _L1_cond_in['g_k'], 'L1_cond_W_out': _L1_cond_in['W_out'], 'L2_cond_W_ih': _L2_cond_in['W_ih'], 'L2_cond_W_hh': _L2_cond_in['W_hh'], 'L2_cond_b_ih': _L2_cond_in['b_ih'], 'L2_cond_b_hh': _L2_cond_in['b_hh'], 'L3_cond_ada_w': _L3_cond_in['ada_w'], 'L3_cond_ada_b': _L3_cond_in['ada_b'], 'L3_cond_qkv_w': _L3_cond_in['qkv_w'], 'L3_cond_qkv_b': _L3_cond_in['qkv_b'], 'L3_cond_out_w': _L3_cond_in['out_w'], 'L3_cond_out_b': _L3_cond_in['out_b'], 'L3_cond_ffn_w1': _L3_cond_in['ffn_w1'], 'L3_cond_ffn_b1': _L3_cond_in['ffn_b1'], 'L3_cond_ffn_w2': _L3_cond_in['ffn_w2'], 'L3_cond_ffn_b2': _L3_cond_in['ffn_b2']}

def reference(x, fside_BxSx1_0, cond_2048, L1_cond_W_emb, L1_cond_b_emb, L1_cond_g_norm, L1_cond_W_qkv, L1_cond_g_q, L1_cond_g_k, L1_cond_W_out, L2_cond_W_ih, L2_cond_W_hh, L2_cond_b_ih, L2_cond_b_hh, L3_cond_ada_w, L3_cond_ada_b, L3_cond_qkv_w, L3_cond_qkv_b, L3_cond_out_w, L3_cond_out_b, L3_cond_ffn_w1, L3_cond_ffn_b1, L3_cond_ffn_w2, L3_cond_ffn_b2):
    import jax
    import jax.numpy as jnp

    def _L0_cond_ref(emb_s, emb_t, attention_weights, k):
        import jax, jax.numpy as jnp
        import numpy as np
        G, N, K = (16, 512, 5120)
        g, n = (emb_s.shape[0], emb_s.shape[1])
        adj = emb_s * emb_t
        att = jax.nn.softmax(attention_weights, axis=-1) * (1.0 / np.sqrt(n).astype(np.float32))
        adj = adj * att
        diag = jnp.arange(n)
        adj = adj.at[:, diag, diag].set(-jnp.inf)
        flat = adj.reshape(g, n * n)
        _, idx = jax.lax.top_k(flat, k)
        rows = jnp.arange(g)[:, None]
        out = jnp.zeros((g, n * n), dtype=adj.dtype).at[rows, idx].set(1.0)
        return out.reshape(g, n, n)

    def _L1_cond_ref(x, emb, W_emb, b_emb, g_norm, W_qkv, g_q, g_k, W_out):
        import jax, jax.numpy as jnp
        import numpy as np
        HEADS = 16
        EPS = 1e-06

        def _rms_norm(x, g):
            xf = x.astype(jnp.float32)
            y = xf * jax.lax.rsqrt(jnp.mean(xf * xf, axis=-1, keepdims=True) + EPS)
            return y.astype(x.dtype) * g
        b, n, dim = x.shape
        h = HEADS
        d = dim // h
        scale_shift = emb @ W_emb + b_emb
        scale, shift = jnp.split(scale_shift, 2, axis=-1)
        xn = _rms_norm(x, g_norm) * (1.0 + scale) + shift
        qkv = xn @ W_qkv
        qkv = qkv.reshape(b, n, 3, h, d)
        q, k, v = jnp.moveaxis(qkv, 2, 0)
        q = jnp.swapaxes(q, 1, 2)
        k = jnp.swapaxes(k, 1, 2)
        v = jnp.swapaxes(v, 1, 2)
        q = _rms_norm(q, g_q)
        k = _rms_norm(k, g_k)
        logits = jnp.einsum('bhqd,bhkd->bhqk', q, k) * d ** (-0.5)
        attn = jax.nn.softmax(logits, axis=-1)
        o = jnp.einsum('bhqk,bhkd->bhqd', attn, v)
        o = jnp.swapaxes(o, 1, 2).reshape(b, n, dim)
        return o + o @ W_out

    def _L2_cond_ref(initial_state, inputs, W_ih, W_hh, b_ih, b_hh):
        import jax, jax.numpy as jnp
        import numpy as np
        B, T, D = (16, 128, 512)
        "ScanOverTime(GRU cell): sequential per-timestep module call with\n            dict-state passing; merge_dict_trees stacks the per-step\n            'state_predicted' tensors along axis=1 -> [B, T, D]."

        def cell(h, x):
            gi = x @ W_ih + b_ih
            gh = h @ W_hh + b_hh
            i_r, i_z, i_n = jnp.split(gi, 3, axis=-1)
            h_r, h_z, h_n = jnp.split(gh, 3, axis=-1)
            r = jax.nn.sigmoid(i_r + h_r)
            z = jax.nn.sigmoid(i_z + h_z)
            n = jnp.tanh(i_n + r * h_n)
            h_new = (1.0 - z) * n + z * h
            return (h_new, h_new)
        xs = jnp.swapaxes(inputs, 0, 1)
        _, hs = jax.lax.scan(cell, initial_state, xs)
        return jnp.swapaxes(hs, 0, 1)

    def _L3_cond_ref(x, timestep_embed, ada_w, ada_b, qkv_w, qkv_b, out_w, out_b, ffn_w1, ffn_b1, ffn_w2, ffn_b2):
        import jax, jax.numpy as jnp
        import numpy as np
        DIM = 512
        H = 16
        DH = 128
        INNER = H * DH
        MLP = 4 * DIM
        B, T = (2, 512)
        EPS = 1e-06

        def _ln(x):
            mu = jnp.mean(x, axis=-1, keepdims=True)
            var = jnp.var(x, axis=-1, keepdims=True)
            return (x - mu) * jax.lax.rsqrt(var + EPS)
        Bc, Tc, D = x.shape
        ada = (timestep_embed @ ada_w + ada_b)[:, None, :]
        shift1, scale1, gate1, shift2, scale2, gate2 = jnp.split(ada, 6, axis=-1)
        x1 = _ln(x) * (1.0 + scale1) + shift1
        qkv = (x1 @ qkv_w + qkv_b).reshape(Bc, Tc, 3, H, DH)
        q, k, v = (qkv[:, :, 0], qkv[:, :, 1], qkv[:, :, 2])
        scale = DH ** (-0.5)
        attn = jnp.einsum('bthd,bshd->bhts', q, k) * scale
        attn = jax.nn.softmax(attn, axis=-1)
        attn_out = jnp.einsum('bhts,bshd->bthd', attn, v).reshape(Bc, Tc, INNER)
        attn_out = attn_out @ out_w + out_b
        x = x + gate1 * attn_out
        x2 = _ln(x) * (1.0 + scale2) + shift2
        h = jax.nn.gelu(x2 @ ffn_w1 + ffn_b1, approximate=False)
        x = x + gate2 * (h @ ffn_w2 + ffn_b2)
        return x
    x = x + _L0_cond_ref(fside_BxSx1_0, cond_2048[:, None, :], x, 5120)
    x = x + _L1_cond_ref(x, cond_2048[:, None, :], L1_cond_W_emb, L1_cond_b_emb, L1_cond_g_norm, L1_cond_W_qkv, L1_cond_g_q, L1_cond_g_k, L1_cond_W_out)
    x = x + _L2_cond_ref(cond_2048, x, L2_cond_W_ih, L2_cond_W_hh, L2_cond_b_ih, L2_cond_b_hh)
    x = x + _L3_cond_ref(x, cond_2048, L3_cond_ada_w, L3_cond_ada_b, L3_cond_qkv_w, L3_cond_qkv_b, L3_cond_out_w, L3_cond_out_b, L3_cond_ffn_w1, L3_cond_ffn_b1, L3_cond_ffn_w2, L3_cond_ffn_b2)
    return x

_drawn_inputs = setup_inputs


def setup_inputs(seed=0):
    import zlib

    import numpy as np

    out = dict(_drawn_inputs(seed))
    spreads = {'L1_cond_b_emb': (0.0, 0.1),
     'L1_cond_g_norm': (1.0, 0.2),
     'L1_cond_g_q': (1.0, 0.6),
     'L1_cond_g_k': (1.0, 0.6),
     'L2_cond_b_ih': (0.0, 0.295),
     'L2_cond_b_hh': (0.0, 0.485),
     'L3_cond_ada_b': (0.0, 0.461),
     'L3_cond_qkv_b': (0.0, 0.785),
     'L3_cond_out_b': (0.0, 0.699),
     'L3_cond_ffn_b1': (0.0, 0.8),
     'L3_cond_ffn_b2': (0.0, 0.656)}
    factors = {}
    for name, (base, spread) in spreads.items():
        noise = np.random.default_rng([zlib.crc32(name.encode()), seed]).standard_normal(out[name].shape)
        drawn = base * np.exp(spread * noise) if base else spread * noise
        out[name] = jnp.asarray(drawn.astype(out[name].dtype))
    for name, factor in factors.items():
        out[name] = (out[name] * factor).astype(out[name].dtype)
    return out
```

```python
from contextlib import ExitStack

import concourse.bass as bass
from concourse import mybir

F32 = mybir.dt.float32
F16 = mybir.dt.float16
I32 = mybir.dt.int32
I16 = mybir.dt.int16
U16 = mybir.dt.uint16
ALU = mybir.AluOpType
ACT = mybir.ActivationFunctionType
AX = mybir.AxisListType

P = 128
B, T, D = 4, 512, 512
TT = T // P
NT = B * TT
KD = D // P
TOPK = 5120

DIT_H, DIT_DH = 16, 128
INNER = DIT_H * DIT_DH
MLP = 4 * D
DIT_EPS = 1e-6
LAST_PHASE = 4


class Mem:

    def __init__(self, nc, ctx, phase=""):
        self.nc, self.ctx, self.phase = nc, ctx, phase
        self.sems = []

    def sb(self, name, shape, dt=F32):
        return self.ctx.enter_context(self.nc.sbuf_tensor(self.phase + name, shape, dt))

    def ps(self, name, shape, dt=F32):
        return self.ctx.enter_context(self.nc.psum_tensor(self.phase + name, shape, dt))

    def sem(self, name):
        if not self.sems:
            self.ctx.callback(self.clear)
        self.sems.append(self.nc.alloc_semaphore(name=self.phase + name))
        return self.sems[-1]

    def clear(self):
        self.nc.clear_and_free_semaphores(self.sems)
        self.nc.all_engine_barrier()


def at(i, n=1):
    return bass.ds(i, n)


def topk_phase(nc, X, const, x_in, side, cond):
    E = T * D // P
    with ExitStack() as ctx:
        m = Mem(nc, ctx, "edge_")
        adj = m.sb("adj", [P, NT, D])
        key = m.sb("key", [P, NT, D], I32)
        hi = m.sb("key_hi", [P, B, E], I16)
        lo = m.sb("key_lo", [P, B, E], U16)
        mask = m.sb("mask", [P, B, E], F16)
        embt = m.sb("embt", [P, B, D])
        rank = m.sb("rank", [P, 2, D])
        zeros = m.sb("zeros", [P, D])
        fs = m.sb("fs", [P, NT])
        nmax = m.sb("nmax", [P, NT])
        rsum = m.sb("rsum", [P, NT])
        rinv = m.sb("rinv", [P, NT])
        rscale = m.sb("rscale", [P, NT])
        digit = m.sb("digit", [P, 17])
        found = m.sb("found", [P, 2, B])
        cand = m.sb("cand", [P, B])
        want = m.sb("want", [P, B])
        ge = m.sb("ge", [P, B])
        part16 = m.sb("part16", [P, B], F16)
        halves = m.sb("halves", [P, 2, B], I32)
        tkey = m.sb("tkey", [P, B], I32)
        tsign = m.sb("tsign", [P, B], I32)
        thr = m.sb("thr", [P, B], I32)
        ties = m.sb("ties", [P, NT])
        before = m.sb("before", [P, NT])
        part = m.ps("part", [P, B])
        total = m.ps("total", [P, B])
        pref = m.ps("pref", [P, B, TT])

        x_loaded = m.sem("x_loaded")
        side_loaded = m.sem("side_loaded")
        max_ready = m.sem("max_ready")
        exp_done = m.sem("exp_done")
        adj_done = m.sem("adj_done")
        diag_done = m.sem("diag_done")
        mask_ready = m.sem("mask_ready")
        part_ready = m.sem("part_ready")
        part_copied = m.sem("part_copied")
        total_ready = m.sem("total_ready")
        ties_counted = m.sem("ties_counted")
        pref_ready = m.sem("pref_ready")
        dv = m.sem("topk_dve")

        block = ctx.enter_context(nc.Block())

        @block.sync
        def _(sp):
            sp.dma_start(X[:], x_in.rearrange("b (t p) d -> p (b t) d", p=P)).then_inc(x_loaded, 16)
            sp.dma_start(fs[:], side).then_inc(side_loaded, 16)
            sp.dma_start(embt[:], cond.rearrange("(o b) d -> o b d", o=1).broadcast_to([P, B, D])).then_inc(side_loaded, 16)

        @block.scalar
        def _(act):
            act.wait_ge(max_ready, 1)
            with act.Fori(0, NT) as n:
                act.activation(adj[:, at(n), :], X[:, at(n), :], ACT.Exp, bias=nmax[:, at(n)],
                               accum_out=rsum[:, at(n)]).then_inc(exp_done, 1)

        @block.gpsimd
        def _(pool):
            pool.wait_ge(adj_done, NT)
            for t in range(TT):
                v = adj[:].rearrange("p (b t) d -> p b t d", t=TT)[:, :, t, t * P:(t + 1) * P]
                pool.affine_select(out=v, in_=v, compare_op=ALU.not_equal, fill=-3.0e38, base=0,
                                   pattern=[[0, B], [-1, P]], channel_multiplier=1).then_inc(diag_done, 1)

        PASSES = 2 * 17

        @block.tensor
        def _(pe):
            with pe.Fori(0, PASSES) as i:
                for b in range(B):
                    pe.wait_ge(mask_ready, i * B + (b + 1))
                    for j in range(E // P):
                        mm = pe.matmul(part[:, b:b + 1], mask[:, b, j * P:(j + 1) * P], const["ones16"][:, 0:1],
                                       start=(j == 0), stop=(j == E // P - 1))
                mm.then_inc(part_ready, 1)
                pe.wait_ge(part_copied, i + 1)
                pe.matmul(total[:], const["ones16"][:], part16[:], start=True, stop=True).then_inc(total_ready, 1)
            pe.wait_ge(ties_counted, NT)
            tv = ties[:].rearrange("p (b t) -> p b t", t=TT)
            pe.matmul(pref[:], const["below"][:], tv, start=True, stop=False)
            for s in range(1, TT):
                mm = pe.matmul(pref[:, :, s:TT], const["ones32"][:], tv[:, :, 0:TT - s], start=False, stop=(s == TT - 1))
            mm.then_inc(pref_ready, 1)

        @block.vector
        def _(dve):
            n_dv = [0]

            def step(ins):
                ins.then_inc(dv, 1)
                n_dv[0] += 1
                dve.wait_ge(dv, n_dv[0])

            for k in range(17):
                dve.memset(digit[:, k:k + 1], float(1 << max(15 - k, 0)))
            dve.memset(want[:], float(TOPK))
            dve.memset(found[:, 0, :], -32768.0)
            dve.memset(found[:, 1, :], 0.0)
            dve.memset(cand[:], 0.0)
            dve.memset(zeros[:], 0.0)
            dve.wait_ge(x_loaded, 16)
            dve.tensor_reduce(nmax[:], X[:], AX.X, ALU.max, negate=True).then_inc(max_ready, 1)
            dve.wait_ge(exp_done, NT)
            step(dve.reciprocal(rinv[:], rsum[:]))
            dve.wait_ge(side_loaded, 32)
            step(dve.scalar_tensor_tensor(out=rscale[:], in0=rinv[:], scalar=float(D) ** -0.5, in1=fs[:],
                                          op0=ALU.mult, op1=ALU.mult))
            with dve.Fori(0, B) as b:
                for t in range(TT):
                    a = adj[:, at(b * TT + t), :].rearrange("p o d -> p (o d)")
                    dve.scalar_tensor_tensor(out=a, in0=a, scalar=rscale[:, at(b * TT + t)],
                                             in1=embt[:, at(b), :].rearrange("p o d -> p (o d)"),
                                             op0=ALU.mult, op1=ALU.mult).then_inc(adj_done, 1)
            dve.wait_ge(diag_done, TT)
            bits = adj[:].bitcast(I32)
            step(dve.tensor_scalar(key[:], bits, 31, 0x7FFFFFFF, ALU.arith_shift_right, ALU.bitwise_and))
            step(dve.tensor_tensor(key[:], key[:], bits, ALU.bitwise_xor))
            k16 = key[:].rearrange("p n d -> p (n d)").bitcast(I16).rearrange("p (e two) -> p e two", two=2)
            dve.tensor_copy(hi[:].rearrange("p b e -> p (b e)"), k16[:, :, 1])
            step(dve.tensor_copy(lo[:].rearrange("p b e -> p (b e)"), k16[:, :, 0].bitcast(U16)))

            for half, src in enumerate((hi, lo)):
                T_ = found[:, half, :]
                base = n_dv[0]
                p0 = half * 17

                def count(i):
                    for b in range(B):
                        dve.tensor_scalar(mask[:, b, :], src[:, b, :], cand[:, b:b + 1], None,
                                          ALU.is_ge).then_inc(mask_ready, 1)
                    dve.wait_ge(part_ready, i + 1)
                    dve.tensor_copy(part16[:], part[:]).then_inc(part_copied, 1)
                    dve.wait_ge(total_ready, i + 1)

                with dve.Fori(0, 16) as k:
                    c = k * 3 + base
                    count(k + p0)
                    dve.tensor_tensor(ge[:], total[:], want[:], ALU.is_ge).then_inc(dv, 1)
                    dve.wait_ge(dv, c + 1)
                    dve.scalar_tensor_tensor(out=T_, in0=ge[:], scalar=digit[:, at(k)], in1=T_,
                                             op0=ALU.mult, op1=ALU.add).then_inc(dv, 1)
                    dve.wait_ge(dv, c + 2)
                    dve.tensor_scalar(cand[:], T_, digit[:, at(k + 1)], None, ALU.add).then_inc(dv, 1)
                    dve.wait_ge(dv, c + 3)
                n_dv[0] += 48
                count(16 + p0)
                step(dve.tensor_tensor(want[:], want[:], total[:], ALU.subtract))
                if half == 0:
                    dve.memset(cand[:], 32768.0)
                    for b in range(B):
                        ins = dve.scalar_tensor_tensor(out=lo[:, b, :], in0=hi[:, b, :], scalar=found[:, 0, b:b + 1],
                                                       in1=lo[:, b, :], op0=ALU.is_equal, op1=ALU.mult)
                    step(ins)

            step(dve.tensor_copy(halves[:], found[:]))
            step(dve.tensor_scalar(halves[:, 0, :], halves[:, 0, :], 16, None, ALU.logical_shift_left))
            step(dve.tensor_tensor(tkey[:], halves[:, 0, :], halves[:, 1, :], ALU.bitwise_or))
            step(dve.tensor_scalar(tsign[:], tkey[:], 31, 0x7FFFFFFF, ALU.arith_shift_right, ALU.bitwise_and))
            step(dve.tensor_tensor(thr[:], tkey[:], tsign[:], ALU.bitwise_xor))
            thrf = thr[:].bitcast(F32)
            eq = key[:].bitcast(F32)
            with dve.Fori(0, B) as b:
                for t in range(TT):
                    n = b * TT + t
                    dve.tensor_scalar(eq[:, at(n), :], adj[:, at(n), :], thrf[:, at(b)], None,
                                      ALU.is_equal, ALU.add, accum_out=ties[:, at(n)]).then_inc(ties_counted, 1)
            dve.wait_ge(pref_ready, 1)
            step(dve.tensor_copy(before[:].rearrange("p (b t) -> p b t", t=TT), pref[:]))
            base = n_dv[0]
            with dve.Fori(0, B) as b:
                for t in range(TT):
                    n = b * TT + t
                    c = n * 3 + base
                    r = rank[:, t % 2, :]
                    flat = lambda v: v.rearrange("p o d -> p (o d)")
                    xs, es = flat(X[:, at(n), :]), flat(eq[:, at(n), :])
                    dve.tensor_tensor_scan(r, es, zeros[:], before[:, at(n)], ALU.add, ALU.add).then_inc(dv, 1)
                    dve.scalar_tensor_tensor(out=xs, in0=flat(adj[:, at(n), :]), scalar=thrf[:, at(b)], in1=xs,
                                             op0=ALU.is_gt, op1=ALU.add)
                    dve.wait_ge(dv, c + 1)
                    dve.scalar_tensor_tensor(out=r, in0=r, scalar=want[:, at(b)], in1=es,
                                             op0=ALU.is_le, op1=ALU.mult).then_inc(dv, 1)
                    dve.wait_ge(dv, c + 2)
                    dve.tensor_tensor(xs, xs, r, ALU.add).then_inc(dv, 1)
            n_dv[0] += 3 * NT


XS = 8.0
WS = 32.0
UNSCALE = 1.0 / (XS * WS)


def flat(v):
    return v.rearrange("p o d -> p (o d)")


def products(pe, out, left, right, start, stop):
    (lh, ll), (rh, rl) = left, right
    pe.matmul(out, lh, rh, start=start, stop=False)
    pe.matmul(out, lh, rl, start=False, stop=False)
    return pe.matmul(out, ll, rh, start=False, stop=stop)


def split_weights(nc, name, jobs):
    WIDE = 2048
    pieces = []
    for src, hi, lo, scale in jobs:
        n = src.shape[2]
        for a in range(src.shape[1]):
            for c in range(0, n, WIDE):
                w = min(WIDE, n - c)
                pieces.append((src[:, a, c:c + w], hi[:, a, c:c + w], lo[:, a, c:c + w], w, scale))
    SLOTS = 3
    with ExitStack() as ctx:
        m = Mem(nc, ctx, name)
        stage = m.sb("w_stage", [P, SLOTS, WIDE])
        loaded = [m.sem(f"w_loaded_{s}") for s in range(SLOTS)]
        hi_done, lo_done = m.sem("w_hi_done"), m.sem("w_lo_done")
        block = ctx.enter_context(nc.Block())

        @block.sync
        def _(sp):
            for j, (src, _, _, w, _) in enumerate(pieces):
                if j >= SLOTS:
                    sp.wait_ge(lo_done, j - SLOTS + 1)
                sp.dma_start(stage[:, j % SLOTS, 0:w], src).then_inc(loaded[j % SLOTS], 16)

        @block.scalar
        def _(act):
            for j, (_, hi, _, w, scale) in enumerate(pieces):
                act.wait_ge(loaded[j % SLOTS], 16 * (j // SLOTS + 1))
                act.activation(hi, stage[:, j % SLOTS, 0:w], ACT.Copy, scale=scale).then_inc(hi_done, 1)

        @block.vector
        def _(dve):
            for j, (_, hi, lo, w, scale) in enumerate(pieces):
                dve.wait_ge(hi_done, j + 1)
                dve.scalar_tensor_tensor(out=lo, in0=stage[:, j % SLOTS, 0:w], scalar=scale, in1=hi, op0=ALU.mult,
                                         op1=ALU.subtract).then_inc(lo_done, 1)


class Heads:

    CREDIT = 2

    def __init__(self, m, S, PT, O, ident, scores, values, out, scale, parts):
        self.S, self.PT, self.O, self.ident = S, PT, O, ident
        self.scores, self.values, self.out, self.scale, self.parts = scores, values, out, scale, parts
        self.prob = m.sb("prob", [P, 2, D])
        self.turned = m.sb("turned", [P, 2, 2, TT, P], F16) if parts else m.sb("turned", [P, 2, TT, P])
        self.nmax = m.sb("head_nmax", [P, TT])
        self.nbias = m.sb("head_nbias", [P, TT])
        self.rsum = m.sb("head_rsum", [P, TT])
        self.rinv = m.sb("head_rinv", [P, TT])
        self.scores_ready = m.sem("scores_ready")
        self.max_raw = m.sem("max_raw")
        self.max_ready = m.sem("max_ready")
        self.exp_done = m.sem("exp_done")
        self.turn_ready = m.sem("turn_ready")
        self.copied_a = m.sem("copied_by_act")
        self.copied_v = m.sem("copied_by_dve")
        self.pv_ready = m.sem("pv_ready")
        self.rinv_ready = m.sem("rinv_ready")
        self.out_copied = m.sem("out_copied")

    def credits(self, pool):
        for s in (self.exp_done, self.turn_ready, self.copied_a, self.copied_v, self.pv_ready, self.out_copied):
            pool.sem_inc(s, self.CREDIT)

    def pe_scores(self, pe, h, t, u):
        pe.wait_ge(self.exp_done, u + 1)
        self.scores(pe, self.S[t % 2], h, t).then_inc(self.scores_ready, 1)

    def pe_wait_copy(self, pe, t, u, ahead):
        if self.parts:
            pe.wait_ge(self.copied_a, u + 1 + ahead)
            pe.wait_ge(self.copied_v, u + 1 + ahead)
        elif t % 2 == 0:
            pe.wait_ge(self.copied_a, u + 2 + ahead)
        else:
            pe.wait_ge(self.copied_v, u + 1 + ahead)

    def pe_turn(self, pe, t, u):
        pe.wait_ge(self.exp_done, u + 1 + self.CREDIT)
        self.pe_wait_copy(pe, t, u, 0)
        for s in range(TT):
            mm = pe.transpose(self.PT[t % 2][:, s * P:(s + 1) * P], self.prob[:, t % 2, s * P:(s + 1) * P],
                              self.ident)
        mm.then_inc(self.turn_ready, 1)

    def pe_values(self, pe, h, t, u):
        self.pe_wait_copy(pe, t, u, self.CREDIT)
        pe.wait_ge(self.out_copied, u + 1)
        for s in range(TT):
            if self.parts:
                mm = products(pe, self.O[t % 2], (self.turned[:, t % 2, 0, s, :], self.turned[:, t % 2, 1, s, :]),
                              self.values(h, s), s == 0, s == TT - 1)
            else:
                mm = pe.matmul(self.O[t % 2], self.turned[:, t % 2, s, :], self.values(h, s), start=(s == 0),
                               stop=(s == TT - 1))
        mm.then_inc(self.pv_ready, 1)

    def act_exp(self, act, t, u):
        act.wait_ge(self.max_ready, u + 1)
        act.wait_ge(self.turn_ready, u + 1)
        bias = self.nmax if self.scale == 1.0 else self.nbias
        act.activation(self.prob[:, t % 2, :], self.S[t % 2], ACT.Exp, bias=bias[:, t:t + 1], scale=self.scale,
                       accum_out=self.rsum[:, t:t + 1]).then_inc(self.exp_done, 1)

    def act_copy(self, act, t, u):
        if not self.parts and t % 2 == 1:
            return
        act.wait_ge(self.turn_ready, u + 1 + self.CREDIT)
        act.wait_ge(self.pv_ready, u + 1)
        if self.parts:
            act.activation(self.turned[:, t % 2, 0].rearrange("p s q -> p (s q)"), self.PT[t % 2], ACT.Copy)\
               .then_inc(self.copied_a, 1)
        else:
            act.activation(self.turned[:, t % 2].rearrange("p s q -> p (s q)"), self.PT[t % 2], ACT.Copy)\
               .then_inc(self.copied_a, 2)

    def dve_max(self, dve, t, u):
        dve.wait_ge(self.scores_ready, u + 1)
        ins = dve.tensor_reduce(self.nmax[:, t:t + 1], self.S[t % 2], AX.X, ALU.max, negate=True)
        if self.scale == 1.0:
            ins.then_inc(self.max_ready, 1)
        else:
            ins.then_inc(self.max_raw, 1)
            dve.wait_ge(self.max_raw, u + 1)
            dve.tensor_scalar(self.nbias[:, t:t + 1], self.nmax[:, t:t + 1], self.scale, None, ALU.mult)\
               .then_inc(self.max_ready, 1)

    def dve_copy(self, dve, t, u):
        dve.wait_ge(self.exp_done, u + 1 + self.CREDIT)
        dve.reciprocal(self.rinv[:, t:t + 1], self.rsum[:, t:t + 1]).then_inc(self.rinv_ready, 1)
        if self.parts:
            dve.wait_ge(self.copied_a, u + 1 + self.CREDIT)
            dve.tensor_tensor(self.turned[:, t % 2, 1].rearrange("p s q -> p (s q)"), self.PT[t % 2],
                              self.turned[:, t % 2, 0].rearrange("p s q -> p (s q)"), ALU.subtract)\
               .then_inc(self.copied_v, 1)
        elif t % 2 == 1:
            dve.wait_ge(self.turn_ready, u + 1 + self.CREDIT)
            dve.wait_ge(self.pv_ready, u + 1)
            dve.tensor_copy(self.turned[:, t % 2].rearrange("p s q -> p (s q)"), self.PT[t % 2])\
               .then_inc(self.copied_v, 2)

    def dve_out(self, dve, h, t, u):
        dve.wait_ge(self.pv_ready, u + 1 + self.CREDIT)
        dve.wait_ge(self.rinv_ready, u + 1)
        dve.tensor_scalar(self.out(h, t), self.O[t % 2], self.rinv[:, t:t + 1], None, ALU.mult)\
           .then_inc(self.out_copied, 1)

    def run(self, eng, heads, first_unit, current, turn, done, beside=None):
        def head(h, first, last):
            u0 = first_unit + h * TT
            for t in range(TT):
                current(h, t, u0 + t)
                if beside is not None:
                    beside(h, t, last)
                if not (first and t < 1):
                    turn(h if t >= 1 else h - 1, (t - 1) % TT, u0 + (t - 1))
                if not (first and t < 2):
                    done(h if t >= 2 else h - 1, (t - 2) % TT, u0 + (t - 2))

        self.parity, self.nth = 0, 1
        head(0, True, False)
        with eng.Fori(0, (heads - 2) // 2) as pair:
            for self.parity in (1, 0):
                self.nth = pair + 2
                head(pair * 2 + (2 - self.parity), False, False)
        self.parity = 1
        head(heads - 1, False, True)
        end = first_unit + heads * TT
        turn(heads - 1, TT - 1, end - 1)
        done(heads - 1, TT - 2, end - 2)
        done(heads - 1, TT - 1, end - 1)


def small_attention_phase(nc, X, const, a, W, Wo):
    H, DH = 16, 32
    EPS = 1e-6
    w_qkv, w_out = W, Wo
    with ExitStack() as ctx:
        m = Mem(nc, ctx, "small_")
        c_T = m.sb("cond_T", [P, KD, B])
        b_emb = m.sb("b_emb", [P, 2 * KD])
        g_norm = m.sb("g_norm", [P, KD])
        g_qk = m.sb("g_qk", [P, 2, DH])
        gg = m.sb("gg", [P, 1, DH])
        mod = m.sb("mod", [P, 2 * KD, B])
        ss = m.sb("ss", [P, NT])
        rstd = m.sb("rstd", [P, NT])
        tmp = m.sb("tmp", [P, 2, D])
        xn = m.sb("xn", [P, TT, D])
        y32 = m.sb("y32", [P, KD, T])
        yh, yl = m.sb("yh", [P, KD, T], F16), m.sb("yl", [P, KD, T], F16)
        raw = m.sb("raw", [P, TT, 2, D])
        w_emb = raw[:].rearrange("p t a d -> p t (a d)")
        V = m.sb("V", [P, TT, D])
        ssq = m.sb("ssq", [P, TT, 2 * H])
        rq = m.sb("rq", [P, TT, 2 * H])
        q4, k4 = m.sb("q4", [P, TT, H, 4, DH], F16), m.sb("k4", [P, TT, H, 4, DH], F16)
        qT, kT = m.sb("qT", [P, H, T], F16), m.sb("kT", [P, H, T], F16)
        O = y32
        oh, ol = yh, yl
        bank = [m.ps(f"bank{i}", [P, D]) for i in range(6)]
        q_bank = [m.ps(f"qbank{i}", [P, T], F16) for i in range(2)]

        cond_loaded = m.sem("cond_loaded")
        mod_sum = m.sem("mod_sum")
        mod_ready = m.sem("mod_ready")
        sq_done = m.sem("sq_done")
        ms_ready = m.sem("ms_ready")
        root_done = m.sem("root_done")
        rstd_ready = m.sem("rstd_ready")
        gg_ready = m.sem("gg_ready")
        xn_ready = m.sem("xn_ready")
        xT_ready = m.sem("xT_ready")
        y_ready = m.sem("y_ready")
        yh_ready = m.sem("yh_ready")
        yl_ready = m.sem("yl_ready")
        qkv_ready = m.sem("qkv_ready")
        square_ready = m.sem("square_ready")
        ssq_ready = m.sem("ssq_ready")
        hms_ready = m.sem("hms_ready")
        hroot_done = m.sem("hroot_done")
        rq_ready = m.sem("rq_ready")
        normed = m.sem("normed")
        q_gained = m.sem("q_gained")
        hi4_done = m.sem("hi4_done")
        lo4_done = m.sem("lo4_done")
        qk_turned = m.sem("qk_turned")
        q_copied = m.sem("q_copied")
        k_copied = m.sem("k_copied")
        o_turned = m.sem("o_turned")
        oh_ready = m.sem("oh_ready")
        ol_ready = m.sem("ol_ready")
        y_out = m.sem("y_out")
        y_added = m.sem("y_added")
        x_added = m.sem("x_added")
        bank_free = m.sem("bank_free")

        hs = Heads(
            m, S=[bank[0][:], bank[1][:]], PT=[bank[2][:], bank[3][:]], O=[bank[4][:, 0:DH], bank[5][:, 0:DH]],
            ident=const["ident"][:],
            scores=lambda pe, s, h, t: pe.matmul(s, flat(qT[:, at(h), t * P:(t + 1) * P]), flat(kT[:, at(h), :]),
                                                 start=True, stop=True),
            values=lambda h, s: V[:, s, at(h * DH, DH)],
            out=lambda h, t: O[:, t, at(h * DH, DH)],
            scale=1.0, parts=False)
        qkv_bank = bank[4:6]

        block = ctx.enter_context(nc.Block())

        @block.sync
        def _(sp):
            sp.dma_start(c_T[:], a["cond_columns"]).then_inc(cond_loaded, 16)
            sp.dma_start(w_emb, a["L1_cond_W_emb"].rearrange("(k p) n -> p k n", p=P)).then_inc(cond_loaded, 16)
            sp.dma_start(b_emb[:], a["b_emb_columns"]).then_inc(cond_loaded, 16)
            sp.dma_start(g_norm[:], a["g_norm_columns"]).then_inc(cond_loaded, 16)
            for j, g in enumerate(("L1_cond_g_q", "L1_cond_g_k")):
                sp.dma_start(g_qk[:, j, :], a[g].rearrange("(o d) -> o d", o=1).broadcast_to([P, DH]))\
                  .then_inc(cond_loaded, 16)

        @block.gpsimd
        def _(pool):
            hs.credits(pool)
            with pool.Fori(0, B) as b:
                for t in range(TT):
                    pool.wait_ge(bank_free, b * 12 + t * 3 + 2 + 2)
                    pool.wait_ge(ssq_ready, b * TT + t + 1)
                    pool.tensor_tensor(tmp[:].rearrange("p a d -> p (a d)"), raw[:, t].rearrange("p a d -> p (a d)"),
                                       raw[:, t].rearrange("p a d -> p (a d)"), ALU.mult).then_inc(square_ready, 1)

        @block.tensor
        def _(pe):
            pe.wait_ge(cond_loaded, 96)
            for f in range(2 * KD):
                for k in range(KD):
                    mm = pe.matmul(bank[0][:, f * B:(f + 1) * B], w_emb[:, k, f * P:(f + 1) * P], c_T[:, k, :],
                                   start=(k == 0), stop=(k == KD - 1))
            mm.then_inc(mod_sum, 1)
            pe.wait_ge(mod_ready, 3)
            with pe.Fori(0, B) as b:
                pe.wait_ge(xn_ready, (b + 1) * TT)
                for k in range(KD):
                    for t in range(TT):
                        mm = pe.transpose(bank[k][:, t * P:(t + 1) * P], xn[:, t, k * P:(k + 1) * P],
                                          const["ident"][:])
                    mm.then_inc(xT_ready, 1)
                for t in range(TT):
                    for j in range(3):
                        n = t * 3 + j
                        if n == 0:
                            pe.wait_ge(yl_ready, (b + 1) * KD)
                        pe.wait_ge(bank_free, b * 12 + n + 1)
                        for k in range(KD):
                            mm = products(pe, qkv_bank[n % 2][:],
                                          (yh[:, k, t * P:(t + 1) * P], yl[:, k, t * P:(t + 1) * P]),
                                          (w_qkv[0][:, k, j * D:(j + 1) * D], w_qkv[1][:, k, j * D:(j + 1) * D]),
                                          k == 0, k == KD - 1)
                        mm.then_inc(qkv_ready, 1)
                hs_first = b * (H * TT)

                def turn_qk(h):
                    pe.wait_ge(q_copied, b * H + h + 1)
                    pe.wait_ge(k_copied, b * H + h + 1)
                    for i, src in enumerate((q4, k4)):
                        for t in range(TT):
                            mm = pe.transpose(q_bank[i][:, t * P:(t + 1) * P],
                                              src[:, t, at(h), :, :].rearrange("p o f d -> p (o f d)"),
                                              const["ident16"][:])
                    mm.then_inc(qk_turned, 1)

                pe.wait_ge(lo4_done, (b + 1) * TT * 2)
                turn_qk(0)

                def current(h, t, u):
                    if t == 0:
                        pe.wait_ge(q_copied, b * H + h + 2)
                        pe.wait_ge(k_copied, b * H + h + 2)
                    hs.pe_scores(pe, h, t, u)

                def beside(h, t, last):
                    if t == 1 and not last:
                        turn_qk(h + 1)

                hs.run(pe, H, hs_first, current, lambda h, t, u: hs.pe_turn(pe, t, u),
                       lambda h, t, u: hs.pe_values(pe, h, t, u), beside)
                pe.wait_ge(hs.out_copied, (b + 1) * (H * TT) + hs.CREDIT)
                for k in range(KD):
                    for t in range(TT):
                        mm = pe.transpose(bank[k][:, t * P:(t + 1) * P], O[:, t, k * P:(k + 1) * P],
                                          const["ident"][:])
                    mm.then_inc(o_turned, 1)
                pe.wait_ge(ol_ready, (b + 1) * KD)
                for t in range(TT):
                    pe.wait_ge(y_added, b * TT + t + 1)
                    for k in range(KD):
                        mm = products(pe, qkv_bank[t % 2][:],
                                      (oh[:, k, t * P:(t + 1) * P], ol[:, k, t * P:(t + 1) * P]),
                                      (w_out[0][:, k, :], w_out[1][:, k, :]), k == 0, k == KD - 1)
                    mm.then_inc(y_out, 1)

        @block.scalar
        def _(act):
            with act.Fori(0, NT) as n:
                act.wait_ge(sq_done, n)
                act.activation(flat(tmp[:, 0:1, :]), flat(X[:, at(n), :]), ACT.Square, accum_out=ss[:, at(n)])\
                   .then_inc(sq_done, 1)
            act.wait_ge(ms_ready, 1)
            act.activation(rstd[:], ss[:], ACT.Sqrt).then_inc(root_done, 1)
            act.wait_ge(rstd_ready, 1)
            with act.Fori(0, B) as b:
                for t in range(TT):
                    act.activation(xn[:, t, :], flat(X[:, at(b * TT + t), :]), ACT.Copy, scale=rstd[:, at(b * TT + t)])\
                       .then_inc(xn_ready, 1)
                for k in range(KD):
                    act.wait_ge(y_ready, b * KD + k + 1)
                    act.activation(yh[:, k, :], y32[:, k, :], ACT.Copy).then_inc(yh_ready, 1)
                for t in range(TT):
                    for j in range(3):
                        n = t * 3 + j
                        act.wait_ge(qkv_ready, b * 12 + n + 1)
                        dst = raw[:, t, j, :] if j < 2 else V[:, t, :]
                        act.activation(dst, qkv_bank[n % 2][:], ACT.Copy, scale=UNSCALE).then_inc(bank_free, 1)
                act.wait_ge(hms_ready, b + 1)
                act.activation(rq[:].rearrange("p t h -> p (t h)"), ssq[:].rearrange("p t h -> p (t h)"), ACT.Sqrt)\
                   .then_inc(hroot_done, 1)
                act.preload_act_table(ACT.Exp)
                for t in range(TT):
                    for j, dst in enumerate((q4, k4)):
                        act.wait_ge(q_gained, b * TT * 2 + t * 2 + j + 1)
                        src = raw[:, t, j, :].rearrange("p (h d) -> p h d", h=H)
                        for e in range(2):
                            slot = e if j == 0 else 2 * e
                            ins = act.activation(dst[:, t, :, slot, :], src, ACT.Copy)
                        ins.then_inc(hi4_done, 1)

                def copy_q(h):
                    act.wait_ge(qk_turned, b * H + h + 1)
                    act.activation(flat(qT[:, at(h), :]), q_bank[0][:], ACT.Copy).then_inc(q_copied, 1)

                copy_q(0)

                def beside(h, t, last):
                    if t == 1 and not last:
                        copy_q(h + 1)

                hs.run(act, H, b * (H * TT), lambda h, t, u: hs.act_exp(act, t, u),
                       lambda h, t, u: hs.act_copy(act, t, u), lambda h, t, u: None, beside)
                for k in range(KD):
                    act.wait_ge(o_turned, b * KD + k + 1)
                    act.activation(oh[:, k, :], bank[k][:], ACT.Copy, scale=XS).then_inc(oh_ready, 1)

        @block.vector
        def _(dve):
            dve.wait_ge(cond_loaded, 96)
            dve.tensor_tensor(gg[:, 0, :], g_qk[:, 0, :], g_qk[:, 1, :], ALU.mult).then_inc(gg_ready, 1)
            dve.wait_ge(gg_ready, 1)
            dve.tensor_scalar(gg[:], gg[:], float(DH) ** -0.5, None, ALU.mult).then_inc(gg_ready, 1)
            dve.wait_ge(mod_sum, 1)
            for f in range(2 * KD):
                dve.tensor_scalar(mod[:, f, :], bank[0][:, f * B:(f + 1) * B], b_emb[:, f:f + 1],
                                  1.0 if f < KD else 0.0, ALU.add, ALU.add)
            dve.engine_nop().then_inc(mod_ready, 1)
            dve.wait_ge(mod_ready, 1)
            for f in range(KD):
                dve.tensor_scalar(mod[:, f, :], mod[:, f, :], g_norm[:, f:f + 1], XS, ALU.mult, ALU.mult)
            dve.tensor_scalar(mod[:, KD:2 * KD, :], mod[:, KD:2 * KD, :], XS, None, ALU.mult).then_inc(mod_ready, 1)
            dve.wait_ge(mod_ready, 2)
            dve.engine_nop().then_inc(mod_ready, 1)
            dve.wait_ge(sq_done, NT)
            dve.tensor_scalar(ss[:], ss[:], 1.0 / D, EPS, ALU.mult, ALU.add).then_inc(ms_ready, 1)
            dve.wait_ge(root_done, 1)
            dve.reciprocal(rstd[:], rstd[:]).then_inc(rstd_ready, 1)
            dve.sem_inc(bank_free, 2)
            dve.sem_inc(y_added, 2)
            dve.sem_inc(q_copied, 1)
            dve.sem_inc(k_copied, 1)
            dve.sem_inc(ssq_ready, 1)
            with dve.Fori(0, B) as b:
                for k in range(KD):
                    dve.wait_ge(xT_ready, b * KD + k + 1)
                    dve.tensor_scalar(y32[:, k, :], bank[k][:], mod[:, k, at(b)], mod[:, KD + k, at(b)], ALU.mult,
                                      ALU.add).then_inc(y_ready, 1)
                for k in range(KD):
                    dve.wait_ge(yh_ready, b * KD + k + 1)
                    dve.tensor_tensor(yl[:, k, :], y32[:, k, :], yh[:, k, :], ALU.subtract).then_inc(yl_ready, 1)
                for t in range(TT):
                    dve.wait_ge(square_ready, b * TT + t + 1)
                    dve.tensor_reduce(ssq[:, t, :], tmp[:].rearrange("p a (h d) -> p (a h) d", d=DH), AX.X, ALU.add)\
                       .then_inc(ssq_ready, 1)
                dve.wait_ge(ssq_ready, b * TT + TT + 1)
                dve.tensor_scalar(ssq[:], ssq[:], 1.0 / DH, EPS, ALU.mult, ALU.add).then_inc(hms_ready, 1)
                dve.wait_ge(hroot_done, b + 1)
                dve.reciprocal(rq[:], rq[:]).then_inc(rq_ready, 1)
                dve.wait_ge(rq_ready, b + 1)
                for t in range(TT):
                    for j in range(2):
                        v = raw[:, t, j, :].rearrange("p (h d) -> p h d", h=H)
                        r = rq[:, t, j * H:(j + 1) * H].rearrange("p (h o) -> p h o", o=1).broadcast_to([P, H, DH])
                        if j == 0:
                            dve.tensor_tensor(v, v, r, ALU.mult).then_inc(normed, 1)
                            dve.wait_ge(normed, b * TT + t + 1)
                            dve.tensor_tensor(v, v, gg[:].broadcast_to([P, H, DH]), ALU.mult).then_inc(q_gained, 1)
                        else:
                            dve.tensor_tensor(v, v, r, ALU.mult).then_inc(q_gained, 1)
                for t in range(TT):
                    for j, dst in enumerate((q4, k4)):
                        src = raw[:, t, j, :].rearrange("p (h d) -> p h d", h=H)
                        dve.wait_ge(hi4_done, b * TT * 2 + t * 2 + j + 1)
                        for e in range(2):
                            slot = 2 + e if j == 0 else 1 + 2 * e
                            ins = dve.tensor_tensor(dst[:, t, :, slot, :], src, dst[:, t, :, 0, :], ALU.subtract)
                        ins.then_inc(lo4_done, 1)

                def copy_k(h):
                    dve.wait_ge(qk_turned, b * H + h + 1)
                    dve.tensor_copy(flat(kT[:, at(h), :]), q_bank[1][:]).then_inc(k_copied, 1)

                copy_k(0)

                def beside(h, t, last):
                    if t == 1 and not last:
                        copy_k(h + 1)

                hs.run(dve, H, b * (H * TT), lambda h, t, u: hs.dve_max(dve, t, u),
                       lambda h, t, u: hs.dve_copy(dve, t, u), lambda h, t, u: hs.dve_out(dve, h, t, u), beside)
                for k in range(KD):
                    dve.wait_ge(oh_ready, b * KD + k + 1)
                    dve.scalar_tensor_tensor(out=ol[:, k, :], in0=bank[k][:], scalar=XS, in1=oh[:, k, :],
                                             op0=ALU.mult, op1=ALU.subtract).then_inc(ol_ready, 1)
                for t in range(TT):
                    xs = flat(X[:, at(b * TT + t), :])
                    dve.wait_ge(y_out, b * TT + t + 1)
                    dve.tensor_tensor(xs, xs, O[:, t, :], ALU.add).then_inc(x_added, 1)
                    dve.wait_ge(x_added, b * TT + t + 1)
                    dve.scalar_tensor_tensor(out=xs, in0=qkv_bank[t % 2][:], scalar=UNSCALE, in1=xs,
                                             op0=ALU.mult, op1=ALU.add).then_inc(y_added, 1)


HS = 64.0
RS = 256.0
GS = HS * RS


def gate_input_phase(nc, X, const, a, w_ih, gi):
    G = 3 * KD
    with ExitStack() as ctx:
        m = Mem(nc, ctx, "gatein_")
        bias = m.sb("gate_bias", [P, 2 * G])
        col = m.sb("gate_col", [P, G])
        x32 = m.sb("gi_x32", [P, TT, D])
        xh, xl = m.sb("gi_xh", [P, KD, T], F16), m.sb("gi_xl", [P, KD, T], F16)
        bank = [m.ps(f"gbank{i}", [P, D]) for i in range(8)]
        bias_loaded, col_ready = m.sem("bias_loaded"), m.sem("col_ready")
        x_copied, x_turned = m.sem("gx_copied"), m.sem("gx_turned")
        xh_ready, xl_ready = m.sem("gxh_ready"), m.sem("gxl_ready")
        sum_ready, even_out, odd_out = m.sem("gate_sum"), m.sem("gate_even_out"), m.sem("gate_odd_out")
        block = ctx.enter_context(nc.Block())
        out_bank = bank[4:8]

        @block.sync
        def _(sp):
            sp.dma_start(bias[:, 0:G], a["b_ih_columns"]).then_inc(bias_loaded, 16)
            sp.dma_start(bias[:, G:2 * G], a["b_hh_columns"]).then_inc(bias_loaded, 16)

        @block.gpsimd
        def _(pool):
            with pool.Fori(0, B) as b:
                for t in range(TT):
                    pool.wait_ge(x_turned, b * KD)
                    pool.tensor_copy(x32[:, t, :], flat(X[:, at(b * TT + t), :])).then_inc(x_copied, 1)

        @block.tensor
        def _(pe):
            with pe.Fori(0, B) as b:
                pe.wait_ge(x_copied, (b + 1) * TT)
                pe.wait_ge(xl_ready, b * KD)
                for k in range(KD):
                    for t in range(TT):
                        mm = pe.transpose(bank[k][:, t * P:(t + 1) * P], x32[:, t, k * P:(k + 1) * P],
                                          const["ident"][:])
                    mm.then_inc(x_turned, 1)
                pe.wait_ge(xl_ready, (b + 1) * KD)
                for g in range(G):
                    pe.wait_ge(even_out if g % 2 == 0 else odd_out, b * (G // 2) + g // 2 + 1)
                    for k in range(KD):
                        mm = products(pe, out_bank[g % 4][:],
                                      (w_ih[0][:, k, g * P:(g + 1) * P], w_ih[1][:, k, g * P:(g + 1) * P]),
                                      (xh[:, k, :], xl[:, k, :]), k == 0, k == KD - 1)
                    mm.then_inc(sum_ready, 1)

        @block.scalar
        def _(act):
            act.wait_ge(col_ready, 2)
            act.sem_inc(even_out, 2)
            with act.Fori(0, B) as b:
                for k in range(KD):
                    act.wait_ge(x_turned, b * KD + k + 1)
                    act.wait_ge(sum_ready, b * G)
                    act.activation(xh[:, k, :], bank[k][:], ACT.Copy, scale=XS).then_inc(xh_ready, 1)
                for g in range(0, G, 2):
                    act.wait_ge(sum_ready, b * G + g + 1)
                    act.activation(flat(gi[:, g, at(b), :]), out_bank[g % 4][:], ACT.Identity,
                                   bias=col[:, g:g + 1], scale=GS * UNSCALE).then_inc(even_out, 1)

        @block.vector
        def _(dve):
            dve.wait_ge(bias_loaded, 32)
            dve.tensor_tensor(col[:, 0:2 * KD], bias[:, 0:2 * KD], bias[:, G:G + 2 * KD], ALU.add)
            dve.tensor_copy(col[:, 2 * KD:G], bias[:, 2 * KD:G]).then_inc(col_ready, 1)
            dve.wait_ge(col_ready, 1)
            dve.tensor_scalar(col[:], col[:], GS, None, ALU.mult).then_inc(col_ready, 1)
            dve.wait_ge(col_ready, 2)
            dve.sem_inc(odd_out, 2)
            with dve.Fori(0, B) as b:
                for k in range(KD):
                    dve.wait_ge(xh_ready, b * KD + k + 1)
                    dve.scalar_tensor_tensor(out=xl[:, k, :], in0=bank[k][:], scalar=XS, in1=xh[:, k, :],
                                             op0=ALU.mult, op1=ALU.subtract).then_inc(xl_ready, 1)
                for g in range(1, G, 2):
                    dve.wait_ge(sum_ready, b * G + g + 1)
                    dve.tensor_scalar(flat(gi[:, g, at(b), :]), out_bank[g % 4][:], GS * UNSCALE, col[:, g:g + 1],
                                      ALU.mult, ALU.add).then_inc(odd_out, 1)


class WeightStore:

    WIDE = 1024
    SLOTS = 2

    def __init__(self, nc, a):
        def scratch(name, shape):
            return nc.dram_tensor(name, shape, F16, kind="Internal").ap()

        self.qk = scratch("w_qk_parts", (P, DIT_H, 2, 2, KD, DIT_DH))
        self.v = scratch("w_v_parts", (P, 2, KD, INNER))
        self.out = scratch("w_out_parts", (P, 2, INNER // P, D))
        self.w1 = scratch("w_1_parts", (P, 2, KD, MLP))
        self.w2 = scratch("w_2_parts", (P, 2, MLP // P, D))
        rows = lambda w: w.rearrange("(k p) n -> p k n", p=P)
        qkv = rows(a["L3_cond_qkv_w"])
        W = self.WIDE
        self.pieces = []
        wide = W // (KD * DIT_DH)
        for h in range(0, DIT_H, wide):
            for i in range(2):
                c = i * INNER + h * DIT_DH
                self.pieces.append((qkv[:, :, c:c + wide * DIT_DH], self.qk[:, h:h + wide, i], True))
        for src, dst in ((qkv[:, :, 2 * INNER:3 * INNER], self.v), (rows(a["L3_cond_out_w"]), self.out),
                         (rows(a["L3_cond_ffn_w1"]), self.w1), (rows(a["L3_cond_ffn_w2"]), self.w2)):
            n = src.shape[2]
            if n >= W:
                for q in range(src.shape[1]):
                    for c in range(0, n, W):
                        self.pieces.append((src[:, q, c:c + W], dst[:, :, q, c:c + W], False))
            else:
                for q in range(0, src.shape[1], W // n):
                    self.pieces.append((src[:, q:q + W // n, :],
                                        dst[:, :, q:q + W // n, :].rearrange("p e k n -> p e (k n)"), False))

    def place(self, m):
        self.given = m.sb("given_w", [P, self.SLOTS, self.WIDE])
        self.parts = m.sb("parts_w", [P, self.SLOTS, 2 * self.WIDE], F16)
        self.loaded = [m.sem(f"piece_loaded_{s}") for s in range(self.SLOTS)]
        self.stored = [m.sem(f"piece_stored_{s}") for s in range(self.SLOTS)]
        self.scaled, self.hi_done, self.lo_done = m.sem("piece_scaled"), m.sem("piece_hi"), m.sem("piece_lo")

    def load(self, sp, j):
        src, s = self.pieces[j][0], j % self.SLOTS
        dst = self.given[:, s, :]
        if len(src.shape) == 3:
            dst = dst.rearrange("p (k n) -> p k n", k=src.shape[1])
        sp.dma_start(dst, src).then_inc(self.loaded[s], 16)

    def sync(self, sp):
        S = self.SLOTS
        for j in range(S):
            self.load(sp, j)
        for j, (_, dst, by_head) in enumerate(self.pieces):
            s = j % S
            sp.wait_ge(self.lo_done, j + 1)
            out = self.parts[:, s, :]
            out = (out.rearrange("p (h e k n) -> p h e k n", e=2, k=KD, n=DIT_DH) if by_head
                   else out.rearrange("p (e n) -> p e n", e=2))
            sp.dma_start(dst, out).then_inc(self.stored[s], 16)
            if j + S < len(self.pieces):
                self.load(sp, j + S)
        for s in range(S):
            sp.wait_ge(self.stored[s], 16 * len(self.pieces[s::S]))

    def pool(self, pool):
        S = self.SLOTS
        parts_begun = 0
        for j, (_, _, by_head) in enumerate(self.pieces):
            s = j % S
            w = self.given[:, s, :]
            pool.wait_ge(self.loaded[s], 16 * (j // S + 1))
            pool.tensor_scalar(w, w, WS, None, ALU.mult).then_inc(self.scaled, 1)
            pool.wait_ge(self.scaled, j + 1)
            if j >= S:
                pool.wait_ge(self.stored[s], 16 * (j // S))
            out = self.parts[:, s, :]
            if by_head:
                v = out.rearrange("p (h e k n) -> p h e k n", e=2, k=KD, n=DIT_DH)
                g = w.rearrange("p (k h n) -> p k h n", k=KD, n=DIT_DH)
                pairs = [(v[:, h, 0], v[:, h, 1], g[:, :, h, :]) for h in range(g.shape[2])]
            else:
                pairs = [(out[:, 0:self.WIDE], out[:, self.WIDE:2 * self.WIDE], w)]
            for n, (hi, lo, src) in enumerate(pairs):
                pool.tensor_copy(hi, src).then_inc(self.hi_done, 1)
            parts_begun += len(pairs)
            pool.wait_ge(self.hi_done, parts_begun)
            for n, (hi, lo, src) in enumerate(pairs):
                ins = pool.tensor_tensor(lo, src, hi, ALU.subtract)
            ins.then_inc(self.lo_done, 1)


def gru_phase(nc, X, const, a, w_hh, gi, x_out, store):
    G = 3 * KD
    with ExitStack() as ctx:
        m = Mem(nc, ctx, "gru_")
        if store is not None:
            store.place(m)
        hist = m.sb("hist", [P, KD, B, T + 1])
        h0 = m.sb("h0", [P, KD, B])
        b_hh = m.sb("b_hh", [P, G])
        ones = m.sb("gru_ones", [P, B])
        bn = m.sb("bn", [P, KD, B])
        parts = m.sb("state_parts", [P, KD, 2 * B], F16)
        r_in, z_in, n_in = (m.sb(f"{g}_in", [P, KD, B]) for g in "rzn")
        r, keep, n = (m.sb(f"{g}_gate", [P, KD, B]) for g in ("r", "new", "n"))
        u = m.sb("u", [P, KD, B])
        d = m.sb("d", [P, KD, B])
        e = m.sb("e", [P, KD, B])
        sums = [m.ps(f"{g}_sum", [P, KD, P]) for g in "rnz"]
        turned = [m.ps(f"hist_turned{i}", [P, D]) for i in range(2)]
        start_loaded = m.sem("start_loaded")
        made = m.sem("gru_made")
        hi_ready, lo_ready = m.sem("state_hi"), m.sem("state_lo")
        r_sum, n_sum, z_sum = m.sem("r_sum_ready"), m.sem("n_sum_ready"), m.sem("z_sum_ready")
        r_half, r_in_ready, r_ready = m.sem("r_half"), m.sem("r_in_ready"), m.sem("r_ready")
        u_half, u_ready, v_ready, n_in_ready, n_ready = (m.sem(s) for s in (
            "u_half", "u_ready", "v_ready", "n_in_ready", "n_ready"))
        z_half, z_in_ready, keep_ready = m.sem("z_half"), m.sem("z_in_ready"), m.sem("keep_ready")
        d_ready, e_ready, state_ready = m.sem("d_ready"), m.sem("e_ready"), m.sem("state_ready")
        back_turned, added = m.sem("back_turned"), m.sem("added")
        stored = m.sem("gru_stored")
        block = ctx.enter_context(nc.Block())

        @block.sync
        def _(sp):
            sp.dma_start(h0[:], a["cond_columns"]).then_inc(start_loaded, 16)
            sp.dma_start(b_hh[:], a["b_hh_columns"]).then_inc(start_loaded, 16)
            if store is not None:
                store.sync(sp)
            xo = x_out.rearrange("b (t p) d -> p (b t) d", p=P)
            for b in range(B):
                sp.wait_ge(added, (b + 1) * TT)
                sp.dma_start(xo[:, b * TT:(b + 1) * TT, :], X[:, b * TT:(b + 1) * TT, :]).then_inc(stored, 16)
            sp.wait_ge(stored, 16 * B)

        @block.gpsimd
        def _(pool):
            if store is not None:
                store.pool(pool)

        @block.tensor
        def _(pe):
            with pe.Fori(0, T) as i:
                for j, (gate, ready) in enumerate(((0, r_sum), (2, n_sum), (1, z_sum))):
                    tile = lambda w, k, f: w[:, k, (gate * KD + f) * P:(gate * KD + f + 1) * P]
                    if j == 0:
                        pe.wait_ge(hi_ready, i + 1)
                    for f in range(KD):
                        for k in range(KD):
                            pe.matmul(sums[j][:, f, 0:B], tile(w_hh[1], k, f), parts[:, k, 0:B],
                                      start=(f == 0 and k == 0), stop=False, skip_group_check=True)
                    if j == 0:
                        pe.wait_ge(lo_ready, i + 1)
                    for f in range(KD):
                        for k in range(KD):
                            mm = pe.matmul(sums[j][:, f, 0:2 * B], tile(w_hh[0], k, f), parts[:, k, :],
                                           start=False, stop=(f == KD - 1 and k == KD - 1), skip_group_check=True)
                    mm.then_inc(ready, 1)
            pe.wait_ge(state_ready, T)
            for b in range(B):
                for t in range(TT):
                    v = b * TT + t
                    if v >= 2:
                        pe.wait_ge(added, v - 1)
                    for f in range(KD):
                        mm = pe.transpose(turned[v % 2][:, f * P:(f + 1) * P],
                                          hist[:, f, b, 1 + t * P:1 + (t + 1) * P], const["ident"][:])
                    mm.then_inc(back_turned, 1)

        @block.scalar
        def _(act):
            act.preload_act_table_set("sigmoid_and_others")
            with act.Fori(0, T) as i:
                act.wait_ge(r_in_ready, i + 1)
                act.activation(r[:], r_in[:], ACT.Sigmoid, scale=1.0 / GS).then_inc(r_ready, 1)
                act.wait_ge(n_in_ready, i + 1)
                act.activation(n[:], n_in[:], ACT.Tanh, scale=1.0 / GS).then_inc(n_ready, 1)
                act.wait_ge(z_in_ready, i + 1)
                act.activation(keep[:], z_in[:], ACT.Sigmoid, scale=-1.0 / GS).then_inc(keep_ready, 1)

        @block.vector
        def _(dve):
            dve.wait_ge(start_loaded, 32)
            dve.memset(ones[:], GS).then_inc(made, 1)
            dve.wait_ge(made, 1)
            for f in range(KD):
                dve.tensor_scalar(bn[:, f, :], ones[:], b_hh[:, 2 * KD + f:2 * KD + f + 1], None, ALU.mult)\
                   .then_inc(made, 1)
            dve.tensor_scalar(hist[:, :, :, 0], h0[:], HS, None, ALU.mult).then_inc(made, 1)
            dve.wait_ge(made, 2 + KD)
            dve.tensor_copy(parts[:, :, 0:B], hist[:, :, :, 0]).then_inc(hi_ready, 1)
            dve.wait_ge(hi_ready, 1)
            dve.tensor_tensor(parts[:, :, B:2 * B], hist[:, :, :, 0], parts[:, :, 0:B], ALU.subtract)\
               .then_inc(lo_ready, 1)
            step_of = lambda v, i: v[:, :, :, at(i)].rearrange("p f b o -> p f (b o)")
            with dve.Fori(0, T) as i:
                before, after = step_of(hist, i), step_of(hist, i + 1)
                gate_in = lambda g: step_of(gi[:, g * KD:(g + 1) * KD], i)
                dve.wait_ge(r_sum, i + 1)
                dve.tensor_tensor(r_in[:], sums[0][:, :, 0:B], gate_in(0), ALU.add).then_inc(r_half, 1)
                dve.wait_ge(r_half, i + 1)
                dve.tensor_tensor(r_in[:], sums[0][:, :, B:2 * B], r_in[:], ALU.add).then_inc(r_in_ready, 1)
                dve.wait_ge(n_sum, i + 1)
                dve.tensor_tensor(u[:], sums[1][:, :, 0:B], bn[:], ALU.add).then_inc(u_half, 1)
                dve.wait_ge(u_half, i + 1)
                dve.tensor_tensor(u[:], sums[1][:, :, B:2 * B], u[:], ALU.add).then_inc(u_ready, 1)
                dve.wait_ge(u_ready, i + 1)
                dve.wait_ge(r_ready, i + 1)
                dve.tensor_tensor(u[:], u[:], r[:], ALU.mult).then_inc(v_ready, 1)
                dve.wait_ge(v_ready, i + 1)
                dve.tensor_tensor(n_in[:], u[:], gate_in(2), ALU.add).then_inc(n_in_ready, 1)
                dve.wait_ge(n_ready, i + 1)
                dve.scalar_tensor_tensor(out=d[:], in0=n[:], scalar=HS, in1=before, op0=ALU.mult,
                                         op1=ALU.subtract).then_inc(d_ready, 1)
                dve.wait_ge(z_sum, i + 1)
                dve.tensor_tensor(z_in[:], sums[2][:, :, 0:B], gate_in(1), ALU.add).then_inc(z_half, 1)
                dve.wait_ge(z_half, i + 1)
                dve.tensor_tensor(z_in[:], sums[2][:, :, B:2 * B], z_in[:], ALU.add).then_inc(z_in_ready, 1)
                dve.wait_ge(keep_ready, i + 1)
                dve.wait_ge(d_ready, i + 1)
                dve.tensor_tensor(e[:], d[:], keep[:], ALU.mult).then_inc(e_ready, 1)
                dve.wait_ge(e_ready, i + 1)
                dve.tensor_tensor(parts[:, :, 0:B], e[:], before, ALU.add).then_inc(hi_ready, 1)
                dve.tensor_tensor(after, e[:], before, ALU.add).then_inc(state_ready, 1)
                dve.wait_ge(hi_ready, i + 2)
                dve.wait_ge(state_ready, i + 1)
                dve.tensor_tensor(parts[:, :, B:2 * B], after, parts[:, :, 0:B], ALU.subtract).then_inc(lo_ready, 1)
            for v in range(NT):
                dve.wait_ge(back_turned, v + 1)
                dve.scalar_tensor_tensor(out=X[:, v, :], in0=turned[v % 2][:], scalar=1.0 / HS, in1=X[:, v, :],
                                         op0=ALU.mult, op1=ALU.add).then_inc(added, 1)


SCALE1, SHIFT1, SCALE2, SHIFT2 = range(4)


def dit_condition_phase(nc, a, store, mod, gates_dram, row_dram):
    with ExitStack() as ctx:
        m = Mem(nc, ctx, "ditcond_")
        w = m.sb("ada_w", [P, KD, 6 * D])
        w_out = m.sb("w_out", [P, 2, INNER // P, D], F16)
        c_T = m.sb("cond_T", [P, KD, B])
        b_col = m.sb("ada_b_col", [P, 6 * KD])
        b_row = m.sb("ada_b_row", [B, 2, D])
        gate = m.sb("gate", [B, 2, D])
        bv = m.sb("bv", [P, 3 * DIT_H])
        bvh, bvl = m.sb("bv_hi", [P, DIT_H], F16), m.sb("bv_lo", [P, DIT_H], F16)
        ob = m.sb("ob", [1, D])
        col_sum = m.ps("col_sum", [P, 4, KD, B])
        row_sum = [m.ps(f"row_sum{i}", [P, D]) for i in range(3)]
        loaded = m.sem("loaded")
        cols_ready, rows_ready, bv_ready, mapped = (m.sem(s) for s in ("cols", "rows", "bv_ready", "mapped"))
        bvh_ready, out_ready, stored = m.sem("bvh_ready"), m.sem("out_ready"), m.sem("stored")
        block = ctx.enter_context(nc.Block())
        chunks = (1, 0, 4, 3)

        @block.sync
        def _(sp):
            sp.dma_start(c_T[:], a["cond_columns"]).then_inc(loaded, 16)
            sp.dma_start(w[:], a["L3_cond_ada_w"].rearrange("(k p) n -> p k n", p=P)).then_inc(loaded, 16)
            sp.dma_start(b_col[:], a["ada_b_columns"]).then_inc(loaded, 16)
            rows = a["L3_cond_ada_b"].rearrange("(o j d) -> o j d", o=1, d=D).broadcast_to([B, 6, D])
            sp.dma_start(b_row[:, 0, :], rows[:, 2, :]).then_inc(loaded, 16)
            sp.dma_start(b_row[:, 1, :], rows[:, 5, :]).then_inc(loaded, 16)
            sp.dma_start(bv[:], a["qkv_b_columns"]).then_inc(loaded, 16)
            sp.dma_start(ob[:], a["L3_cond_out_b"].rearrange("(o d) -> o d", o=1)).then_inc(loaded, 16)
            sp.dma_start(w_out[:], store.out).then_inc(loaded, 16)
            sp.wait_ge(out_ready, 3)
            sp.dma_start(gates_dram, gate[:]).then_inc(stored, 16)
            sp.dma_start(row_dram, ob[:]).then_inc(stored, 16)
            sp.wait_ge(stored, 32)

        @block.tensor
        def _(pe):
            pe.wait_ge(loaded, 128)
            for i, j in enumerate(chunks):
                for f in range(KD):
                    for k in range(KD):
                        mm = pe.matmul(col_sum[:, i, f, :], w[:, k, j * D + f * P:j * D + (f + 1) * P], c_T[:, k, :],
                                       start=(k == 0), stop=(k == KD - 1))
            mm.then_inc(cols_ready, 1)
            for i, j in enumerate((2, 5)):
                for k in range(KD):
                    mm = pe.matmul(row_sum[i][0:B, :], c_T[:, k, :], w[:, k, j * D:(j + 1) * D], start=(k == 0),
                                   stop=(k == KD - 1))
            mm.then_inc(rows_ready, 1)
            pe.wait_ge(bv_ready, 1)
            for h in range(DIT_H):
                mm = products(pe, row_sum[2][0:1, :], (bvh[:, h:h + 1], bvl[:, h:h + 1]),
                              (w_out[:, 0, h, :], w_out[:, 1, h, :]), h == 0, h == DIT_H - 1)
            mm.then_inc(mapped, 1)

        @block.vector
        def _(dve):
            dve.wait_ge(loaded, 128)
            v = bv[:, 2 * DIT_H:3 * DIT_H]
            dve.tensor_scalar(bvh[:], v, XS, None, ALU.mult).then_inc(bvh_ready, 1)
            dve.wait_ge(bvh_ready, 1)
            dve.scalar_tensor_tensor(out=bvl[:], in0=v, scalar=XS, in1=bvh[:], op0=ALU.mult, op1=ALU.subtract)\
               .then_inc(bv_ready, 1)
            dve.wait_ge(cols_ready, 1)
            for i, j in enumerate(chunks):
                for f in range(KD):
                    dve.tensor_scalar(mod[:, i, f, :], col_sum[:, i, f, :], b_col[:, j * KD + f:j * KD + f + 1],
                                      1.0 if i in (SCALE1, SCALE2) else 0.0, ALU.add, ALU.add).then_inc(bvh_ready, 1)
            dve.wait_ge(bvh_ready, 1 + 4 * KD)
            dve.tensor_scalar(mod[:], mod[:], XS, None, ALU.mult)
            dve.wait_ge(rows_ready, 1)
            for i in range(2):
                dve.tensor_tensor(gate[:, i, :], row_sum[i][0:B, :], b_row[:, i, :], ALU.add).then_inc(out_ready, 1)
            dve.wait_ge(mapped, 1)
            dve.scalar_tensor_tensor(out=ob[:], in0=row_sum[2][0:1, :], scalar=UNSCALE, in1=ob[:], op0=ALU.mult,
                                     op1=ALU.add).then_inc(out_ready, 1)


def dit_phase(nc, const, a, store, mod, gates_dram, row_dram, x_in, out):
    H, DH = DIT_H, DIT_DH
    FT = MLP // P
    C = INNER // D
    with ExitStack() as ctx:
        m = Mem(nc, ctx, "dit_")
        X = m.sb("X", [P, TT, D])
        yh, yl = m.sb("yh", [P, KD, T], F16), m.sb("yl", [P, KD, T], F16)
        big = m.sb("big", [P, TT, INNER])
        O = big
        A = big[:, :, 0:D]
        xn = big[:, :, D:2 * D]
        y32 = big[:, :, 2 * D:3 * D]
        V = m.sb("V", [P, 2, TT, INNER], F16)
        hid = V[:].rearrange("p e t n -> p e (t n)").rearrange("p e (f t) -> p e f t", f=FT)
        qk = m.sb("qk", [P, 2, 2, 2, T], F16)
        oT = [[yh[:].rearrange("p k t -> p (k t)").rearrange("p (h q) -> p h q", h=H),
               yl[:].rearrange("p k t -> p (k t)").rearrange("p (h q) -> p h q", h=H)],
              [qk[:, 0].rearrange("p a e t -> p (a e t)").rearrange("p (h q) -> p h q", h=H),
               qk[:, 1].rearrange("p a e t -> p (a e t)").rearrange("p (h q) -> p h q", h=H)]]
        region = [m.sb(f"weights{i}", [P, 2, KD * INNER], F16) for i in range(2)]
        cut = lambda r, k: r[:].rearrange("p e (k n) -> p e k n", k=k)
        w_v, w_1 = cut(region[0], KD), cut(region[0], KD)
        w_out, w_2 = cut(region[1], H), cut(region[1], FT)
        w_qk = m.sb("w_qk", [P, 2, 2, 2, KD, DH], F16)
        gates = m.sb("gates", [P, 2, D])
        rows = m.sb("bias_rows", [P, 2, D])
        gb = m.sb("gated_bias", [P, 2, D])
        qk_b = m.sb("qk_b", [P, 3 * H])
        b_1 = m.sb("b_1", [P, FT])
        stats = m.sb("stats", [P, TT, 6])
        mv = m.sb("mv", [P, TT, 2])
        rstd = m.sb("rstd", [P, TT])
        bank = [m.ps(f"bank{i}", [P, D]) for i in range(8)]
        work = bank[4:8]

        wv_loaded, w1_loaded, wo_loaded, w2_loaded = (m.sem(s) for s in "wv_loaded w1_loaded wo_loaded w2_loaded".split())
        wqk_loaded = [m.sem(f"wqk_loaded_{i}") for i in range(2)]
        (stats_taken, params_loaded, x_loaded, gates_loaded, b_scaled, gated, a_begun, stats_ready, mv_ready, var_ready,
         root_done, rstd_ready, xn_ready, rows_turned, y_ready, yh_ready, yl_ready, v_sum, vh_ready, vl_ready,
         qk_sum, qk_hi, qk_lo, o_turned, oh_ready, ol_ready, att_sum, att_gated, a_ready, x_again, hid_sum, hid_ready,
         hh_ready, hl_ready, mlp_sum, mlp_gated, out_ready, stored) = (m.sem(s) for s in (
             "stats_taken params_loaded x_loaded gates_loaded b_scaled gated a_begun stats_ready mv_ready var_ready root_done "
             "rstd_ready xn_ready rows_turned y_ready yh_ready yl_ready v_sum vh_ready vl_ready qk_sum qk_hi qk_lo "
             "o_turned oh_ready ol_ready att_sum att_gated a_ready x_again hid_sum hid_ready hh_ready hl_ready "
             "mlp_sum mlp_gated out_ready stored").split())

        def scores(pe, s, h, t):
            for (qe, ke) in ((0, 0), (0, 1), (1, 0)):
                mm = pe.matmul(s, qk[:, hs.parity, 0, qe, t * P:(t + 1) * P], qk[:, hs.parity, 1, ke, :],
                               start=(qe + ke == 0), stop=(qe == 1))
            return mm

        hs = Heads(
            m, S=[bank[0][:], bank[1][:]], PT=[bank[2][:], bank[3][:]], O=[bank[4][:, 0:DH], bank[5][:, 0:DH]],
            ident=const["ident"][:], scores=scores,
            values=lambda h, s: (V[:, 0, s, at(h * DH, DH)], V[:, 1, s, at(h * DH, DH)]),
            out=lambda h, t: O[:, t, at(h * DH, DH)],
            scale=UNSCALE * UNSCALE * float(DH) ** -0.5, parts=True)
        gelu = hs.prob

        x_rows = x_in.rearrange("b (t p) d -> p b t d", p=P)
        o_rows = out.rearrange("b (t p) d -> p b t d", p=P)
        flat_head = lambda v: v.rearrange("p o a e k n -> p (o a) e k n")
        block = ctx.enter_context(nc.Block())

        @block.sync
        def _(sp):
            sp.dma_start(qk_b[:], a["qkv_b_columns"]).then_inc(params_loaded, 16)
            sp.dma_start(b_1[:], a["ffn_b1_columns"]).then_inc(params_loaded, 16)
            sp.dma_start(rows[:, 0, :], row_dram.broadcast_to([P, D])).then_inc(params_loaded, 16)
            sp.dma_start(rows[:, 1, :], a["L3_cond_ffn_b2"].rearrange("(o d) -> o d", o=1).broadcast_to([P, D]))\
              .then_inc(params_loaded, 16)
            sp.dma_start(w_v, store.v).then_inc(wv_loaded, 16)
            with sp.Fori(0, B) as b:
                def load_qk(h, parity):
                    sp.dma_start(w_qk[:, parity], flat_head(store.qk[:, at(h)])).then_inc(wqk_loaded[parity], 16)

                sp.wait_ge(stored, b * (16 * TT))
                sp.dma_start(X[:], x_rows[:, at(b), :, :].rearrange("p o t d -> p (o t) d")).then_inc(x_loaded, 16)
                sp.dma_start(gates[:], gates_dram[at(b), :, :].broadcast_to([P, 2, D])).then_inc(gates_loaded, 16)
                sp.wait_ge(qk_sum, b * (2 * H))
                load_qk(0, 0)
                load_qk(1, 1)
                sp.wait_ge(mlp_sum, b * TT)
                sp.dma_start(w_out, store.out).then_inc(wo_loaded, 16)
                sp.wait_ge(v_sum, (b + 1) * (TT * C))
                sp.dma_start(w_1, store.w1).then_inc(w1_loaded, 16)
                with sp.Fori(0, (H - 2) // 2) as pair:
                    for parity in range(2):
                        sp.wait_ge(qk_sum, b * (2 * H) + pair * 4 + (parity * 2 + 2))
                        load_qk(pair * 2 + (2 + parity), parity)
                sp.wait_ge(att_sum, (b + 1) * TT)
                sp.dma_start(w_2, store.w2).then_inc(w2_loaded, 16)
                sp.wait_ge(hid_sum, (b + 1) * FT)
                sp.dma_start(w_v, store.v).then_inc(wv_loaded, 16)
                for t in range(TT):
                    sp.wait_ge(out_ready, b * TT + t + 1)
                    sp.dma_start(o_rows[:, at(b), t, :], X[:, t, :]).then_inc(stored, 16)
            sp.wait_ge(wv_loaded, (B + 1) * 16)
            sp.wait_ge(stored, B * TT * 16)

        @block.gpsimd
        def _(pool):
            hs.credits(pool)
            pool.sem_inc(att_gated, 2)
            pool.sem_inc(mlp_gated, 2)
            pool.sem_inc(hl_ready, 2)
            pool.sem_inc(vl_ready, C)
            pool.wait_ge(params_loaded, 64)
            with pool.Fori(0, B) as b:
                pool.wait_ge(gates_loaded, (b + 1) * 16)
                pool.tensor_tensor(gb[:], gates[:], rows[:], ALU.mult).then_inc(gated, 1)
                pool.wait_ge(gated, b + 1)
                for t in range(TT):
                    pool.wait_ge(att_gated, b * TT + t + 3)
                    pool.tensor_tensor(A[:, t, :], A[:, t, :], gb[:, 0, :], ALU.add).then_inc(a_begun, 1)
                    pool.wait_ge(a_begun, b * TT + t + 1)
                    pool.tensor_tensor(A[:, t, :], A[:, t, :], X[:, t, :], ALU.add).then_inc(a_ready, 1)
                for t in range(TT):
                    pool.wait_ge(a_ready, b * TT + t + 1)
                    pool.tensor_tensor(X[:, t, :], A[:, t, :], X[:, t, :], ALU.add).then_inc(x_again, 1)
                    pool.wait_ge(x_again, (b * TT + t) * 2 + 1)
                    pool.tensor_tensor(X[:, t, :], X[:, t, :], gb[:, 1, :], ALU.add).then_inc(x_again, 1)

        @block.tensor
        def _(pe):
            pe.wait_ge(b_scaled, 1)
            with pe.Fori(0, B) as b:
                def turn_rows(n):
                    pe.wait_ge(xn_ready, n * TT + TT)
                    for k in range(KD):
                        for t in range(TT):
                            mm = pe.transpose(bank[k][:, t * P:(t + 1) * P], xn[:, t, k * P:(k + 1) * P],
                                              const["ident"][:])
                        mm.then_inc(rows_turned, 1)

                pe.wait_ge(wv_loaded, (b + 1) * 16)
                turn_rows(b * 2)
                with pe.Fori(0, TT) as t:
                    pe.wait_ge(yl_ready, b * (2 * KD) + KD)
                    for c in range(C):
                        pe.wait_ge(vl_ready, b * (TT * C) + t * C + (c + 1))
                        for k in range(KD):
                            w = lambda e: w_v[:, e, k, c * D:(c + 1) * D]
                            mm = products(pe, work[c][:], (yh[:, k, at(t * P, P)], yl[:, k, at(t * P, P)]),
                                          (w(0), w(1)), k == 0, k == KD - 1)
                        mm.then_inc(v_sum, 1)
                pe.wait_ge(vl_ready, (b + 1) * (TT * C) + C)

                def project(h, i, parity, nth):
                    if i == 0:
                        pe.wait_ge(wqk_loaded[parity], b * (16 * (H // 2)) + nth * 16)
                    for k in range(KD):
                        w = lambda e: w_qk[:, parity, i, e, k, :]
                        mm = products(pe, work[2 + i][:], (w(0), w(1)), (yh[:, k, :], yl[:, k, :]), k == 0,
                                      k == KD - 1)
                    mm.then_inc(qk_sum, 1)

                project(0, 0, 0, 1)
                project(0, 1, 0, 1)

                def current(h, t, u):
                    if t == 0:
                        pe.wait_ge(qk_lo, b * (2 * H) + h * 2 + 2)
                    hs.pe_scores(pe, h, t, u)

                def beside(h, t, last):
                    if t in (1, 2) and not last:
                        project(h + 1, t - 1, 1 - hs.parity, hs.nth)

                hs.run(pe, H, b * (H * TT), current, lambda h, t, u: hs.pe_turn(pe, t, u),
                       lambda h, t, u: hs.pe_values(pe, h, t, u), beside)

                def project_out(t):
                    pe.wait_ge(ol_ready, b * (4 * TT) + 4 * t + 4)
                    pe.wait_ge(att_gated, b * TT + t + 1)
                    for h in range(H):
                        mm = products(pe, work[t % 2][:], (oT[t % 2][0][:, h, :], oT[t % 2][1][:, h, :]),
                                      (w_out[:, 0, h, :], w_out[:, 1, h, :]), h == 0, h == H - 1)
                    mm.then_inc(att_sum, 1)

                pe.wait_ge(hs.out_copied, (b + 1) * (H * TT) + hs.CREDIT)
                pe.wait_ge(wo_loaded, (b + 1) * 16)
                for t in range(TT):
                    for q in range(4):
                        if t >= 1:
                            pe.wait_ge(ol_ready, b * (4 * TT) + 4 * (t - 1) + q + 1)
                        for h in range(4):
                            mm = pe.transpose(bank[q][:, h * P:(h + 1) * P],
                                              O[:, t, (4 * q + h) * P:(4 * q + h + 1) * P], const["ident"][:])
                        mm.then_inc(o_turned, 1)
                    if t >= 1:
                        project_out(t - 1)
                project_out(TT - 1)
                pe.wait_ge(w1_loaded, (b + 1) * 16)
                turn_rows(b * 2 + 1)
                with pe.Fori(0, FT // 4) as g:
                    pe.wait_ge(yl_ready, (b + 1) * (2 * KD))
                    for j in range(4):
                        pe.wait_ge(hid_ready, b * FT + g * 4 + (j + 1))
                        for k in range(KD):
                            w = lambda e: w_1[:, e, k, at(g * (4 * P) + j * P, P)]
                            mm = products(pe, work[j][:], (w(0), w(1)), (yh[:, k, :], yl[:, k, :]), k == 0,
                                          k == KD - 1)
                        mm.then_inc(hid_sum, 1)
                with pe.Fori(0, TT // 2) as g:
                    pe.wait_ge(hl_ready, (b + 1) * FT + 2)
                    pe.wait_ge(w2_loaded, (b + 1) * 16)
                    for j in range(2):
                        pe.wait_ge(mlp_gated, b * TT + g * 2 + (j + 1))
                        for f in range(FT):
                            left = lambda e: hid[:, e, f, at(g * (2 * P) + j * P, P)]
                            mm = products(pe, work[j][:], (left(0), left(1)), (w_2[:, 0, f, :], w_2[:, 1, f, :]),
                                          f == 0, f == FT - 1)
                        mm.then_inc(mlp_sum, 1)

        @block.scalar
        def _(act):
            act.wait_ge(b_scaled, 1)
            act.sem_inc(hid_ready, 4)
            with act.Fori(0, B) as b:
                def parts_of_rows(n):
                    act.wait_ge(var_ready, n + 1)
                    act.activation(rstd[:], mv[:, :, 1], ACT.Sqrt).then_inc(root_done, 1)
                    for k in range(KD):
                        act.wait_ge(y_ready, n * KD + k + 1)
                        act.activation(yh[:, k, :], y32[:, k, :], ACT.Copy).then_inc(yh_ready, 1)

                parts_of_rows(b * 2)
                with act.Fori(0, TT) as t:
                    for c in range(C):
                        act.wait_ge(v_sum, b * (TT * C) + t * C + (c + 1))
                        act.activation(V[:, 0, at(t), c * D:(c + 1) * D].rearrange("p o n -> p (o n)"), work[c][:],
                                       ACT.Copy).then_inc(vh_ready, 1)
                act.preload_act_table(ACT.Exp)

                def take(h, i, parity):
                    act.wait_ge(qk_sum, b * (2 * H) + h * 2 + (i + 1))
                    act.activation(qk[:, parity, i, 0, :], work[2 + i][:], ACT.Identity,
                                   bias=qk_b[:, at(h + i * H)]).then_inc(qk_hi, 1)

                take(0, 0, 0)
                take(0, 1, 0)

                def beside(h, t, last):
                    if t in (2, 3) and not last:
                        take(h + 1, t - 2, 1 - hs.parity)

                hs.run(act, H, b * (H * TT), lambda h, t, u: hs.act_exp(act, t, u),
                       lambda h, t, u: hs.act_copy(act, t, u), lambda h, t, u: None, beside)
                for t in range(TT):
                    for q in range(4):
                        act.wait_ge(o_turned, b * (4 * TT) + 4 * t + q + 1)
                        if t >= 2:
                            act.wait_ge(att_sum, b * TT + t - 1)
                        act.activation(oT[t % 2][0][:, 4 * q:4 * q + 4, :].rearrange("p h q -> p (h q)"),
                                       bank[q][:], ACT.Copy, scale=XS * UNSCALE).then_inc(oh_ready, 1)
                parts_of_rows(b * 2 + 1)
                act.preload_act_table(ACT.Gelu)
                with act.Fori(0, FT // 4) as g:
                    for j in range(4):
                        n = b * FT + g * 4 + j
                        act.wait_ge(hid_sum, n + 1)
                        act.wait_ge(hl_ready, n + 1)
                        act.activation(gelu[:, j % 2, :], work[j][:], ACT.Gelu, bias=b_1[:, at(g * 4 + j)],
                                       scale=UNSCALE).then_inc(hid_ready, 1)
                        act.wait_ge(hid_ready, n + 5)
                        act.activation(flat(hid[:, 0, at(g * 4 + j), :]), gelu[:, j % 2, :], ACT.Copy, scale=XS)\
                           .then_inc(hh_ready, 1)

        @block.vector
        def _(dve):
            dve.wait_ge(params_loaded, 64)
            dve.tensor_scalar(qk_b[:], qk_b[:], XS * WS, None, ALU.mult).then_inc(b_scaled, 1)
            dve.wait_ge(b_scaled, 1)
            with dve.Fori(0, B) as b:
                def norm(n, src, ready, scale, shift):
                    for t in range(TT):
                        ready(t)
                        dve.bn_stats(stats[:, t, :], src[:, t, :]).then_inc(stats_ready, 1)
                    dve.wait_ge(stats_ready, (n + 1) * TT)
                    dve.sem_inc(stats_taken, 1)
                    for t in range(TT):
                        dve.bn_aggr(mv[:, t, :], stats[:, t, :]).then_inc(mv_ready, 1)
                    dve.wait_ge(mv_ready, (n + 1) * TT)
                    dve.tensor_scalar(mv[:, :, 1], mv[:, :, 1], DIT_EPS, None, ALU.add).then_inc(var_ready, 1)
                    dve.wait_ge(root_done, n + 1)
                    dve.reciprocal(rstd[:], rstd[:]).then_inc(rstd_ready, 1)
                    dve.wait_ge(rstd_ready, n + 1)
                    for t in range(TT):
                        dve.tensor_scalar(xn[:, t, :], src[:, t, :], mv[:, t, 0:1], rstd[:, t:t + 1], ALU.subtract,
                                          ALU.mult).then_inc(xn_ready, 1)
                    for k in range(KD):
                        dve.wait_ge(rows_turned, n * KD + k + 1)
                        dve.tensor_scalar(y32[:, k, :], bank[k][:], mod[:, scale, k, at(b)], mod[:, shift, k, at(b)],
                                          ALU.mult, ALU.add).then_inc(y_ready, 1)
                    for k in range(KD):
                        dve.wait_ge(yh_ready, n * KD + k + 1)
                        dve.tensor_tensor(yl[:, k, :], y32[:, k, :], yh[:, k, :], ALU.subtract).then_inc(yl_ready, 1)

                norm(b * 2, X, lambda t: dve.wait_ge(x_loaded, (b + 1) * 16) if t == 0 else None, SCALE1, SHIFT1)
                with dve.Fori(0, TT) as t:
                    for c in range(C):
                        dve.wait_ge(vh_ready, b * (TT * C) + t * C + (c + 1))
                        cols = slice(c * D, (c + 1) * D)
                        dve.tensor_tensor(flat(V[:, 1, at(t), cols]), work[c][:], flat(V[:, 0, at(t), cols]),
                                          ALU.subtract).then_inc(vl_ready, 1)

                def take(h, i, parity):
                    dve.wait_ge(qk_hi, b * (2 * H) + h * 2 + (i + 1))
                    dve.scalar_tensor_tensor(out=qk[:, parity, i, 1, :], in0=work[2 + i][:],
                                             scalar=qk_b[:, at(h + i * H)], in1=qk[:, parity, i, 0, :],
                                             op0=ALU.add, op1=ALU.subtract).then_inc(qk_lo, 1)

                take(0, 0, 0)
                take(0, 1, 0)

                def beside(h, t, last):
                    if t in (2, 3) and not last:
                        take(h + 1, t - 2, 1 - hs.parity)

                hs.run(dve, H, b * (H * TT), lambda h, t, u: hs.dve_max(dve, t, u),
                       lambda h, t, u: hs.dve_copy(dve, t, u), lambda h, t, u: hs.dve_out(dve, h, t, u), beside)

                def gate_attention(t):
                    dve.wait_ge(att_sum, b * TT + t + 1)
                    dve.wait_ge(gates_loaded, (b + 1) * 16)
                    dve.scalar_tensor_tensor(out=A[:, t, :], in0=work[t % 2][:], scalar=UNSCALE, in1=gates[:, 0, :],
                                             op0=ALU.mult, op1=ALU.mult).then_inc(att_gated, 1)

                for t in range(TT):
                    for q in range(4):
                        dve.wait_ge(oh_ready, b * (4 * TT) + 4 * t + q + 1)
                        part = lambda e: oT[t % 2][e][:, 4 * q:4 * q + 4, :].rearrange("p h q -> p (h q)")
                        dve.scalar_tensor_tensor(out=part(1), in0=bank[q][:], scalar=XS * UNSCALE, in1=part(0),
                                                 op0=ALU.mult, op1=ALU.subtract).then_inc(ol_ready, 1)
                    if t >= 1:
                        gate_attention(t - 1)
                gate_attention(TT - 1)
                norm(b * 2 + 1, A, lambda t: dve.wait_ge(a_ready, b * TT + t + 1), SCALE2, SHIFT2)
                with dve.Fori(0, FT // 4) as g:
                    for j in range(4):
                        n = b * FT + g * 4 + j
                        dve.wait_ge(hh_ready, n + 1)
                        dve.scalar_tensor_tensor(out=flat(hid[:, 1, at(g * 4 + j), :]), in0=gelu[:, j % 2, :],
                                                 scalar=XS, in1=flat(hid[:, 0, at(g * 4 + j), :]), op0=ALU.mult,
                                                 op1=ALU.subtract).then_inc(hl_ready, 1)
                for t in range(TT):
                    dve.wait_ge(mlp_sum, b * TT + t + 1)
                    if t >= 2:
                        dve.wait_ge(out_ready, b * TT + t - 1)
                    dve.scalar_tensor_tensor(out=gelu[:, t % 2, :], in0=work[t % 2][:], scalar=UNSCALE,
                                             in1=gates[:, 1, :], op0=ALU.mult, op1=ALU.mult).then_inc(mlp_gated, 1)
                    dve.wait_ge(mlp_gated, b * TT + t + 3)
                    dve.wait_ge(x_again, (b * TT + t) * 2 + 2)
                    dve.tensor_tensor(X[:, t, :], X[:, t, :], gelu[:, t % 2, :], ALU.add).then_inc(out_ready, 1)


def program(nc, a, out):
    rows = lambda w: w.rearrange("(k p) n -> p k n", p=P)
    x_gru = out if LAST_PHASE == 3 else nc.dram_tensor("x_gru", (B, T, D), F32, kind="Internal").ap()
    store = WeightStore(nc, a) if LAST_PHASE >= 4 else None
    gates_dram = nc.dram_tensor("gates", (B, 2, D), F32, kind="Internal").ap()
    row_dram = nc.dram_tensor("out_bias_row", (1, D), F32, kind="Internal").ap()

    def parts(ctx, name, k, n):
        return [Mem(nc, ctx).sb(f"{name}_{e}", [P, k, n], F16) for e in ("hi", "lo")]

    with ExitStack() as ctx:
        m = Mem(nc, ctx)
        const = {
            "ones16": m.sb("ones16", [P, P], F16),
            "ones32": m.sb("ones32", [P, P]),
            "below": m.sb("below", [P, P]),
            "ident": m.sb("ident", [P, P]),
            "ident16": m.sb("ident16", [P, P], F16),
        }
        made = m.sem("const_made")
        with nc.Block() as block:
            @block.gpsimd
            def _(pool):
                pool.memset(const["ones16"][:], 1.0).then_inc(made, 1)
                pool.memset(const["ones32"][:], 1.0).then_inc(made, 1)
                pool.wait_ge(made, 2)
                pool.affine_select(out=const["below"][:], in_=const["ones32"][:], compare_op=ALU.is_gt, fill=0.0,
                                   base=0, pattern=[[1, P]], channel_multiplier=-1)
                pool.affine_select(out=const["ident"][:], in_=const["ones32"][:], compare_op=ALU.is_equal, fill=0.0,
                                   base=0, pattern=[[1, P]], channel_multiplier=-1)
                pool.affine_select(out=const["ident16"][:], in_=const["ones16"][:], compare_op=ALU.is_equal,
                                   fill=0.0, base=0, pattern=[[1, P]], channel_multiplier=-1)

        with ExitStack() as inner:
            X = Mem(nc, inner).sb("X", [P, NT, D])
            topk_phase(nc, X, const, a["x"], a["side_columns"], a["cond_2048"])
            if LAST_PHASE >= 2:
                with ExitStack() as weights:
                    w_qkv, w_out = parts(weights, "small_qkv", KD, 3 * D), parts(weights, "small_out", KD, D)
                    split_weights(nc, "small_", [(rows(a["L1_cond_W_qkv"]), w_qkv[0][:], w_qkv[1][:], WS),
                                                 (rows(a["L1_cond_W_out"]), w_out[0][:], w_out[1][:], WS)])
                    small_attention_phase(nc, X, const, a, w_qkv, w_out)
            if LAST_PHASE >= 3:
                with ExitStack() as weights:
                    gi = Mem(nc, weights).sb("gi", [P, 3 * KD, B, T])
                    w_hh = parts(weights, "w_hh", KD, 3 * D)
                    with ExitStack() as deeper:
                        w_ih = parts(deeper, "w_ih", KD, 3 * D)
                        split_weights(nc, "gru_", [(rows(a["L2_cond_W_ih"]), w_ih[0][:], w_ih[1][:], WS),
                                                   (rows(a["L2_cond_W_hh"]), w_hh[0][:], w_hh[1][:], RS)])
                        gate_input_phase(nc, X, const, a, w_ih, gi)
                    gru_phase(nc, X, const, a, w_hh, gi, x_gru, store)
            if LAST_PHASE <= 2:
                stored = m.sem("stored")
                with nc.Block() as block:
                    @block.sync
                    def _(sp):
                        sp.dma_start(out.rearrange("b (t p) d -> p (b t) d", p=P), X[:]).then_inc(stored, 16)
                        sp.wait_ge(stored, 16)

        if LAST_PHASE >= 4:
            mod = m.sb("dit_mod", [P, 4, KD, B])
            dit_condition_phase(nc, a, store, mod, gates_dram, row_dram)
            dit_phase(nc, const, a, store, mod, gates_dram, row_dram, x_gru, out)


def kernel(**inputs):
    import numpy as np
    import concourse.bacc as bacc
    from concourse.bass_utils import run_bass_kernel_spmd

    nc = bacc.Bacc("TRN2", target_bir_lowering=False, num_devices=1)
    given = {k: np.asarray(v) for k, v in inputs.items()}
    given["side_columns"] = given["fside_BxSx1_0"].reshape(NT, P).T
    columns = lambda v: v.reshape(-1, P).T
    given["cond_columns"] = given["cond_2048"].reshape(B, KD, P).transpose(2, 1, 0)
    given["b_emb_columns"] = columns(given["L1_cond_b_emb"])
    given["b_ih_columns"] = columns(given["L2_cond_b_ih"])
    given["b_hh_columns"] = columns(given["L2_cond_b_hh"])
    given["ada_b_columns"] = columns(given["L3_cond_ada_b"])
    given["qkv_b_columns"] = columns(given["L3_cond_qkv_b"])
    given["ffn_b1_columns"] = columns(given["L3_cond_ffn_b1"])
    given["g_norm_columns"] = columns(given["L1_cond_g_norm"])
    arrays = {f"in_{k}": np.ascontiguousarray(v) for k, v in given.items()}
    args = {k: nc.dram_tensor(f"in_{k}", arrays[f"in_{k}"].shape, mybir.dt.from_np(arrays[f"in_{k}"].dtype),
                              kind="ExternalInput").ap() for k in given}
    out = nc.dram_tensor("out", (B, T, D), F32, kind="ExternalOutput").ap()
    program(nc, args, out)
    r = run_bass_kernel_spmd(nc, [arrays], core_ids=[0])
    return r.results[0]["out"]
```

```python
from contextlib import ExitStack

import concourse.bass as bass
from concourse import mybir

F32 = mybir.dt.float32
F16 = mybir.dt.float16
I32 = mybir.dt.int32
I16 = mybir.dt.int16
U16 = mybir.dt.uint16
ALU = mybir.AluOpType
ACT = mybir.ActivationFunctionType
AX = mybir.AxisListType

P = 128
B, T, D = 4, 512, 512
TT = T // P
NT = B * TT
KD = D // P
TOPK = 5120

DIT_H, DIT_DH = 16, 128
INNER = DIT_H * DIT_DH
MLP = 4 * D
DIT_EPS = 1e-6
SCALE1, SHIFT1, SCALE2, SHIFT2 = range(4)
LAST_PHASE = 4


class Mem:

    def __init__(self, nc, ctx, phase=""):
        self.nc, self.ctx, self.phase = nc, ctx, phase
        self.sems = []

    def sb(self, name, shape, dt=F32):
        return self.ctx.enter_context(self.nc.sbuf_tensor(self.phase + name, shape, dt))

    def ps(self, name, shape, dt=F32):
        return self.ctx.enter_context(self.nc.psum_tensor(self.phase + name, shape, dt))

    def sem(self, name):
        if not self.sems:
            self.ctx.callback(self.clear)
        self.sems.append(self.nc.alloc_semaphore(name=self.phase + name))
        return self.sems[-1]

    def clear(self):
        self.nc.clear_and_free_semaphores(self.sems)
        self.nc.all_engine_barrier()


def at(i, n=1):
    return bass.ds(i, n)


def topk_phase(nc, X, const, x_in, side, cond):
    E = T * D // P
    with ExitStack() as ctx:
        m = Mem(nc, ctx, "edge_")
        adj = m.sb("adj", [P, NT, D])
        key = m.sb("key", [P, NT, D], I32)
        hi = m.sb("key_hi", [P, B, E], I16)
        lo = m.sb("key_lo", [P, B, E], U16)
        mask = m.sb("mask", [P, B, E], F16)
        embt = m.sb("embt", [P, B, D])
        rank = m.sb("rank", [P, 2, D])
        zeros = m.sb("zeros", [P, D])
        fs = m.sb("fs", [P, NT])
        nmax = m.sb("nmax", [P, NT])
        rsum = m.sb("rsum", [P, NT])
        rinv = m.sb("rinv", [P, NT])
        rscale = m.sb("rscale", [P, NT])
        digit = m.sb("digit", [P, 17])
        found = m.sb("found", [P, 2, B])
        cand = m.sb("cand", [P, B])
        want = m.sb("want", [P, B])
        ge = m.sb("ge", [P, B])
        part16 = m.sb("part16", [P, B], F16)
        halves = m.sb("halves", [P, 2, B], I32)
        tkey = m.sb("tkey", [P, B], I32)
        tsign = m.sb("tsign", [P, B], I32)
        thr = m.sb("thr", [P, B], I32)
        ties = m.sb("ties", [P, NT])
        before = m.sb("before", [P, NT])
        part = m.ps("part", [P, B])
        total = m.ps("total", [P, B])
        pref = m.ps("pref", [P, B, TT])

        x_loaded = m.sem("x_loaded")
        side_loaded = m.sem("side_loaded")
        max_ready = m.sem("max_ready")
        exp_done = m.sem("exp_done")
        adj_done = m.sem("adj_done")
        diag_done = m.sem("diag_done")
        mask_ready = m.sem("mask_ready")
        part_ready = m.sem("part_ready")
        part_copied = m.sem("part_copied")
        total_ready = m.sem("total_ready")
        ties_counted = m.sem("ties_counted")
        pref_ready = m.sem("pref_ready")
        dv = m.sem("topk_dve")

        block = ctx.enter_context(nc.Block())

        @block.sync
        def _(sp):
            sp.dma_start(X[:], x_in.rearrange("b (t p) d -> p (b t) d", p=P)).then_inc(x_loaded, 16)
            sp.dma_start(fs[:], side).then_inc(side_loaded, 16)
            sp.dma_start(embt[:], cond.rearrange("(o b) d -> o b d", o=1).broadcast_to([P, B, D])).then_inc(side_loaded, 16)

        @block.scalar
        def _(act):
            act.wait_ge(max_ready, 1)
            with act.Fori(0, NT) as n:
                act.activation(adj[:, at(n), :], X[:, at(n), :], ACT.Exp, bias=nmax[:, at(n)],
                               accum_out=rsum[:, at(n)]).then_inc(exp_done, 1)

        @block.gpsimd
        def _(pool):
            pool.wait_ge(adj_done, NT)
            for t in range(TT):
                v = adj[:].rearrange("p (b t) d -> p b t d", t=TT)[:, :, t, t * P:(t + 1) * P]
                pool.affine_select(out=v, in_=v, compare_op=ALU.not_equal, fill=-3.0e38, base=0,
                                   pattern=[[0, B], [-1, P]], channel_multiplier=1).then_inc(diag_done, 1)

        PASSES = 2 * 17

        @block.tensor
        def _(pe):
            with pe.Fori(0, PASSES) as i:
                for b in range(B):
                    pe.wait_ge(mask_ready, i * B + (b + 1))
                    for j in range(E // P):
                        mm = pe.matmul(part[:, b:b + 1], mask[:, b, j * P:(j + 1) * P], const["ones16"][:, 0:1],
                                       start=(j == 0), stop=(j == E // P - 1))
                mm.then_inc(part_ready, 1)
                pe.wait_ge(part_copied, i + 1)
                pe.matmul(total[:], const["ones16"][:], part16[:], start=True, stop=True).then_inc(total_ready, 1)
            pe.wait_ge(ties_counted, NT)
            tv = ties[:].rearrange("p (b t) -> p b t", t=TT)
            pe.matmul(pref[:], const["below"][:], tv, start=True, stop=False)
            for s in range(1, TT):
                mm = pe.matmul(pref[:, :, s:TT], const["ones32"][:], tv[:, :, 0:TT - s], start=False, stop=(s == TT - 1))
            mm.then_inc(pref_ready, 1)

        @block.vector
        def _(dve):
            n_dv = [0]

            def step(ins):
                ins.then_inc(dv, 1)
                n_dv[0] += 1
                dve.wait_ge(dv, n_dv[0])

            for k in range(17):
                dve.memset(digit[:, k:k + 1], float(1 << max(15 - k, 0)))
            dve.memset(want[:], float(TOPK))
            dve.memset(found[:, 0, :], -32768.0)
            dve.memset(found[:, 1, :], 0.0)
            dve.memset(cand[:], 0.0)
            dve.memset(zeros[:], 0.0)
            dve.wait_ge(x_loaded, 16)
            dve.tensor_reduce(nmax[:], X[:], AX.X, ALU.max, negate=True).then_inc(max_ready, 1)
            dve.wait_ge(exp_done, NT)
            step(dve.reciprocal(rinv[:], rsum[:]))
            dve.wait_ge(side_loaded, 32)
            step(dve.scalar_tensor_tensor(out=rscale[:], in0=rinv[:], scalar=float(D) ** -0.5, in1=fs[:],
                                          op0=ALU.mult, op1=ALU.mult))
            with dve.Fori(0, B) as b:
                for t in range(TT):
                    a = adj[:, at(b * TT + t), :].rearrange("p o d -> p (o d)")
                    dve.scalar_tensor_tensor(out=a, in0=a, scalar=rscale[:, at(b * TT + t)],
                                             in1=embt[:, at(b), :].rearrange("p o d -> p (o d)"),
                                             op0=ALU.mult, op1=ALU.mult).then_inc(adj_done, 1)
            dve.wait_ge(diag_done, TT)
            bits = adj[:].bitcast(I32)
            step(dve.tensor_scalar(key[:], bits, 31, 0x7FFFFFFF, ALU.arith_shift_right, ALU.bitwise_and))
            step(dve.tensor_tensor(key[:], key[:], bits, ALU.bitwise_xor))
            k16 = key[:].rearrange("p n d -> p (n d)").bitcast(I16).rearrange("p (e two) -> p e two", two=2)
            dve.tensor_copy(hi[:].rearrange("p b e -> p (b e)"), k16[:, :, 1])
            step(dve.tensor_copy(lo[:].rearrange("p b e -> p (b e)"), k16[:, :, 0].bitcast(U16)))

            for half, src in enumerate((hi, lo)):
                T_ = found[:, half, :]
                base = n_dv[0]
                p0 = half * 17

                def count(i):
                    for b in range(B):
                        dve.tensor_scalar(mask[:, b, :], src[:, b, :], cand[:, b:b + 1], None,
                                          ALU.is_ge).then_inc(mask_ready, 1)
                    dve.wait_ge(part_ready, i + 1)
                    dve.tensor_copy(part16[:], part[:]).then_inc(part_copied, 1)
                    dve.wait_ge(total_ready, i + 1)

                with dve.Fori(0, 16) as k:
                    c = k * 3 + base
                    count(k + p0)
                    dve.tensor_tensor(ge[:], total[:], want[:], ALU.is_ge).then_inc(dv, 1)
                    dve.wait_ge(dv, c + 1)
                    dve.scalar_tensor_tensor(out=T_, in0=ge[:], scalar=digit[:, at(k)], in1=T_,
                                             op0=ALU.mult, op1=ALU.add).then_inc(dv, 1)
                    dve.wait_ge(dv, c + 2)
                    dve.tensor_scalar(cand[:], T_, digit[:, at(k + 1)], None, ALU.add).then_inc(dv, 1)
                    dve.wait_ge(dv, c + 3)
                n_dv[0] += 48
                count(16 + p0)
                step(dve.tensor_tensor(want[:], want[:], total[:], ALU.subtract))
                if half == 0:
                    dve.memset(cand[:], 32768.0)
                    for b in range(B):
                        ins = dve.scalar_tensor_tensor(out=lo[:, b, :], in0=hi[:, b, :], scalar=found[:, 0, b:b + 1],
                                                       in1=lo[:, b, :], op0=ALU.is_equal, op1=ALU.mult)
                    step(ins)

            step(dve.tensor_copy(halves[:], found[:]))
            step(dve.tensor_scalar(halves[:, 0, :], halves[:, 0, :], 16, None, ALU.logical_shift_left))
            step(dve.tensor_tensor(tkey[:], halves[:, 0, :], halves[:, 1, :], ALU.bitwise_or))
            step(dve.tensor_scalar(tsign[:], tkey[:], 31, 0x7FFFFFFF, ALU.arith_shift_right, ALU.bitwise_and))
            step(dve.tensor_tensor(thr[:], tkey[:], tsign[:], ALU.bitwise_xor))
            thrf = thr[:].bitcast(F32)
            eq = key[:].bitcast(F32)
            with dve.Fori(0, B) as b:
                for t in range(TT):
                    n = b * TT + t
                    dve.tensor_scalar(eq[:, at(n), :], adj[:, at(n), :], thrf[:, at(b)], None,
                                      ALU.is_equal, ALU.add, accum_out=ties[:, at(n)]).then_inc(ties_counted, 1)
            dve.wait_ge(pref_ready, 1)
            step(dve.tensor_copy(before[:].rearrange("p (b t) -> p b t", t=TT), pref[:]))
            base = n_dv[0]
            with dve.Fori(0, B) as b:
                for t in range(TT):
                    n = b * TT + t
                    c = n * 3 + base
                    r = rank[:, t % 2, :]
                    flat = lambda v: v.rearrange("p o d -> p (o d)")
                    xs, es = flat(X[:, at(n), :]), flat(eq[:, at(n), :])
                    dve.tensor_tensor_scan(r, es, zeros[:], before[:, at(n)], ALU.add, ALU.add).then_inc(dv, 1)
                    dve.scalar_tensor_tensor(out=xs, in0=flat(adj[:, at(n), :]), scalar=thrf[:, at(b)], in1=xs,
                                             op0=ALU.is_gt, op1=ALU.add)
                    dve.wait_ge(dv, c + 1)
                    dve.scalar_tensor_tensor(out=r, in0=r, scalar=want[:, at(b)], in1=es,
                                             op0=ALU.is_le, op1=ALU.mult).then_inc(dv, 1)
                    dve.wait_ge(dv, c + 2)
                    dve.tensor_tensor(xs, xs, r, ALU.add).then_inc(dv, 1)
            n_dv[0] += 3 * NT


XS = 8.0
WS = 32.0
UNSCALE = 1.0 / (XS * WS)


def flat(v):
    return v.rearrange("p o d -> p (o d)")


def products(pe, out, left, right, start, stop):
    (lh, ll), (rh, rl) = left, right
    pe.matmul(out, lh, rh, start=start, stop=False)
    pe.matmul(out, lh, rl, start=False, stop=False)
    return pe.matmul(out, ll, rh, start=False, stop=stop)


def split_weights(nc, name, jobs):
    WIDE = 2048
    pieces = []
    for src, hi, lo, scale in jobs:
        n = src.shape[2]
        for a in range(src.shape[1]):
            for c in range(0, n, WIDE):
                w = min(WIDE, n - c)
                pieces.append((src[:, a, c:c + w], hi[:, a, c:c + w], lo[:, a, c:c + w], w, scale))
    SLOTS = 3
    with ExitStack() as ctx:
        m = Mem(nc, ctx, name)
        stage = m.sb("w_stage", [P, SLOTS, WIDE])
        loaded = [m.sem(f"w_loaded_{s}") for s in range(SLOTS)]
        hi_done, lo_done = m.sem("w_hi_done"), m.sem("w_lo_done")
        block = ctx.enter_context(nc.Block())

        @block.sync
        def _(sp):
            for j, (src, _, _, w, _) in enumerate(pieces):
                if j >= SLOTS:
                    sp.wait_ge(lo_done, j - SLOTS + 1)
                sp.dma_start(stage[:, j % SLOTS, 0:w], src).then_inc(loaded[j % SLOTS], 16)

        @block.scalar
        def _(act):
            for j, (_, hi, _, w, scale) in enumerate(pieces):
                act.wait_ge(loaded[j % SLOTS], 16 * (j // SLOTS + 1))
                act.activation(hi, stage[:, j % SLOTS, 0:w], ACT.Copy, scale=scale).then_inc(hi_done, 1)

        @block.vector
        def _(dve):
            for j, (_, hi, lo, w, scale) in enumerate(pieces):
                dve.wait_ge(hi_done, j + 1)
                dve.scalar_tensor_tensor(out=lo, in0=stage[:, j % SLOTS, 0:w], scalar=scale, in1=hi, op0=ALU.mult,
                                         op1=ALU.subtract).then_inc(lo_done, 1)


class Heads:

    CREDIT = 2

    def __init__(self, m, S, PT, O, ident, scores, values, out, scale, lag=2):
        self.S, self.PT, self.O, self.ident = S, PT, O, ident
        self.scores, self.values, self.out, self.scale = scores, values, out, scale
        self.lag, self.slots = lag, 2 if lag == 2 else 4
        self.prob = m.sb("prob", [P, 2, D])
        self.turned = m.sb("turned", [P, self.slots, 2, TT, P], F16)
        self.nmax = m.sb("head_nmax", [P, TT])
        self.nbias = m.sb("head_nbias", [P, TT])
        self.rsum = m.sb("head_rsum", [P, TT])
        self.rinv = m.sb("head_rinv", [P, TT])
        self.scores_ready = m.sem("scores_ready")
        self.max_raw = m.sem("max_raw")
        self.max_ready = m.sem("max_ready")
        self.exp_done = m.sem("exp_done")
        self.turn_ready = m.sem("turn_ready")
        self.copied_a = m.sem("copied_by_act")
        self.copied_v = m.sem("copied_by_dve")
        self.pv_ready = m.sem("pv_ready")
        self.rinv_ready = m.sem("rinv_ready")
        self.out_copied = m.sem("out_copied")

    def credits(self, pool):
        for s in (self.exp_done, self.turn_ready, self.copied_a, self.copied_v, self.out_copied):
            pool.sem_inc(s, self.CREDIT)
        pool.sem_inc(self.pv_ready, self.slots)

    def pe_scores(self, pe, h, t, u):
        pe.wait_ge(self.exp_done, u + 1)
        self.scores(pe, self.S[t % 2], h, t).then_inc(self.scores_ready, 1)

    def pe_wait_copy(self, pe, u, ahead):
        pe.wait_ge(self.copied_a, u + 1 + ahead)
        pe.wait_ge(self.copied_v, u + 1 + ahead)

    def pe_turn(self, pe, t, u):
        pe.wait_ge(self.exp_done, u + 1 + self.CREDIT)
        self.pe_wait_copy(pe, u, 0)
        for s in range(TT):
            mm = pe.transpose(self.PT[t % 2][:, s * P:(s + 1) * P], self.prob[:, t % 2, s * P:(s + 1) * P],
                              self.ident)
        mm.then_inc(self.turn_ready, 1)

    def pe_values(self, pe, h, t, u):
        self.pe_wait_copy(pe, u, self.CREDIT)
        pe.wait_ge(self.out_copied, u + 1)
        for s in range(TT):
            slot = self.turned[:, t % self.slots]
            mm = products(pe, self.O[t % 2], (slot[:, 0, s, :], slot[:, 1, s, :]), self.values(h, s),
                          s == 0, s == TT - 1)
        mm.then_inc(self.pv_ready, 1)

    def act_exp(self, act, t, u):
        act.wait_ge(self.max_ready, u + 1)
        act.wait_ge(self.turn_ready, u + 1)
        bias = self.nmax if self.scale == 1.0 else self.nbias
        act.activation(self.prob[:, t % 2, :], self.S[t % 2], ACT.Exp, bias=bias[:, t:t + 1], scale=self.scale,
                       accum_out=self.rsum[:, t:t + 1]).then_inc(self.exp_done, 1)

    def act_copy(self, act, t, u):
        act.wait_ge(self.turn_ready, u + 1 + self.CREDIT)
        act.wait_ge(self.pv_ready, u + 1)
        act.activation(self.turned[:, t % self.slots, 0].rearrange("p s q -> p (s q)"), self.PT[t % 2], ACT.Copy)\
           .then_inc(self.copied_a, 1)

    def dve_max(self, dve, t, u):
        dve.wait_ge(self.scores_ready, u + 1)
        ins = dve.tensor_reduce(self.nmax[:, t:t + 1], self.S[t % 2], AX.X, ALU.max, negate=True)
        if self.scale == 1.0:
            ins.then_inc(self.max_ready, 1)
        else:
            ins.then_inc(self.max_raw, 1)
            dve.wait_ge(self.max_raw, u + 1)
            dve.tensor_scalar(self.nbias[:, t:t + 1], self.nmax[:, t:t + 1], self.scale, None, ALU.mult)\
               .then_inc(self.max_ready, 1)

    def dve_copy(self, dve, t, u):
        dve.wait_ge(self.exp_done, u + 1 + self.CREDIT)
        dve.reciprocal(self.rinv[:, t:t + 1], self.rsum[:, t:t + 1]).then_inc(self.rinv_ready, 1)
        dve.wait_ge(self.copied_a, u + 1 + self.CREDIT)
        slot = self.turned[:, t % self.slots]
        dve.tensor_tensor(slot[:, 1].rearrange("p s q -> p (s q)"), self.PT[t % 2],
                          slot[:, 0].rearrange("p s q -> p (s q)"), ALU.subtract).then_inc(self.copied_v, 1)

    def dve_out(self, dve, h, t, u):
        dve.wait_ge(self.pv_ready, u + 1 + self.slots)
        dve.wait_ge(self.rinv_ready, u + 1)
        dve.tensor_scalar(self.out(h, t), self.O[t % 2], self.rinv[:, t:t + 1], None, ALU.mult)\
           .then_inc(self.out_copied, 1)

    def run(self, eng, heads, first_unit, current, turn, done, beside=None, turn_lag=1, done_lag=None):
        stages = ((turn, turn_lag), (done, done_lag or self.lag))

        def head(h, first, last):
            u0 = first_unit + h * TT
            for t in range(TT):
                current(h, t, u0 + t)
                if beside is not None:
                    beside(h, t, last)
                for stage, lag in stages:
                    if not (first and t < lag):
                        stage(h if t >= lag else h - 1, (t - lag) % TT, u0 + (t - lag))

        self.parity, self.nth = 0, 1
        head(0, True, False)
        with eng.Fori(0, (heads - 2) // 2) as pair:
            for self.parity in (1, 0):
                self.nth = pair + 2
                head(pair * 2 + (2 - self.parity), False, False)
        self.parity = 1
        head(heads - 1, False, True)
        end = first_unit + heads * TT
        for more in range(self.lag):
            for stage, lag in stages:
                if more < lag:
                    stage(heads - 1, TT + more - lag, end + more - lag)


def small_attention_phase(nc, X, const, a, W, Wo):
    H, DH = 16, 32
    EPS = 1e-6
    w_qkv, w_out = W, Wo
    with ExitStack() as ctx:
        m = Mem(nc, ctx, "small_")
        c_T = m.sb("cond_T", [P, KD, B])
        b_emb = m.sb("b_emb", [P, 2 * KD])
        g_norm = m.sb("g_norm", [P, KD])
        g_qk = m.sb("g_qk", [P, 2, DH])
        gg = m.sb("gg", [P, 1, DH])
        mod = m.sb("mod", [P, 2 * KD, B])
        ss = m.sb("ss", [P, NT])
        rstd = m.sb("rstd", [P, NT])
        tmp = m.sb("tmp", [P, 2, D])
        xn = m.sb("xn", [P, TT, D])
        y32 = m.sb("y32", [P, KD, T])
        yh, yl = m.sb("yh", [P, KD, T], F16), m.sb("yl", [P, KD, T], F16)
        raw = m.sb("raw", [P, TT, 2, D])
        w_emb = raw[:].rearrange("p t a d -> p t (a d)")
        vh, vl = m.sb("vh", [P, TT, D], F16), m.sb("vl", [P, TT, D], F16)
        ssq = m.sb("ssq", [P, TT, 2 * H])
        rq = m.sb("rq", [P, TT, 2 * H])
        q4, k4 = m.sb("q4", [P, TT, H, 4, DH], F16), m.sb("k4", [P, TT, H, 4, DH], F16)
        qT, kT = m.sb("qT", [P, H, T], F16), m.sb("kT", [P, H, T], F16)
        O = y32
        oh, ol = yh, yl
        bank = [m.ps(f"bank{i}", [P, D]) for i in range(6)]
        q_bank = [m.ps(f"qbank{i}", [P, T], F16) for i in range(2)]

        cond_loaded = m.sem("cond_loaded")
        mod_sum = m.sem("mod_sum")
        mod_ready = m.sem("mod_ready")
        sq_done = m.sem("sq_done")
        ms_ready = m.sem("ms_ready")
        root_done = m.sem("root_done")
        rstd_ready = m.sem("rstd_ready")
        gg_ready = m.sem("gg_ready")
        xn_ready = m.sem("xn_ready")
        xT_ready = m.sem("xT_ready")
        y_ready = m.sem("y_ready")
        yh_ready = m.sem("yh_ready")
        yl_ready = m.sem("yl_ready")
        qkv_ready = m.sem("qkv_ready")
        square_ready = m.sem("square_ready")
        ssq_ready = m.sem("ssq_ready")
        hms_ready = m.sem("hms_ready")
        hroot_done = m.sem("hroot_done")
        rq_ready = m.sem("rq_ready")
        normed = m.sem("normed")
        q_gained = m.sem("q_gained")
        hi4_done = m.sem("hi4_done")
        lo4_done = m.sem("lo4_done")
        qk_turned = m.sem("qk_turned")
        q_copied = m.sem("q_copied")
        k_copied = m.sem("k_copied")
        o_turned = m.sem("o_turned")
        oh_ready = m.sem("oh_ready")
        ol_ready = m.sem("ol_ready")
        y_out = m.sem("y_out")
        y_added = m.sem("y_added")
        x_added = m.sem("x_added")
        bank_free = m.sem("bank_free")
        vl_ready = m.sem("vl_ready")

        hs = Heads(
            m, S=[bank[0][:], bank[1][:]], PT=[bank[2][:], bank[3][:]], O=[bank[4][:, 0:DH], bank[5][:, 0:DH]],
            ident=const["ident"][:],
            scores=lambda pe, s, h, t: pe.matmul(s, flat(qT[:, at(h), t * P:(t + 1) * P]), flat(kT[:, at(h), :]),
                                                 start=True, stop=True),
            values=lambda h, s: (vh[:, s, at(h * DH, DH)], vl[:, s, at(h * DH, DH)]),
            out=lambda h, t: O[:, t, at(h * DH, DH)],
            scale=1.0, lag=3)
        qkv_bank = bank[4:6]

        block = ctx.enter_context(nc.Block())

        @block.sync
        def _(sp):
            sp.dma_start(c_T[:], a["cond_columns"]).then_inc(cond_loaded, 16)
            sp.dma_start(w_emb, a["L1_cond_W_emb"].rearrange("(k p) n -> p k n", p=P)).then_inc(cond_loaded, 16)
            sp.dma_start(b_emb[:], a["b_emb_columns"]).then_inc(cond_loaded, 16)
            sp.dma_start(g_norm[:], a["g_norm_columns"]).then_inc(cond_loaded, 16)
            for j, g in enumerate(("L1_cond_g_q", "L1_cond_g_k")):
                sp.dma_start(g_qk[:, j, :], a[g].rearrange("(o d) -> o d", o=1).broadcast_to([P, DH]))\
                  .then_inc(cond_loaded, 16)

        @block.gpsimd
        def _(pool):
            hs.credits(pool)
            with pool.Fori(0, B) as b:
                for t in range(TT):
                    pool.wait_ge(bank_free, b * 12 + t * 3 + 2 + 2)
                    pool.wait_ge(ssq_ready, b * TT + t + 1)
                    pool.tensor_tensor(tmp[:].rearrange("p a d -> p (a d)"), raw[:, t].rearrange("p a d -> p (a d)"),
                                       raw[:, t].rearrange("p a d -> p (a d)"), ALU.mult).then_inc(square_ready, 1)

        @block.tensor
        def _(pe):
            pe.wait_ge(cond_loaded, 96)
            for f in range(2 * KD):
                for k in range(KD):
                    mm = pe.matmul(bank[0][:, f * B:(f + 1) * B], w_emb[:, k, f * P:(f + 1) * P], c_T[:, k, :],
                                   start=(k == 0), stop=(k == KD - 1))
            mm.then_inc(mod_sum, 1)
            pe.wait_ge(mod_ready, 3)
            with pe.Fori(0, B) as b:
                pe.wait_ge(xn_ready, (b + 1) * TT)
                for k in range(KD):
                    for t in range(TT):
                        mm = pe.transpose(bank[k][:, t * P:(t + 1) * P], xn[:, t, k * P:(k + 1) * P],
                                          const["ident"][:])
                    mm.then_inc(xT_ready, 1)
                for t in range(TT):
                    for j in range(3):
                        n = t * 3 + j
                        if n == 0:
                            pe.wait_ge(yl_ready, (b + 1) * KD)
                        pe.wait_ge(bank_free, b * 12 + n + 1)
                        if j == 1:
                            pe.wait_ge(vl_ready, b * TT + t + 1)
                        for k in range(KD):
                            mm = products(pe, qkv_bank[n % 2][:],
                                          (yh[:, k, t * P:(t + 1) * P], yl[:, k, t * P:(t + 1) * P]),
                                          (w_qkv[0][:, k, j * D:(j + 1) * D], w_qkv[1][:, k, j * D:(j + 1) * D]),
                                          k == 0, k == KD - 1)
                        mm.then_inc(qkv_ready, 1)
                hs_first = b * (H * TT)

                def turn_qk(h):
                    pe.wait_ge(q_copied, b * H + h + 1)
                    pe.wait_ge(k_copied, b * H + h + 1)
                    for i, src in enumerate((q4, k4)):
                        for t in range(TT):
                            mm = pe.transpose(q_bank[i][:, t * P:(t + 1) * P],
                                              src[:, t, at(h), :, :].rearrange("p o f d -> p (o f d)"),
                                              const["ident16"][:])
                    mm.then_inc(qk_turned, 1)

                pe.wait_ge(vl_ready, (b + 1) * TT + 1)
                pe.wait_ge(lo4_done, (b + 1) * TT * 2)
                turn_qk(0)

                def current(h, t, u):
                    if t == 0:
                        pe.wait_ge(q_copied, b * H + h + 2)
                        pe.wait_ge(k_copied, b * H + h + 2)
                    hs.pe_scores(pe, h, t, u)

                def beside(h, t, last):
                    if t == 1 and not last:
                        turn_qk(h + 1)

                hs.run(pe, H, hs_first, current, lambda h, t, u: hs.pe_turn(pe, t, u),
                       lambda h, t, u: hs.pe_values(pe, h, t, u), beside)
                pe.wait_ge(hs.out_copied, (b + 1) * (H * TT) + hs.CREDIT)
                for k in range(KD):
                    for t in range(TT):
                        mm = pe.transpose(bank[k][:, t * P:(t + 1) * P], O[:, t, k * P:(k + 1) * P],
                                          const["ident"][:])
                    mm.then_inc(o_turned, 1)
                pe.wait_ge(ol_ready, (b + 1) * KD)
                for t in range(TT):
                    pe.wait_ge(y_added, b * TT + t + 1)
                    for k in range(KD):
                        mm = products(pe, qkv_bank[t % 2][:],
                                      (oh[:, k, t * P:(t + 1) * P], ol[:, k, t * P:(t + 1) * P]),
                                      (w_out[0][:, k, :], w_out[1][:, k, :]), k == 0, k == KD - 1)
                    mm.then_inc(y_out, 1)

        @block.scalar
        def _(act):
            with act.Fori(0, NT) as n:
                act.wait_ge(sq_done, n)
                act.activation(flat(tmp[:, 0:1, :]), flat(X[:, at(n), :]), ACT.Square, accum_out=ss[:, at(n)])\
                   .then_inc(sq_done, 1)
            act.wait_ge(ms_ready, 1)
            act.activation(rstd[:], ss[:], ACT.Sqrt).then_inc(root_done, 1)
            act.wait_ge(rstd_ready, 1)
            with act.Fori(0, B) as b:
                for t in range(TT):
                    act.activation(xn[:, t, :], flat(X[:, at(b * TT + t), :]), ACT.Copy, scale=rstd[:, at(b * TT + t)])\
                       .then_inc(xn_ready, 1)
                for k in range(KD):
                    act.wait_ge(y_ready, b * KD + k + 1)
                    act.activation(yh[:, k, :], y32[:, k, :], ACT.Copy).then_inc(yh_ready, 1)
                for t in range(TT):
                    for j in range(3):
                        n = t * 3 + j
                        act.wait_ge(qkv_ready, b * 12 + n + 1)
                        dst, scale = (raw[:, t, j, :], UNSCALE) if j < 2 else (vh[:, t, :], XS * UNSCALE)
                        act.activation(dst, qkv_bank[n % 2][:], ACT.Copy, scale=scale).then_inc(bank_free, 1)
                act.wait_ge(hms_ready, b + 1)
                act.activation(rq[:].rearrange("p t h -> p (t h)"), ssq[:].rearrange("p t h -> p (t h)"), ACT.Sqrt)\
                   .then_inc(hroot_done, 1)
                act.preload_act_table(ACT.Exp)
                for t in range(TT):
                    for j, dst in enumerate((q4, k4)):
                        act.wait_ge(q_gained, b * TT * 2 + t * 2 + j + 1)
                        src = raw[:, t, j, :].rearrange("p (h d) -> p h d", h=H)
                        for e in range(2):
                            slot = e if j == 0 else 2 * e
                            ins = act.activation(dst[:, t, :, slot, :], src, ACT.Copy)
                        ins.then_inc(hi4_done, 1)

                def copy_q(h):
                    act.wait_ge(qk_turned, b * H + h + 1)
                    act.activation(flat(qT[:, at(h), :]), q_bank[0][:], ACT.Copy).then_inc(q_copied, 1)

                copy_q(0)

                def beside(h, t, last):
                    if t == 1 and not last:
                        copy_q(h + 1)

                hs.run(act, H, b * (H * TT), lambda h, t, u: hs.act_exp(act, t, u),
                       lambda h, t, u: hs.act_copy(act, t, u), lambda h, t, u: None, beside)
                for k in range(KD):
                    act.wait_ge(o_turned, b * KD + k + 1)
                    act.activation(oh[:, k, :], bank[k][:], ACT.Copy).then_inc(oh_ready, 1)

        @block.vector
        def _(dve):
            dve.wait_ge(cond_loaded, 96)
            dve.tensor_tensor(gg[:, 0, :], g_qk[:, 0, :], g_qk[:, 1, :], ALU.mult).then_inc(gg_ready, 1)
            dve.wait_ge(gg_ready, 1)
            dve.tensor_scalar(gg[:], gg[:], float(DH) ** -0.5, None, ALU.mult).then_inc(gg_ready, 1)
            dve.wait_ge(mod_sum, 1)
            for f in range(2 * KD):
                dve.tensor_scalar(mod[:, f, :], bank[0][:, f * B:(f + 1) * B], b_emb[:, f:f + 1],
                                  1.0 if f < KD else 0.0, ALU.add, ALU.add)
            dve.engine_nop().then_inc(mod_ready, 1)
            dve.wait_ge(mod_ready, 1)
            for f in range(KD):
                dve.tensor_scalar(mod[:, f, :], mod[:, f, :], g_norm[:, f:f + 1], XS, ALU.mult, ALU.mult)
            dve.tensor_scalar(mod[:, KD:2 * KD, :], mod[:, KD:2 * KD, :], XS, None, ALU.mult).then_inc(mod_ready, 1)
            dve.wait_ge(mod_ready, 2)
            dve.engine_nop().then_inc(mod_ready, 1)
            dve.wait_ge(sq_done, NT)
            dve.tensor_scalar(ss[:], ss[:], 1.0 / D, EPS, ALU.mult, ALU.add).then_inc(ms_ready, 1)
            dve.wait_ge(root_done, 1)
            dve.reciprocal(rstd[:], rstd[:]).then_inc(rstd_ready, 1)
            dve.sem_inc(bank_free, 2)
            dve.sem_inc(y_added, 2)
            dve.sem_inc(q_copied, 1)
            dve.sem_inc(k_copied, 1)
            dve.sem_inc(ssq_ready, 1)
            dve.sem_inc(vl_ready, 1)
            with dve.Fori(0, B) as b:
                for k in range(KD):
                    dve.wait_ge(xT_ready, b * KD + k + 1)
                    dve.tensor_scalar(y32[:, k, :], bank[k][:], mod[:, k, at(b)], mod[:, KD + k, at(b)], ALU.mult,
                                      ALU.add).then_inc(y_ready, 1)
                for k in range(KD):
                    dve.wait_ge(yh_ready, b * KD + k + 1)
                    dve.tensor_tensor(yl[:, k, :], y32[:, k, :], yh[:, k, :], ALU.subtract).then_inc(yl_ready, 1)
                for t in range(TT):
                    dve.wait_ge(bank_free, b * 12 + t * 3 + 3 + 2)
                    dve.scalar_tensor_tensor(out=vl[:, t, :], in0=qkv_bank[(t * 3 + 2) % 2][:], scalar=XS * UNSCALE,
                                             in1=vh[:, t, :], op0=ALU.mult, op1=ALU.subtract).then_inc(vl_ready, 1)
                    dve.wait_ge(square_ready, b * TT + t + 1)
                    dve.tensor_reduce(ssq[:, t, :], tmp[:].rearrange("p a (h d) -> p (a h) d", d=DH), AX.X, ALU.add)\
                       .then_inc(ssq_ready, 1)
                dve.wait_ge(ssq_ready, b * TT + TT + 1)
                dve.tensor_scalar(ssq[:], ssq[:], 1.0 / DH, EPS, ALU.mult, ALU.add).then_inc(hms_ready, 1)
                dve.wait_ge(hroot_done, b + 1)
                dve.reciprocal(rq[:], rq[:]).then_inc(rq_ready, 1)
                dve.wait_ge(rq_ready, b + 1)
                for t in range(TT):
                    for j in range(2):
                        v = raw[:, t, j, :].rearrange("p (h d) -> p h d", h=H)
                        r = rq[:, t, j * H:(j + 1) * H].rearrange("p (h o) -> p h o", o=1).broadcast_to([P, H, DH])
                        if j == 0:
                            dve.tensor_tensor(v, v, r, ALU.mult).then_inc(normed, 1)
                            dve.wait_ge(normed, b * TT + t + 1)
                            dve.tensor_tensor(v, v, gg[:].broadcast_to([P, H, DH]), ALU.mult).then_inc(q_gained, 1)
                        else:
                            dve.tensor_tensor(v, v, r, ALU.mult).then_inc(q_gained, 1)
                for t in range(TT):
                    for j, dst in enumerate((q4, k4)):
                        src = raw[:, t, j, :].rearrange("p (h d) -> p h d", h=H)
                        dve.wait_ge(hi4_done, b * TT * 2 + t * 2 + j + 1)
                        for e in range(2):
                            slot = 2 + e if j == 0 else 1 + 2 * e
                            ins = dve.tensor_tensor(dst[:, t, :, slot, :], src, dst[:, t, :, 0, :], ALU.subtract)
                        ins.then_inc(lo4_done, 1)

                def copy_k(h):
                    dve.wait_ge(qk_turned, b * H + h + 1)
                    dve.tensor_copy(flat(kT[:, at(h), :]), q_bank[1][:]).then_inc(k_copied, 1)

                copy_k(0)

                def beside(h, t, last):
                    if t == 1 and not last:
                        copy_k(h + 1)

                hs.run(dve, H, b * (H * TT), lambda h, t, u: hs.dve_max(dve, t, u),
                       lambda h, t, u: hs.dve_copy(dve, t, u), lambda h, t, u: hs.dve_out(dve, h, t, u), beside,
                       turn_lag=2)
                for k in range(KD):
                    dve.wait_ge(oh_ready, b * KD + k + 1)
                    dve.tensor_tensor(ol[:, k, :], bank[k][:], oh[:, k, :], ALU.subtract).then_inc(ol_ready, 1)
                for t in range(TT):
                    xs = flat(X[:, at(b * TT + t), :])
                    dve.wait_ge(y_out, b * TT + t + 1)
                    dve.scalar_tensor_tensor(out=xs, in0=O[:, t, :], scalar=1.0 / XS, in1=xs,
                                             op0=ALU.mult, op1=ALU.add).then_inc(x_added, 1)
                    dve.wait_ge(x_added, b * TT + t + 1)
                    dve.scalar_tensor_tensor(out=xs, in0=qkv_bank[t % 2][:], scalar=UNSCALE, in1=xs,
                                             op0=ALU.mult, op1=ALU.add).then_inc(y_added, 1)


HS = 64.0
RS = 256.0
GS = HS * RS
GIS = 64.0


def gate_input_phase(nc, X, const, a, w_ih, gi):
    G = 3 * KD
    with ExitStack() as ctx:
        m = Mem(nc, ctx, "gatein_")
        bias = m.sb("gate_bias", [P, 2 * G])
        col = m.sb("gate_col", [P, G])
        x32 = m.sb("gi_x32", [P, TT, D])
        xh, xl = m.sb("gi_xh", [P, KD, T], F16), m.sb("gi_xl", [P, KD, T], F16)
        bank = [m.ps(f"gbank{i}", [P, D]) for i in range(8)]
        bias_loaded, col_ready = m.sem("bias_loaded"), m.sem("col_ready")
        x_copied, x_turned = m.sem("gx_copied"), m.sem("gx_turned")
        xh_ready, xl_ready = m.sem("gxh_ready"), m.sem("gxl_ready")
        full = m.sb("gi_full", [P, 2, T])
        sum_ready, out_taken = m.sem("gate_sum"), m.sem("gate_out_taken")
        hi_done, lo_done = m.sem("gi_hi_done"), m.sem("gi_lo_done")
        block = ctx.enter_context(nc.Block())
        out_bank = bank[4:8]
        place = lambda g: g if g < KD else g + KD if g < 2 * KD else g - KD

        @block.sync
        def _(sp):
            sp.dma_start(bias[:, 0:G], a["b_ih_columns"]).then_inc(bias_loaded, 16)
            sp.dma_start(bias[:, G:2 * G], a["b_hh_columns"]).then_inc(bias_loaded, 16)

        @block.gpsimd
        def _(pool):
            with pool.Fori(0, B) as b:
                for t in range(TT):
                    pool.wait_ge(x_turned, b * KD)
                    pool.tensor_copy(x32[:, t, :], flat(X[:, at(b * TT + t), :])).then_inc(x_copied, 1)

        @block.tensor
        def _(pe):
            with pe.Fori(0, B) as b:
                pe.wait_ge(x_copied, (b + 1) * TT)
                pe.wait_ge(xl_ready, b * KD)
                for k in range(KD):
                    for t in range(TT):
                        mm = pe.transpose(bank[k][:, t * P:(t + 1) * P], x32[:, t, k * P:(k + 1) * P],
                                          const["ident"][:])
                    mm.then_inc(x_turned, 1)
                pe.wait_ge(xl_ready, (b + 1) * KD)
                for g in range(G):
                    pe.wait_ge(out_taken, b * G + g + 1)
                    for k in range(KD):
                        mm = products(pe, out_bank[g % 4][:],
                                      (w_ih[0][:, k, g * P:(g + 1) * P], w_ih[1][:, k, g * P:(g + 1) * P]),
                                      (xh[:, k, :], xl[:, k, :]), k == 0, k == KD - 1)
                    mm.then_inc(sum_ready, 1)

        @block.scalar
        def _(act):
            act.wait_ge(col_ready, 2)
            act.sem_inc(out_taken, 4)
            with act.Fori(0, B) as b:
                for k in range(KD):
                    act.wait_ge(x_turned, b * KD + k + 1)
                    act.wait_ge(sum_ready, b * G)
                    act.activation(xh[:, k, :], bank[k][:], ACT.Copy, scale=XS).then_inc(xh_ready, 1)
                for g in range(G):
                    act.wait_ge(sum_ready, b * G + g + 1)
                    act.wait_ge(lo_done, b * G + g + 1)
                    act.activation(full[:, g % 2, :], out_bank[g % 4][:], ACT.Identity,
                                   bias=col[:, g:g + 1], scale=GIS * UNSCALE).then_inc(out_taken, 1)
                    act.wait_ge(out_taken, b * G + g + 5)
                    act.activation(flat(gi[:, 0, place(g), at(b), :]), full[:, g % 2, :], ACT.Copy).then_inc(hi_done, 1)

        @block.vector
        def _(dve):
            dve.wait_ge(bias_loaded, 32)
            dve.tensor_tensor(col[:, 0:2 * KD], bias[:, 0:2 * KD], bias[:, G:G + 2 * KD], ALU.add)
            dve.tensor_copy(col[:, 2 * KD:G], bias[:, 2 * KD:G]).then_inc(col_ready, 1)
            dve.wait_ge(col_ready, 1)
            dve.tensor_scalar(col[:], col[:], GIS, None, ALU.mult).then_inc(col_ready, 1)
            dve.sem_inc(lo_done, 2)
            with dve.Fori(0, B) as b:
                for k in range(KD):
                    dve.wait_ge(xh_ready, b * KD + k + 1)
                    dve.scalar_tensor_tensor(out=xl[:, k, :], in0=bank[k][:], scalar=XS, in1=xh[:, k, :],
                                             op0=ALU.mult, op1=ALU.subtract).then_inc(xl_ready, 1)
                for g in range(G):
                    dve.wait_ge(hi_done, b * G + g + 1)
                    dve.tensor_tensor(flat(gi[:, 1, place(g), at(b), :]), full[:, g % 2, :], flat(gi[:, 0, place(g), at(b), :]),
                                      ALU.subtract).then_inc(lo_done, 1)


class WeightStore:

    WIDE = 1024
    SLOTS = 2

    def __init__(self, nc, a):
        def scratch(name, shape):
            return nc.dram_tensor(name, shape, F16, kind="Internal").ap()

        self.qk = scratch("w_qk_parts", (P, DIT_H, 2, 2, KD, DIT_DH))
        self.v = scratch("w_v_parts", (P, 2, KD, INNER))
        self.out = scratch("w_out_parts", (P, 2, INNER // P, D))
        self.w1 = scratch("w_1_parts", (P, 2, KD, MLP))
        self.w2 = scratch("w_2_parts", (P, 2, MLP // P, D))
        rows = lambda w: w.rearrange("(k p) n -> p k n", p=P)
        qkv = rows(a["L3_cond_qkv_w"])
        W = self.WIDE
        self.pieces = []
        wide = W // (KD * DIT_DH)
        for h in range(0, DIT_H, wide):
            for i in range(2):
                c = i * INNER + h * DIT_DH
                self.pieces.append((qkv[:, :, c:c + wide * DIT_DH], self.qk[:, h:h + wide, i], True))
        for src, dst in ((qkv[:, :, 2 * INNER:3 * INNER], self.v), (rows(a["L3_cond_out_w"]), self.out),
                         (rows(a["L3_cond_ffn_w1"]), self.w1), (rows(a["L3_cond_ffn_w2"]), self.w2)):
            n = src.shape[2]
            if n >= W:
                for q in range(src.shape[1]):
                    for c in range(0, n, W):
                        self.pieces.append((src[:, q, c:c + W], dst[:, :, q, c:c + W], False))
            else:
                for q in range(0, src.shape[1], W // n):
                    self.pieces.append((src[:, q:q + W // n, :],
                                        dst[:, :, q:q + W // n, :].rearrange("p e k n -> p e (k n)"), False))

    def place(self, m):
        self.given = m.sb("given_w", [P, self.SLOTS, self.WIDE])
        self.parts = m.sb("parts_w", [P, self.SLOTS, 2 * self.WIDE], F16)
        self.loaded = [m.sem(f"piece_loaded_{s}") for s in range(self.SLOTS)]
        self.stored = [m.sem(f"piece_stored_{s}") for s in range(self.SLOTS)]
        self.scaled, self.hi_done, self.lo_done = m.sem("piece_scaled"), m.sem("piece_hi"), m.sem("piece_lo")

    def load(self, sp, j):
        src, s = self.pieces[j][0], j % self.SLOTS
        dst = self.given[:, s, :]
        if len(src.shape) == 3:
            dst = dst.rearrange("p (k n) -> p k n", k=src.shape[1])
        sp.dma_start(dst, src).then_inc(self.loaded[s], 16)

    def sync(self, sp):
        S = self.SLOTS
        for j in range(S):
            self.load(sp, j)
        for j, (_, dst, by_head) in enumerate(self.pieces):
            s = j % S
            sp.wait_ge(self.lo_done, j + 1)
            out = self.parts[:, s, :]
            out = (out.rearrange("p (h e k n) -> p h e k n", e=2, k=KD, n=DIT_DH) if by_head
                   else out.rearrange("p (e n) -> p e n", e=2))
            sp.dma_start(dst, out).then_inc(self.stored[s], 16)
            if j + S < len(self.pieces):
                self.load(sp, j + S)
        for s in range(S):
            sp.wait_ge(self.stored[s], 16 * len(self.pieces[s::S]))

    def pool(self, pool):
        S = self.SLOTS
        parts_begun = 0
        for j, (_, _, by_head) in enumerate(self.pieces):
            s = j % S
            w = self.given[:, s, :]
            pool.wait_ge(self.loaded[s], 16 * (j // S + 1))
            pool.tensor_scalar(w, w, WS, None, ALU.mult).then_inc(self.scaled, 1)
            pool.wait_ge(self.scaled, j + 1)
            if j >= S:
                pool.wait_ge(self.stored[s], 16 * (j // S))
            out = self.parts[:, s, :]
            if by_head:
                v = out.rearrange("p (h e k n) -> p h e k n", e=2, k=KD, n=DIT_DH)
                g = w.rearrange("p (k h n) -> p k h n", k=KD, n=DIT_DH)
                pairs = [(v[:, h, 0], v[:, h, 1], g[:, :, h, :]) for h in range(g.shape[2])]
            else:
                pairs = [(out[:, 0:self.WIDE], out[:, self.WIDE:2 * self.WIDE], w)]
            for n, (hi, lo, src) in enumerate(pairs):
                pool.tensor_copy(hi, src).then_inc(self.hi_done, 1)
            parts_begun += len(pairs)
            pool.wait_ge(self.hi_done, parts_begun)
            for n, (hi, lo, src) in enumerate(pairs):
                ins = pool.tensor_tensor(lo, src, hi, ALU.subtract)
            ins.then_inc(self.lo_done, 1)


def gru_phase(nc, X, const, a, w_hh, gi, x_out, store):
    G = 3 * KD
    HALF = KD // 2
    A, Z = slice(0, HALF), slice(HALF, KD)
    every, first, second = range(KD), range(HALF), range(HALF, KD)
    with ExitStack() as ctx:
        m = Mem(nc, ctx, "gru_")
        if store is not None:
            store.place(m)
        hist = m.sb("hist", [P, KD, B, T + 1])
        h0 = m.sb("h0", [P, KD, B])
        b_hh = m.sb("b_hh", [P, G])
        ones = m.sb("gru_ones", [P, B])
        scaled_ident = m.sb("scaled_ident", [P, P], F16)
        bn32 = m.sb("bn32", [P, KD, B])
        bn = m.sb("bn", [P, 2, KD, B], F16)
        state = m.sb("state", [P, 2, KD, B])
        parts = m.sb("state_parts", [P, KD, 2 * B], F16)
        r_in, z_in, n_in = (m.sb(f"{g}_in", [P, KD, B]) for g in "rzn")
        r, keep, n = (m.sb(f"{g}_gate", [P, KD, B]) for g in ("r", "new", "n"))
        u, v, d, e = (m.sb(s, [P, KD, B]) for s in "uvde")
        r_bank, na_bank, nb_bank, za_bank, zb_bank, turned_0, turned_1 = \
            (m.ps(s, [P, 4 * P]) for s in ("sum_r", "sum_na", "sum_nb", "sum_za", "sum_zb", "turned_0", "turned_1"))
        turned = [turned_0, turned_1]
        start_loaded, made = m.sem("start_loaded"), m.sem("gru_made")
        hi_a, hi_b, lo_a, lo_b = (m.sem(s) for s in ("hi_a", "hi_b", "lo_a", "lo_b"))
        state_a, state_b, kept = m.sem("state_a"), m.sem("state_b"), m.sem("history_kept")
        r_sum, na_sum, nb_sum, za_sum, zb_sum = (m.sem(s) for s in ("r_sum", "na_sum", "nb_sum", "za_sum", "zb_sum"))
        r_in_ready, r_ready = m.sem("r_in_ready"), m.sem("r_ready")
        ua, ub, va, vb = (m.sem(s) for s in ("ua_ready", "ub_ready", "va_ready", "vb_ready"))
        n_in_a, n_in_b, n_a, n_b = (m.sem(s) for s in ("n_in_a", "n_in_b", "n_a", "n_b"))
        za_in, zb_in, keep_a, keep_b = (m.sem(s) for s in ("za_in_ready", "zb_in_ready", "keep_a", "keep_b"))
        da, db, ea, eb = (m.sem(s) for s in ("da_ready", "db_ready", "ea_ready", "eb_ready"))
        back_turned, added, stored = m.sem("back_turned"), m.sem("added"), m.sem("gru_stored")
        block = ctx.enter_context(nc.Block())

        def column(bank, f):
            return bank[:, f * 2 * B:(f + 1) * 2 * B]

        def n_part(fs):
            columns = r_bank[:, (KD + fs[0]) * 2 * B:(KD + fs[-1] + 1) * 2 * B]
            return columns.rearrange("p (f c) -> p f c", c=2 * B)[:, :, 0:B]

        @block.sync
        def _(sp):
            sp.dma_start(h0[:], a["cond_columns"]).then_inc(start_loaded, 16)
            sp.dma_start(b_hh[:], a["b_hh_columns"]).then_inc(start_loaded, 16)
            if store is not None:
                store.sync(sp)
            xo = x_out.rearrange("b (t p) d -> p (b t) d", p=P)
            for b in range(B):
                sp.wait_ge(added, (b + 1) * TT)
                sp.dma_start(xo[:, b * TT:(b + 1) * TT, :], X[:, b * TT:(b + 1) * TT, :]).then_inc(stored, 16)
            sp.wait_ge(stored, 16 * B)

        @block.gpsimd
        def _(pool):
            if store is not None:
                store.pool(pool)

        @block.tensor
        def _(pe):
            def low(bank, gate, fs, ks):
                for f in fs:
                    for k in ks:
                        c = (gate * KD + f) * P
                        mm = pe.matmul(column(bank, f)[:, 0:B], w_hh[1][:, k, c:c + P], parts[:, k, 0:B],
                                       start=False, stop=False, skip_group_check=True)
                return mm

            def high(bank, gate, fs, ks):
                for f in fs:
                    for k in ks:
                        c = (gate * KD + f) * P
                        mm = pe.matmul(column(bank, f), w_hh[0][:, k, c:c + P], parts[:, k, :],
                                       start=False, stop=False, skip_group_check=True)
                return mm

            def bring(out, what, start=True):
                pe.matmul(out, scaled_ident[:], what, start=start, stop=False, skip_group_check=True)

            def columns(bank, fs):
                return bank[:, fs[0] * 2 * B:(fs[-1] + 1) * 2 * B]

            def step_in(e, g, n, i):
                return gi[:, e, g:g + n, :, at(i)].rearrange("p f b o -> p f (b o)")

            pe.wait_ge(made, KD + 6)
            with pe.Fori(0, T // 2) as pair:
                for par in range(2):
                    i = pair * 2 + par
                    pe.wait_ge(n_in_b, i + 1)
                    for bank, fs in ((na_bank, first), (nb_bank, second)):
                        bring(columns(bank, fs), bn[:, :, fs[0]:fs[-1] + 1, :].rearrange("p e f b -> p f e b"))
                    r_and_n = r_bank[:, 0:2 * KD * 2 * B].rearrange("p (f c) -> p f c", c=2 * B)[:, :, 0:B]
                    for e in range(2):
                        bring(r_and_n, step_in(e, 0, 2 * KD, i), start=e == 0)
                    pe.wait_ge(hi_a, i + 1)
                    low(r_bank, 0, every, first)
                    low(na_bank, 2, first, first)
                    pe.wait_ge(zb_in, i + 1)
                    for bank, fs in ((za_bank, first), (zb_bank, second)):
                        bring(columns(bank, fs), gi[:, :, 2 * KD + fs[0]:2 * KD + fs[-1] + 1, :, at(i)]
                              .rearrange("p e f b o -> p f e (b o)"))
                    low(nb_bank, 2, second, first)
                    low(za_bank, 1, first, first)
                    low(zb_bank, 1, second, first)
                    pe.wait_ge(hi_b, i + 1)
                    low(r_bank, 0, every, second)
                    pe.wait_ge(lo_a, i + 1)
                    high(r_bank, 0, every, first)
                    pe.wait_ge(lo_b, i + 1)
                    high(r_bank, 0, every, second).then_inc(r_sum, 1)
                    low(na_bank, 2, first, second)
                    high(na_bank, 2, first, every).then_inc(na_sum, 1)
                    low(za_bank, 1, first, second)
                    high(za_bank, 1, first, every).then_inc(za_sum, 1)
                    low(nb_bank, 2, second, second)
                    high(nb_bank, 2, second, every).then_inc(nb_sum, 1)
                    low(zb_bank, 1, second, second)
                    high(zb_bank, 1, second, every).then_inc(zb_sum, 1)
            pe.wait_ge(kept, T + 1)
            for b in range(B):
                for t in range(TT):
                    w = b * TT + t
                    if w >= 2:
                        pe.wait_ge(added, w - 1)
                    for f in range(KD):
                        mm = pe.transpose(turned[w % 2][:, f * P:(f + 1) * P],
                                          hist[:, f, b, 1 + t * P:1 + (t + 1) * P], const["ident"][:])
                    mm.then_inc(back_turned, 1)

        step_of = lambda v, i: v[:, :, :, at(i)].rearrange("p f b o -> p f (b o)")

        @block.scalar
        def _(act):
            act.preload_act_table_set("sigmoid_and_others")
            with act.Fori(0, T // 2) as pair:
                for par in range(2):
                    i = pair * 2 + par
                    act.wait_ge(state_a, i + 1)
                    act.wait_ge(state_b, i + 1)
                    act.activation(step_of(hist, i), state[:, par], ACT.Copy).then_inc(kept, 1)
                    act.wait_ge(r_in_ready, i + 1)
                    act.activation(r[:], r_in[:], ACT.Sigmoid, scale=1.0 / GS).then_inc(r_ready, 1)
                    act.wait_ge(n_in_a, i + 1)
                    act.activation(n[:, A], n_in[:, A], ACT.Tanh, scale=1.0 / GS).then_inc(n_a, 1)
                    act.wait_ge(za_in, i + 1)
                    act.activation(keep[:, A], z_in[:, A], ACT.Sigmoid, scale=-1.0 / GS).then_inc(keep_a, 1)
                    act.wait_ge(n_in_b, i + 2)
                    act.activation(n[:, Z], n_in[:, Z], ACT.Tanh, scale=1.0 / GS).then_inc(n_b, 1)
                    act.wait_ge(zb_in, i + 2)
                    act.activation(keep[:, Z], z_in[:, Z], ACT.Sigmoid, scale=-1.0 / GS).then_inc(keep_b, 1)
            act.wait_ge(state_a, T + 1)
            act.wait_ge(state_b, T + 1)
            act.activation(hist[:, :, :, T], state[:, T % 2], ACT.Copy).then_inc(kept, 1)

        @block.vector
        def _(dve):
            dve.wait_ge(start_loaded, 32)
            dve.memset(ones[:], GIS).then_inc(made, 1)
            dve.tensor_scalar(scaled_ident[:], const["ident16"][:], GS / GIS, None, ALU.mult).then_inc(made, 1)
            dve.wait_ge(made, 2)
            for f in range(KD):
                dve.tensor_scalar(bn32[:, f, :], ones[:], b_hh[:, 2 * KD + f:2 * KD + f + 1], None, ALU.mult)\
                   .then_inc(made, 1)
            dve.wait_ge(made, KD + 2)
            dve.tensor_copy(bn[:, 0], bn32[:]).then_inc(made, 1)
            dve.wait_ge(made, KD + 3)
            dve.tensor_tensor(bn[:, 1], bn32[:], bn[:, 0], ALU.subtract).then_inc(made, 1)
            dve.tensor_scalar(state[:, 0], h0[:], HS, None, ALU.mult).then_inc(state_a, 1)
            dve.wait_ge(state_a, 1)
            dve.tensor_copy(parts[:, :, 0:B], state[:, 0]).then_inc(made, 1)
            dve.wait_ge(made, KD + 5)
            dve.tensor_tensor(parts[:, :, B:2 * B], state[:, 0], parts[:, :, 0:B], ALU.subtract).then_inc(made, 1)
            for s in (state_b, hi_a, hi_b, lo_a, lo_b, n_in_b, zb_in):
                dve.sem_inc(s, 1)

            def total(out, bank, fs):
                columns = bank[:, fs[0] * 2 * B:(fs[-1] + 1) * 2 * B]
                return dve.tensor_reduce(out, columns.rearrange("p (f e b) -> p f b e", e=2, b=B), AX.X, ALU.add)

            with dve.Fori(0, T // 2) as pair:
                for par in range(2):
                    i = pair * 2 + par
                    before, after = state[:, par], state[:, 1 - par]
                    dve.wait_ge(r_sum, i + 1)
                    total(r_in[:], r_bank, every).then_inc(r_in_ready, 1)
                    dve.wait_ge(na_sum, i + 1)
                    total(u[:, A], na_bank, first).then_inc(ua, 1)
                    dve.wait_ge(ua, i + 1)
                    dve.wait_ge(r_ready, i + 1)
                    dve.tensor_tensor(v[:, A], u[:, A], r[:, A], ALU.mult).then_inc(va, 1)
                    dve.wait_ge(va, i + 1)
                    dve.tensor_tensor(n_in[:, A], v[:, A], n_part(first), ALU.add).then_inc(n_in_a, 1)
                    dve.wait_ge(za_sum, i + 1)
                    total(z_in[:, A], za_bank, first).then_inc(za_in, 1)
                    dve.wait_ge(nb_sum, i + 1)
                    total(u[:, Z], nb_bank, second).then_inc(ub, 1)
                    dve.wait_ge(n_a, i + 1)
                    dve.scalar_tensor_tensor(out=d[:, A], in0=n[:, A], scalar=HS, in1=before[:, A], op0=ALU.mult,
                                             op1=ALU.subtract).then_inc(da, 1)
                    dve.wait_ge(ub, i + 1)
                    dve.tensor_tensor(v[:, Z], u[:, Z], r[:, Z], ALU.mult).then_inc(vb, 1)
                    dve.wait_ge(da, i + 1)
                    dve.wait_ge(keep_a, i + 1)
                    dve.tensor_tensor(e[:, A], d[:, A], keep[:, A], ALU.mult).then_inc(ea, 1)
                    dve.wait_ge(vb, i + 1)
                    dve.tensor_tensor(n_in[:, Z], v[:, Z], n_part(second), ALU.add).then_inc(n_in_b, 1)
                    dve.wait_ge(zb_sum, i + 1)
                    total(z_in[:, Z], zb_bank, second).then_inc(zb_in, 1)
                    dve.wait_ge(ea, i + 1)
                    dve.tensor_tensor(parts[:, A, 0:B], e[:, A], before[:, A], ALU.add).then_inc(hi_a, 1)
                    dve.tensor_tensor(after[:, A], e[:, A], before[:, A], ALU.add).then_inc(state_a, 1)
                    dve.wait_ge(n_b, i + 1)
                    dve.scalar_tensor_tensor(out=d[:, Z], in0=n[:, Z], scalar=HS, in1=before[:, Z], op0=ALU.mult,
                                             op1=ALU.subtract).then_inc(db, 1)
                    dve.wait_ge(db, i + 1)
                    dve.wait_ge(keep_b, i + 1)
                    dve.tensor_tensor(e[:, Z], d[:, Z], keep[:, Z], ALU.mult).then_inc(eb, 1)
                    dve.wait_ge(eb, i + 1)
                    dve.tensor_tensor(parts[:, Z, 0:B], e[:, Z], before[:, Z], ALU.add).then_inc(hi_b, 1)
                    dve.tensor_tensor(after[:, Z], e[:, Z], before[:, Z], ALU.add).then_inc(state_b, 1)
                    dve.wait_ge(hi_a, i + 2)
                    dve.wait_ge(state_a, i + 2)
                    dve.tensor_tensor(parts[:, A, B:2 * B], after[:, A], parts[:, A, 0:B], ALU.subtract)\
                       .then_inc(lo_a, 1)
                    dve.wait_ge(hi_b, i + 2)
                    dve.wait_ge(state_b, i + 2)
                    dve.tensor_tensor(parts[:, Z, B:2 * B], after[:, Z], parts[:, Z, 0:B], ALU.subtract)\
                       .then_inc(lo_b, 1)
            for w in range(NT):
                dve.wait_ge(back_turned, w + 1)
                dve.scalar_tensor_tensor(out=X[:, w, :], in0=turned[w % 2][:], scalar=1.0 / HS, in1=X[:, w, :],
                                         op0=ALU.mult, op1=ALU.add).then_inc(added, 1)


def dit_condition_phase(nc, a, store, mod, gates_dram, row_dram):
    with ExitStack() as ctx:
        m = Mem(nc, ctx, "ditcond_")
        w = m.sb("ada_w", [P, KD, 6 * D])
        w_out = m.sb("w_out", [P, 2, INNER // P, D], F16)
        c_T = m.sb("cond_T", [P, KD, B])
        b_col = m.sb("ada_b_col", [P, 6 * KD])
        b_row = m.sb("ada_b_row", [B, 2, D])
        gate = m.sb("gate", [B, 2, D])
        bv = m.sb("bv", [P, 3 * DIT_H])
        bvh, bvl = m.sb("bv_hi", [P, DIT_H], F16), m.sb("bv_lo", [P, DIT_H], F16)
        ob = m.sb("ob", [1, D])
        col_sum = m.ps("col_sum", [P, 4, KD, B])
        row_sum = [m.ps(f"row_sum{i}", [P, D]) for i in range(3)]
        loaded = m.sem("loaded")
        cols_ready, rows_ready, bv_ready, mapped = (m.sem(s) for s in ("cols", "rows", "bv_ready", "mapped"))
        bvh_ready, out_ready, stored = m.sem("bvh_ready"), m.sem("out_ready"), m.sem("stored")
        block = ctx.enter_context(nc.Block())
        chunks = (1, 0, 4, 3)

        @block.sync
        def _(sp):
            sp.dma_start(c_T[:], a["cond_columns"]).then_inc(loaded, 16)
            sp.dma_start(w[:], a["L3_cond_ada_w"].rearrange("(k p) n -> p k n", p=P)).then_inc(loaded, 16)
            sp.dma_start(b_col[:], a["ada_b_columns"]).then_inc(loaded, 16)
            rows = a["L3_cond_ada_b"].rearrange("(o j d) -> o j d", o=1, d=D).broadcast_to([B, 6, D])
            sp.dma_start(b_row[:, 0, :], rows[:, 2, :]).then_inc(loaded, 16)
            sp.dma_start(b_row[:, 1, :], rows[:, 5, :]).then_inc(loaded, 16)
            sp.dma_start(bv[:], a["qkv_b_columns"]).then_inc(loaded, 16)
            sp.dma_start(ob[:], a["L3_cond_out_b"].rearrange("(o d) -> o d", o=1)).then_inc(loaded, 16)
            sp.dma_start(w_out[:], store.out).then_inc(loaded, 16)
            sp.wait_ge(out_ready, 3)
            sp.dma_start(gates_dram, gate[:]).then_inc(stored, 16)
            sp.dma_start(row_dram, ob[:]).then_inc(stored, 16)
            sp.wait_ge(stored, 32)

        @block.tensor
        def _(pe):
            pe.wait_ge(loaded, 128)
            for i, j in enumerate(chunks):
                for f in range(KD):
                    for k in range(KD):
                        mm = pe.matmul(col_sum[:, i, f, :], w[:, k, j * D + f * P:j * D + (f + 1) * P], c_T[:, k, :],
                                       start=(k == 0), stop=(k == KD - 1))
            mm.then_inc(cols_ready, 1)
            for i, j in enumerate((2, 5)):
                for k in range(KD):
                    mm = pe.matmul(row_sum[i][0:B, :], c_T[:, k, :], w[:, k, j * D:(j + 1) * D], start=(k == 0),
                                   stop=(k == KD - 1))
            mm.then_inc(rows_ready, 1)
            pe.wait_ge(bv_ready, 1)
            for h in range(DIT_H):
                mm = products(pe, row_sum[2][0:1, :], (bvh[:, h:h + 1], bvl[:, h:h + 1]),
                              (w_out[:, 0, h, :], w_out[:, 1, h, :]), h == 0, h == DIT_H - 1)
            mm.then_inc(mapped, 1)

        @block.vector
        def _(dve):
            dve.wait_ge(loaded, 128)
            v = bv[:, 2 * DIT_H:3 * DIT_H]
            dve.tensor_scalar(bvh[:], v, XS, None, ALU.mult).then_inc(bvh_ready, 1)
            dve.wait_ge(bvh_ready, 1)
            dve.scalar_tensor_tensor(out=bvl[:], in0=v, scalar=XS, in1=bvh[:], op0=ALU.mult, op1=ALU.subtract)\
               .then_inc(bv_ready, 1)
            dve.wait_ge(cols_ready, 1)
            for i, j in enumerate(chunks):
                for f in range(KD):
                    dve.tensor_scalar(mod[:, i, f, :], col_sum[:, i, f, :], b_col[:, j * KD + f:j * KD + f + 1],
                                      1.0 if i in (SCALE1, SCALE2) else 0.0, ALU.add, ALU.add).then_inc(bvh_ready, 1)
            dve.wait_ge(bvh_ready, 1 + 4 * KD)
            dve.tensor_scalar(mod[:], mod[:], XS, None, ALU.mult)
            dve.wait_ge(rows_ready, 1)
            for i in range(2):
                dve.tensor_tensor(gate[:, i, :], row_sum[i][0:B, :], b_row[:, i, :], ALU.add).then_inc(out_ready, 1)
            dve.wait_ge(mapped, 1)
            dve.scalar_tensor_tensor(out=ob[:], in0=row_sum[2][0:1, :], scalar=UNSCALE, in1=ob[:], op0=ALU.mult,
                                     op1=ALU.add).then_inc(out_ready, 1)


def dit_phase(nc, const, a, store, mod, gates_dram, row_dram, x_in, out):
    H, DH = DIT_H, DIT_DH
    FT = MLP // P
    C = INNER // D
    with ExitStack() as ctx:
        m = Mem(nc, ctx, "dit_")
        X = m.sb("X", [P, TT, D])
        yh, yl = m.sb("yh", [P, KD, T], F16), m.sb("yl", [P, KD, T], F16)
        big = m.sb("big", [P, TT, INNER])
        O = big
        A = big[:, :, 0:D]
        xn = big[:, :, D:2 * D]
        y32 = big[:, :, 2 * D:3 * D]
        V = m.sb("V", [P, 2, TT, INNER], F16)
        hid = V[:].rearrange("p e t n -> p e (t n)").rearrange("p e (f t) -> p e f t", f=FT)
        qk = m.sb("qk", [P, 2, 2, 2, T], F16)
        oT = [[yh[:].rearrange("p k t -> p (k t)").rearrange("p (h q) -> p h q", h=H),
               yl[:].rearrange("p k t -> p (k t)").rearrange("p (h q) -> p h q", h=H)],
              [qk[:, 0].rearrange("p a e t -> p (a e t)").rearrange("p (h q) -> p h q", h=H),
               qk[:, 1].rearrange("p a e t -> p (a e t)").rearrange("p (h q) -> p h q", h=H)]]
        region = [m.sb(f"weights{i}", [P, 2, KD * INNER], F16) for i in range(2)]
        cut = lambda r, k: r[:].rearrange("p e (k n) -> p e k n", k=k)
        w_v, w_1 = cut(region[0], KD), cut(region[0], KD)
        w_out, w_2 = cut(region[1], H), cut(region[1], FT)
        w_qk = m.sb("w_qk", [P, 2, 2, 2, KD, DH], F16)
        gates = m.sb("gates", [P, 2, D])
        rows = m.sb("bias_rows", [P, 2, D])
        gb = m.sb("gated_bias", [P, 2, D])
        qk_b = m.sb("qk_b", [P, 3 * H])
        b_1 = m.sb("b_1", [P, FT])
        stats = m.sb("stats", [P, TT, 6])
        mv = m.sb("mv", [P, TT, 2])
        rstd = m.sb("rstd", [P, TT])
        bank = [m.ps(f"bank{i}", [P, D]) for i in range(8)]
        work = bank[4:8]

        wv_loaded, w1_loaded, wo_loaded, w2_loaded = (m.sem(s) for s in "wv_loaded w1_loaded wo_loaded w2_loaded".split())
        wqk_loaded = [m.sem(f"wqk_loaded_{i}") for i in range(2)]
        (stats_taken, params_loaded, x_loaded, gates_loaded, b_scaled, gated, a_begun, stats_ready, mv_ready, var_ready,
         root_done, rstd_ready, xn_ready, rows_turned, y_ready, yh_ready, yl_ready, v_sum, vh_ready, vl_ready,
         qk_sum, qk_hi, qk_lo, o_turned, oh_ready, ol_ready, att_sum, att_gated, a_ready, x_again, hid_sum, hid_ready,
         hh_ready, hl_ready, mlp_sum, mlp_gated, out_ready, stored) = (m.sem(s) for s in (
             "stats_taken params_loaded x_loaded gates_loaded b_scaled gated a_begun stats_ready mv_ready var_ready root_done "
             "rstd_ready xn_ready rows_turned y_ready yh_ready yl_ready v_sum vh_ready vl_ready qk_sum qk_hi qk_lo "
             "o_turned oh_ready ol_ready att_sum att_gated a_ready x_again hid_sum hid_ready hh_ready hl_ready "
             "mlp_sum mlp_gated out_ready stored").split())

        def scores(pe, s, h, t):
            for (qe, ke) in ((0, 0), (0, 1), (1, 0)):
                mm = pe.matmul(s, qk[:, hs.parity, 0, qe, t * P:(t + 1) * P], qk[:, hs.parity, 1, ke, :],
                               start=(qe + ke == 0), stop=(qe == 1))
            return mm

        hs = Heads(
            m, S=[bank[0][:], bank[1][:]], PT=[bank[2][:], bank[3][:]], O=[bank[4][:, 0:DH], bank[5][:, 0:DH]],
            ident=const["ident"][:], scores=scores,
            values=lambda h, s: (V[:, 0, s, at(h * DH, DH)], V[:, 1, s, at(h * DH, DH)]),
            out=lambda h, t: O[:, t, at(h * DH, DH)],
            scale=UNSCALE * UNSCALE * float(DH) ** -0.5)
        gelu = hs.prob

        x_rows = x_in.rearrange("b (t p) d -> p b t d", p=P)
        o_rows = out.rearrange("b (t p) d -> p b t d", p=P)
        flat_head = lambda v: v.rearrange("p o a e k n -> p (o a) e k n")
        block = ctx.enter_context(nc.Block())

        @block.sync
        def _(sp):
            sp.dma_start(qk_b[:], a["qkv_b_columns"]).then_inc(params_loaded, 16)
            sp.dma_start(b_1[:], a["ffn_b1_columns"]).then_inc(params_loaded, 16)
            sp.dma_start(rows[:, 0, :], row_dram.broadcast_to([P, D])).then_inc(params_loaded, 16)
            sp.dma_start(rows[:, 1, :], a["L3_cond_ffn_b2"].rearrange("(o d) -> o d", o=1).broadcast_to([P, D]))\
              .then_inc(params_loaded, 16)
            sp.dma_start(w_v, store.v).then_inc(wv_loaded, 16)
            with sp.Fori(0, B) as b:
                def load_qk(h, parity):
                    sp.dma_start(w_qk[:, parity], flat_head(store.qk[:, at(h)])).then_inc(wqk_loaded[parity], 16)

                sp.wait_ge(stored, b * (16 * TT))
                sp.dma_start(X[:], x_rows[:, at(b), :, :].rearrange("p o t d -> p (o t) d")).then_inc(x_loaded, 16)
                sp.dma_start(gates[:], gates_dram[at(b), :, :].broadcast_to([P, 2, D])).then_inc(gates_loaded, 16)
                sp.wait_ge(qk_sum, b * (2 * H))
                load_qk(0, 0)
                load_qk(1, 1)
                sp.wait_ge(mlp_sum, b * TT)
                sp.dma_start(w_out, store.out).then_inc(wo_loaded, 16)
                sp.wait_ge(v_sum, (b + 1) * (TT * C))
                sp.dma_start(w_1, store.w1).then_inc(w1_loaded, 16)
                with sp.Fori(0, (H - 2) // 2) as pair:
                    for parity in range(2):
                        sp.wait_ge(qk_sum, b * (2 * H) + pair * 4 + (parity * 2 + 2))
                        load_qk(pair * 2 + (2 + parity), parity)
                sp.wait_ge(att_sum, (b + 1) * TT)
                sp.dma_start(w_2, store.w2).then_inc(w2_loaded, 16)
                sp.wait_ge(hid_sum, (b + 1) * FT)
                sp.dma_start(w_v, store.v).then_inc(wv_loaded, 16)
                for t in range(TT):
                    sp.wait_ge(out_ready, b * TT + t + 1)
                    sp.dma_start(o_rows[:, at(b), t, :], X[:, t, :]).then_inc(stored, 16)
            sp.wait_ge(wv_loaded, (B + 1) * 16)
            sp.wait_ge(stored, B * TT * 16)

        @block.gpsimd
        def _(pool):
            hs.credits(pool)
            pool.sem_inc(att_gated, 2)
            pool.sem_inc(mlp_gated, 2)
            pool.sem_inc(hl_ready, 2)
            pool.sem_inc(vl_ready, C)
            pool.wait_ge(params_loaded, 64)
            with pool.Fori(0, B) as b:
                pool.wait_ge(gates_loaded, (b + 1) * 16)
                pool.tensor_tensor(gb[:], gates[:], rows[:], ALU.mult).then_inc(gated, 1)
                pool.wait_ge(gated, b + 1)
                for t in range(TT):
                    pool.wait_ge(att_gated, b * TT + t + 3)
                    pool.tensor_tensor(A[:, t, :], A[:, t, :], gb[:, 0, :], ALU.add).then_inc(a_begun, 1)
                    pool.wait_ge(a_begun, b * TT + t + 1)
                    pool.tensor_tensor(A[:, t, :], A[:, t, :], X[:, t, :], ALU.add).then_inc(a_ready, 1)
                for t in range(TT):
                    pool.wait_ge(a_ready, b * TT + t + 1)
                    pool.tensor_tensor(X[:, t, :], A[:, t, :], X[:, t, :], ALU.add).then_inc(x_again, 1)
                    pool.wait_ge(x_again, (b * TT + t) * 2 + 1)
                    pool.tensor_tensor(X[:, t, :], X[:, t, :], gb[:, 1, :], ALU.add).then_inc(x_again, 1)

        @block.tensor
        def _(pe):
            pe.wait_ge(b_scaled, 1)
            with pe.Fori(0, B) as b:
                def turn_rows(n):
                    pe.wait_ge(xn_ready, n * TT + TT)
                    for k in range(KD):
                        for t in range(TT):
                            mm = pe.transpose(bank[k][:, t * P:(t + 1) * P], xn[:, t, k * P:(k + 1) * P],
                                              const["ident"][:])
                        mm.then_inc(rows_turned, 1)

                pe.wait_ge(wv_loaded, (b + 1) * 16)
                turn_rows(b * 2)
                with pe.Fori(0, TT) as t:
                    pe.wait_ge(yl_ready, b * (2 * KD) + KD)
                    for c in range(C):
                        pe.wait_ge(vl_ready, b * (TT * C) + t * C + (c + 1))
                        for k in range(KD):
                            w = lambda e: w_v[:, e, k, c * D:(c + 1) * D]
                            mm = products(pe, work[c][:], (yh[:, k, at(t * P, P)], yl[:, k, at(t * P, P)]),
                                          (w(0), w(1)), k == 0, k == KD - 1)
                        mm.then_inc(v_sum, 1)
                pe.wait_ge(vl_ready, (b + 1) * (TT * C) + C)

                def project(h, i, parity, nth):
                    if i == 0:
                        pe.wait_ge(wqk_loaded[parity], b * (16 * (H // 2)) + nth * 16)
                    for k in range(KD):
                        w = lambda e: w_qk[:, parity, i, e, k, :]
                        mm = products(pe, work[2 + i][:], (w(0), w(1)), (yh[:, k, :], yl[:, k, :]), k == 0,
                                      k == KD - 1)
                    mm.then_inc(qk_sum, 1)

                project(0, 0, 0, 1)
                project(0, 1, 0, 1)

                def current(h, t, u):
                    if t == 0:
                        pe.wait_ge(qk_lo, b * (2 * H) + h * 2 + 2)
                    hs.pe_scores(pe, h, t, u)

                def beside(h, t, last):
                    if t in (1, 2) and not last:
                        project(h + 1, t - 1, 1 - hs.parity, hs.nth)

                hs.run(pe, H, b * (H * TT), current, lambda h, t, u: hs.pe_turn(pe, t, u),
                       lambda h, t, u: hs.pe_values(pe, h, t, u), beside)

                def project_out(t):
                    pe.wait_ge(ol_ready, b * (4 * TT) + 4 * t + 4)
                    pe.wait_ge(att_gated, b * TT + t + 1)
                    for h in range(H):
                        mm = products(pe, work[t % 2][:], (oT[t % 2][0][:, h, :], oT[t % 2][1][:, h, :]),
                                      (w_out[:, 0, h, :], w_out[:, 1, h, :]), h == 0, h == H - 1)
                    mm.then_inc(att_sum, 1)

                pe.wait_ge(hs.out_copied, (b + 1) * (H * TT) + hs.CREDIT)
                pe.wait_ge(wo_loaded, (b + 1) * 16)
                for t in range(TT):
                    for q in range(4):
                        if t >= 1:
                            pe.wait_ge(ol_ready, b * (4 * TT) + 4 * (t - 1) + q + 1)
                        for h in range(4):
                            mm = pe.transpose(bank[q][:, h * P:(h + 1) * P],
                                              O[:, t, (4 * q + h) * P:(4 * q + h + 1) * P], const["ident"][:])
                        mm.then_inc(o_turned, 1)
                    if t >= 1:
                        project_out(t - 1)
                project_out(TT - 1)
                pe.wait_ge(w1_loaded, (b + 1) * 16)
                turn_rows(b * 2 + 1)
                with pe.Fori(0, FT // 4) as g:
                    pe.wait_ge(yl_ready, (b + 1) * (2 * KD))
                    for j in range(4):
                        pe.wait_ge(hid_ready, b * FT + g * 4 + (j + 1))
                        for k in range(KD):
                            w = lambda e: w_1[:, e, k, at(g * (4 * P) + j * P, P)]
                            mm = products(pe, work[j][:], (w(0), w(1)), (yh[:, k, :], yl[:, k, :]), k == 0,
                                          k == KD - 1)
                        mm.then_inc(hid_sum, 1)
                with pe.Fori(0, TT // 2) as g:
                    pe.wait_ge(hl_ready, (b + 1) * FT + 2)
                    pe.wait_ge(w2_loaded, (b + 1) * 16)
                    for j in range(2):
                        pe.wait_ge(mlp_gated, b * TT + g * 2 + (j + 1))
                        for f in range(FT):
                            left = lambda e: hid[:, e, f, at(g * (2 * P) + j * P, P)]
                            mm = products(pe, work[j][:], (left(0), left(1)), (w_2[:, 0, f, :], w_2[:, 1, f, :]),
                                          f == 0, f == FT - 1)
                        mm.then_inc(mlp_sum, 1)

        @block.scalar
        def _(act):
            act.wait_ge(b_scaled, 1)
            act.sem_inc(hid_ready, 4)
            with act.Fori(0, B) as b:
                def parts_of_rows(n):
                    act.wait_ge(var_ready, n + 1)
                    act.activation(rstd[:], mv[:, :, 1], ACT.Sqrt).then_inc(root_done, 1)
                    for k in range(KD):
                        act.wait_ge(y_ready, n * KD + k + 1)
                        act.activation(yh[:, k, :], y32[:, k, :], ACT.Copy).then_inc(yh_ready, 1)

                parts_of_rows(b * 2)
                with act.Fori(0, TT) as t:
                    for c in range(C):
                        act.wait_ge(v_sum, b * (TT * C) + t * C + (c + 1))
                        act.activation(V[:, 0, at(t), c * D:(c + 1) * D].rearrange("p o n -> p (o n)"), work[c][:],
                                       ACT.Copy).then_inc(vh_ready, 1)
                act.preload_act_table(ACT.Exp)

                def take(h, i, parity):
                    act.wait_ge(qk_sum, b * (2 * H) + h * 2 + (i + 1))
                    act.activation(qk[:, parity, i, 0, :], work[2 + i][:], ACT.Identity,
                                   bias=qk_b[:, at(h + i * H)]).then_inc(qk_hi, 1)

                take(0, 0, 0)
                take(0, 1, 0)

                def beside(h, t, last):
                    if t in (2, 3) and not last:
                        take(h + 1, t - 2, 1 - hs.parity)

                hs.run(act, H, b * (H * TT), lambda h, t, u: hs.act_exp(act, t, u),
                       lambda h, t, u: hs.act_copy(act, t, u), lambda h, t, u: None, beside)
                for t in range(TT):
                    for q in range(4):
                        act.wait_ge(o_turned, b * (4 * TT) + 4 * t + q + 1)
                        if t >= 2:
                            act.wait_ge(att_sum, b * TT + t - 1)
                        act.activation(oT[t % 2][0][:, 4 * q:4 * q + 4, :].rearrange("p h q -> p (h q)"),
                                       bank[q][:], ACT.Copy, scale=XS * UNSCALE).then_inc(oh_ready, 1)
                parts_of_rows(b * 2 + 1)
                act.preload_act_table(ACT.Gelu)
                with act.Fori(0, FT // 4) as g:
                    for j in range(4):
                        n = b * FT + g * 4 + j
                        act.wait_ge(hid_sum, n + 1)
                        act.wait_ge(hl_ready, n + 1)
                        act.activation(gelu[:, j % 2, :], work[j][:], ACT.Gelu, bias=b_1[:, at(g * 4 + j)],
                                       scale=UNSCALE).then_inc(hid_ready, 1)
                        act.wait_ge(hid_ready, n + 5)
                        act.activation(flat(hid[:, 0, at(g * 4 + j), :]), gelu[:, j % 2, :], ACT.Copy, scale=XS)\
                           .then_inc(hh_ready, 1)

        @block.vector
        def _(dve):
            dve.wait_ge(params_loaded, 64)
            dve.tensor_scalar(qk_b[:], qk_b[:], XS * WS, None, ALU.mult).then_inc(b_scaled, 1)
            dve.wait_ge(b_scaled, 1)
            with dve.Fori(0, B) as b:
                def norm(n, src, ready, scale, shift):
                    for t in range(TT):
                        ready(t)
                        dve.bn_stats(stats[:, t, :], src[:, t, :]).then_inc(stats_ready, 1)
                    dve.wait_ge(stats_ready, (n + 1) * TT)
                    dve.sem_inc(stats_taken, 1)
                    for t in range(TT):
                        dve.bn_aggr(mv[:, t, :], stats[:, t, :]).then_inc(mv_ready, 1)
                    dve.wait_ge(mv_ready, (n + 1) * TT)
                    dve.tensor_scalar(mv[:, :, 1], mv[:, :, 1], DIT_EPS, None, ALU.add).then_inc(var_ready, 1)
                    dve.wait_ge(root_done, n + 1)
                    dve.reciprocal(rstd[:], rstd[:]).then_inc(rstd_ready, 1)
                    dve.wait_ge(rstd_ready, n + 1)
                    for t in range(TT):
                        dve.tensor_scalar(xn[:, t, :], src[:, t, :], mv[:, t, 0:1], rstd[:, t:t + 1], ALU.subtract,
                                          ALU.mult).then_inc(xn_ready, 1)
                    for k in range(KD):
                        dve.wait_ge(rows_turned, n * KD + k + 1)
                        dve.tensor_scalar(y32[:, k, :], bank[k][:], mod[:, scale, k, at(b)], mod[:, shift, k, at(b)],
                                          ALU.mult, ALU.add).then_inc(y_ready, 1)
                    for k in range(KD):
                        dve.wait_ge(yh_ready, n * KD + k + 1)
                        dve.tensor_tensor(yl[:, k, :], y32[:, k, :], yh[:, k, :], ALU.subtract).then_inc(yl_ready, 1)

                norm(b * 2, X, lambda t: dve.wait_ge(x_loaded, (b + 1) * 16) if t == 0 else None, SCALE1, SHIFT1)
                with dve.Fori(0, TT) as t:
                    for c in range(C):
                        dve.wait_ge(vh_ready, b * (TT * C) + t * C + (c + 1))
                        cols = slice(c * D, (c + 1) * D)
                        dve.tensor_tensor(flat(V[:, 1, at(t), cols]), work[c][:], flat(V[:, 0, at(t), cols]),
                                          ALU.subtract).then_inc(vl_ready, 1)

                def take(h, i, parity):
                    dve.wait_ge(qk_hi, b * (2 * H) + h * 2 + (i + 1))
                    dve.scalar_tensor_tensor(out=qk[:, parity, i, 1, :], in0=work[2 + i][:],
                                             scalar=qk_b[:, at(h + i * H)], in1=qk[:, parity, i, 0, :],
                                             op0=ALU.add, op1=ALU.subtract).then_inc(qk_lo, 1)

                take(0, 0, 0)
                take(0, 1, 0)

                def beside(h, t, last):
                    if t in (2, 3) and not last:
                        take(h + 1, t - 2, 1 - hs.parity)

                hs.run(dve, H, b * (H * TT), lambda h, t, u: hs.dve_max(dve, t, u),
                       lambda h, t, u: hs.dve_copy(dve, t, u), lambda h, t, u: hs.dve_out(dve, h, t, u), beside)

                def gate_attention(t):
                    dve.wait_ge(att_sum, b * TT + t + 1)
                    dve.wait_ge(gates_loaded, (b + 1) * 16)
                    dve.scalar_tensor_tensor(out=A[:, t, :], in0=work[t % 2][:], scalar=UNSCALE, in1=gates[:, 0, :],
                                             op0=ALU.mult, op1=ALU.mult).then_inc(att_gated, 1)

                for t in range(TT):
                    for q in range(4):
                        dve.wait_ge(oh_ready, b * (4 * TT) + 4 * t + q + 1)
                        part = lambda e: oT[t % 2][e][:, 4 * q:4 * q + 4, :].rearrange("p h q -> p (h q)")
                        dve.scalar_tensor_tensor(out=part(1), in0=bank[q][:], scalar=XS * UNSCALE, in1=part(0),
                                                 op0=ALU.mult, op1=ALU.subtract).then_inc(ol_ready, 1)
                    if t >= 1:
                        gate_attention(t - 1)
                gate_attention(TT - 1)
                norm(b * 2 + 1, A, lambda t: dve.wait_ge(a_ready, b * TT + t + 1), SCALE2, SHIFT2)
                with dve.Fori(0, FT // 4) as g:
                    for j in range(4):
                        n = b * FT + g * 4 + j
                        dve.wait_ge(hh_ready, n + 1)
                        dve.scalar_tensor_tensor(out=flat(hid[:, 1, at(g * 4 + j), :]), in0=gelu[:, j % 2, :],
                                                 scalar=XS, in1=flat(hid[:, 0, at(g * 4 + j), :]), op0=ALU.mult,
                                                 op1=ALU.subtract).then_inc(hl_ready, 1)
                for t in range(TT):
                    dve.wait_ge(mlp_sum, b * TT + t + 1)
                    if t >= 2:
                        dve.wait_ge(out_ready, b * TT + t - 1)
                    dve.scalar_tensor_tensor(out=gelu[:, t % 2, :], in0=work[t % 2][:], scalar=UNSCALE,
                                             in1=gates[:, 1, :], op0=ALU.mult, op1=ALU.mult).then_inc(mlp_gated, 1)
                    dve.wait_ge(mlp_gated, b * TT + t + 3)
                    dve.wait_ge(x_again, (b * TT + t) * 2 + 2)
                    dve.tensor_tensor(X[:, t, :], X[:, t, :], gelu[:, t % 2, :], ALU.add).then_inc(out_ready, 1)


def program(nc, a, out):
    rows = lambda w: w.rearrange("(k p) n -> p k n", p=P)
    x_gru = out if LAST_PHASE == 3 else nc.dram_tensor("x_gru", (B, T, D), F32, kind="Internal").ap()
    store = WeightStore(nc, a) if LAST_PHASE >= 4 else None
    gates_dram = nc.dram_tensor("gates", (B, 2, D), F32, kind="Internal").ap()
    row_dram = nc.dram_tensor("out_bias_row", (1, D), F32, kind="Internal").ap()

    def parts(ctx, name, k, n):
        return [Mem(nc, ctx).sb(f"{name}_{e}", [P, k, n], F16) for e in ("hi", "lo")]

    with ExitStack() as ctx:
        m = Mem(nc, ctx)
        const = {
            "ones16": m.sb("ones16", [P, P], F16),
            "ones32": m.sb("ones32", [P, P]),
            "below": m.sb("below", [P, P]),
            "ident": m.sb("ident", [P, P]),
            "ident16": m.sb("ident16", [P, P], F16),
        }
        made = m.sem("const_made")
        with nc.Block() as block:
            @block.gpsimd
            def _(pool):
                pool.memset(const["ones16"][:], 1.0).then_inc(made, 1)
                pool.memset(const["ones32"][:], 1.0).then_inc(made, 1)
                pool.wait_ge(made, 2)
                pool.affine_select(out=const["below"][:], in_=const["ones32"][:], compare_op=ALU.is_gt, fill=0.0,
                                   base=0, pattern=[[1, P]], channel_multiplier=-1)
                pool.affine_select(out=const["ident"][:], in_=const["ones32"][:], compare_op=ALU.is_equal, fill=0.0,
                                   base=0, pattern=[[1, P]], channel_multiplier=-1)
                pool.affine_select(out=const["ident16"][:], in_=const["ones16"][:], compare_op=ALU.is_equal,
                                   fill=0.0, base=0, pattern=[[1, P]], channel_multiplier=-1)

        with ExitStack() as inner:
            X = Mem(nc, inner).sb("X", [P, NT, D])
            topk_phase(nc, X, const, a["x"], a["side_columns"], a["cond_2048"])
            if LAST_PHASE >= 2:
                with ExitStack() as weights:
                    w_qkv, w_out = parts(weights, "small_qkv", KD, 3 * D), parts(weights, "small_out", KD, D)
                    split_weights(nc, "small_", [(rows(a["L1_cond_W_qkv"]), w_qkv[0][:], w_qkv[1][:], WS),
                                                 (rows(a["L1_cond_W_out"]), w_out[0][:], w_out[1][:], WS)])
                    small_attention_phase(nc, X, const, a, w_qkv, w_out)
            if LAST_PHASE >= 3:
                with ExitStack() as weights:
                    gi = Mem(nc, weights).sb("gi", [P, 2, 3 * KD, B, T], F16)
                    w_hh = parts(weights, "w_hh", KD, 3 * D)
                    with ExitStack() as deeper:
                        w_ih = parts(deeper, "w_ih", KD, 3 * D)
                        split_weights(nc, "gru_", [(rows(a["L2_cond_W_ih"]), w_ih[0][:], w_ih[1][:], WS),
                                                   (rows(a["L2_cond_W_hh"]), w_hh[0][:], w_hh[1][:], RS)])
                        gate_input_phase(nc, X, const, a, w_ih, gi)
                    gru_phase(nc, X, const, a, w_hh, gi, x_gru, store)
            if LAST_PHASE <= 2:
                stored = m.sem("stored")
                with nc.Block() as block:
                    @block.sync
                    def _(sp):
                        sp.dma_start(out.rearrange("b (t p) d -> p (b t) d", p=P), X[:]).then_inc(stored, 16)
                        sp.wait_ge(stored, 16)

        if LAST_PHASE >= 4:
            mod = m.sb("dit_mod", [P, 4, KD, B])
            dit_condition_phase(nc, a, store, mod, gates_dram, row_dram)
            dit_phase(nc, const, a, store, mod, gates_dram, row_dram, x_gru, out)


def kernel(**inputs):
    import numpy as np
    import concourse.bacc as bacc
    from concourse.bass_utils import run_bass_kernel_spmd

    nc = bacc.Bacc("TRN2", target_bir_lowering=False, num_devices=1)
    given = {k: np.asarray(v) for k, v in inputs.items()}
    given["side_columns"] = given["fside_BxSx1_0"].reshape(NT, P).T
    columns = lambda v: v.reshape(-1, P).T
    given["cond_columns"] = given["cond_2048"].reshape(B, KD, P).transpose(2, 1, 0)
    given["b_emb_columns"] = columns(given["L1_cond_b_emb"])
    given["b_ih_columns"] = columns(given["L2_cond_b_ih"])
    given["b_hh_columns"] = columns(given["L2_cond_b_hh"])
    given["ada_b_columns"] = columns(given["L3_cond_ada_b"])
    given["qkv_b_columns"] = columns(given["L3_cond_qkv_b"])
    given["ffn_b1_columns"] = columns(given["L3_cond_ffn_b1"])
    given["g_norm_columns"] = columns(given["L1_cond_g_norm"])
    arrays = {f"in_{k}": np.ascontiguousarray(v) for k, v in given.items()}
    args = {k: nc.dram_tensor(f"in_{k}", arrays[f"in_{k}"].shape, mybir.dt.from_np(arrays[f"in_{k}"].dtype),
                              kind="ExternalInput").ap() for k in given}
    out = nc.dram_tensor("out", (B, T, D), F32, kind="ExternalOutput").ap()
    program(nc, args, out)
    r = run_bass_kernel_spmd(nc, [arrays], core_ids=[0])
    return r.results[0]["out"]
```

```python
from contextlib import ExitStack

import concourse.bass as bass
from concourse import mybir

F32 = mybir.dt.float32
F16 = mybir.dt.float16
I32 = mybir.dt.int32
I16 = mybir.dt.int16
U16 = mybir.dt.uint16
ALU = mybir.AluOpType
ACT = mybir.ActivationFunctionType
AX = mybir.AxisListType

P = 128
B, T, D = 4, 512, 512
TT = T // P
NT = B * TT
KD = D // P
TOPK = 5120

DIT_H, DIT_DH = 16, 128
INNER = DIT_H * DIT_DH
MLP = 4 * D
DIT_EPS = 1e-6
SCALE1, SHIFT1, SCALE2, SHIFT2 = range(4)


class Mem:

    def __init__(self, nc, ctx, phase=""):
        self.nc, self.ctx, self.phase = nc, ctx, phase
        self.sems = []

    def sb(self, name, shape, dt=F32):
        return self.ctx.enter_context(self.nc.sbuf_tensor(self.phase + name, shape, dt))

    def ps(self, name, shape, dt=F32):
        return self.ctx.enter_context(self.nc.psum_tensor(self.phase + name, shape, dt))

    def sem(self, name):
        if not self.sems:
            self.ctx.callback(self.clear)
        self.sems.append(self.nc.alloc_semaphore(name=self.phase + name))
        return self.sems[-1]

    def clear(self):
        self.nc.clear_and_free_semaphores(self.sems)
        self.nc.all_engine_barrier()


def at(i, n=1):
    return bass.ds(i, n)


class SplitBeside:

    SLOTS, WIDE = 2, 1536

    def __init__(self, m, jobs):
        self.pieces = []
        for src, hi, lo, scale in jobs:
            for a in range(src.shape[1]):
                for c in range(0, src.shape[2], self.WIDE):
                    e = min(c + self.WIDE, src.shape[2])
                    self.pieces.append((src[:, a, c:e], hi[:, a, c:e], lo[:, a, c:e], scale))
        self.stage = m.sb("split_stage", [P, self.SLOTS, self.WIDE])
        self.loaded = [m.sem(f"split_loaded_{s}") for s in range(self.SLOTS)]
        self.scaled, self.lo_done = m.sem("split_scaled"), m.sem("split_lo_done")

    def slot(self, j):
        return self.stage[:, j % self.SLOTS, 0:self.pieces[j][1].shape[1]]

    def sync(self, sp):
        for j, (src, _, _, _) in enumerate(self.pieces):
            if j >= self.SLOTS:
                sp.wait_ge(self.lo_done, j - self.SLOTS + 1)
            sp.dma_start(self.slot(j), src).then_inc(self.loaded[j % self.SLOTS], 16)

    def scalar(self, act):
        for j, (_, hi, _, scale) in enumerate(self.pieces):
            act.wait_ge(self.loaded[j % self.SLOTS], 16 * (j // self.SLOTS + 1))
            act.activation(hi, self.slot(j), ACT.Copy, scale=scale)
            act.activation(self.slot(j), self.slot(j), ACT.Copy, scale=scale).then_inc(self.scaled, 1)

    def pool(self, pool):
        for j, (_, hi, lo, _) in enumerate(self.pieces):
            pool.wait_ge(self.scaled, j + 1)
            pool.tensor_tensor(lo, self.slot(j), hi, ALU.subtract).then_inc(self.lo_done, 1)


def topk_phase(nc, X, const, x_in, side, cond, jobs):
    E = T * D // P
    with ExitStack() as ctx:
        m = Mem(nc, ctx, "edge_")
        adj = m.sb("adj", [P, NT, D])
        key = m.sb("key", [P, NT, D], I32)
        hi = m.sb("key_hi", [P, B, E], I16)
        lo = m.sb("key_lo", [P, B, E], U16)
        mask = m.sb("mask", [P, B, E], F16)
        embt = m.sb("embt", [P, B, D])
        rank = m.sb("rank", [P, 2, D])
        zeros = m.sb("zeros", [P, D])
        fs = m.sb("fs", [P, NT])
        nmax = m.sb("nmax", [P, NT])
        rsum = m.sb("rsum", [P, NT])
        rinv = m.sb("rinv", [P, NT])
        rscale = m.sb("rscale", [P, NT])
        digit = m.sb("digit", [P, 17])
        found = m.sb("found", [P, 2, B])
        cand = m.sb("cand", [P, B])
        want = m.sb("want", [P, B])
        ge = m.sb("ge", [P, B])
        part16 = m.sb("part16", [P, B], F16)
        halves = m.sb("halves", [P, 2, B], I32)
        tkey = m.sb("tkey", [P, B], I32)
        tsign = m.sb("tsign", [P, B], I32)
        thr = m.sb("thr", [P, B], I32)
        ties = m.sb("ties", [P, NT])
        before = m.sb("before", [P, NT])
        low = m.sb("low", [P, B])
        pair_of = [slice(0, 2), slice(2, 4)]
        part = [m.ps(f"part{g}", [P, 2]) for g in range(2)]
        total = [m.ps(f"total{g}", [P, 2]) for g in range(2)]
        pref = m.ps("pref", [P, B, TT])

        x_loaded = m.sem("x_loaded")
        side_loaded = m.sem("side_loaded")
        max_ready = m.sem("max_ready")
        exp_done = m.sem("exp_done")
        adj_done = m.sem("adj_done")
        diag_done = m.sem("diag_done")
        mask_ready = [m.sem(f"mask_ready_{g}") for g in range(2)]
        part_ready = [m.sem(f"part_ready_{g}") for g in range(2)]
        part_copied = [m.sem(f"part_copied_{g}") for g in range(2)]
        total_ready = [m.sem(f"total_ready_{g}") for g in range(2)]
        low_ready = [m.sem(f"low_ready_{g}") for g in range(2)]
        ge_ready = [m.sem(f"ge_ready_{g}") for g in range(2)]
        cand_ready = [m.sem(f"cand_ready_{g}") for g in range(2)]
        ties_counted = m.sem("ties_counted")
        pref_ready = m.sem("pref_ready")
        dv = m.sem("topk_dve")
        split = SplitBeside(m, jobs)

        block = ctx.enter_context(nc.Block())

        @block.sync
        def _(sp):
            sp.dma_start(X[:], x_in.rearrange("b (t p) d -> p (b t) d", p=P)).then_inc(x_loaded, 16)
            sp.dma_start(fs[:], side).then_inc(side_loaded, 16)
            sp.dma_start(embt[:], cond.rearrange("(o b) d -> o b d", o=1).broadcast_to([P, B, D])).then_inc(side_loaded, 16)
            split.sync(sp)

        @block.scalar
        def _(act):
            act.preload_act_table(ACT.Exp)
            act.wait_ge(max_ready, 1)
            with act.Fori(0, NT) as n:
                act.activation(adj[:, at(n), :], X[:, at(n), :], ACT.Exp, bias=nmax[:, at(n)],
                               accum_out=rsum[:, at(n)]).then_inc(exp_done, 1)
            split.scalar(act)

        @block.gpsimd
        def _(pool):
            pool.wait_ge(adj_done, NT)
            for t in range(TT):
                v = adj[:].rearrange("p (b t) d -> p b t d", t=TT)[:, :, t, t * P:(t + 1) * P]
                pool.affine_select(out=v, in_=v, compare_op=ALU.not_equal, fill=-3.0e38, base=0,
                                   pattern=[[0, B], [-1, P]], channel_multiplier=1).then_inc(diag_done, 1)
            split.pool(pool)

        BITS = 16

        @block.tensor
        def _(pe):
            def counts(g, j, i):
                pe.wait_ge(mask_ready[g], i * 2 + (j + 1))
                for c in range(E // P):
                    mm = pe.matmul(part[g][:, j:j + 1], mask[:, g * 2 + j, c * P:(c + 1) * P], const["ones16"][:, 0:1],
                                   start=(c == 0), stop=(c == E // P - 1))
                if j == 1:
                    mm.then_inc(part_ready[g], 1)

            def sum_up(g, i):
                pe.wait_ge(part_copied[g], i + 1)
                pe.matmul(total[g][:], const["ones16"][:], part16[:, pair_of[g]], start=True, stop=True)\
                  .then_inc(total_ready[g], 1)

            for half in range(2):
                base = half * (BITS + 1)

                def search_pass(i, first):
                    counts(0, 0, i)
                    if not first:
                        sum_up(1, i - 1)
                    counts(0, 1, i)
                    counts(1, 0, i)
                    sum_up(0, i)
                    counts(1, 1, i)

                search_pass(base, True)
                with pe.Fori(0, (BITS - 1) // 3) as three:
                    for more in range(3):
                        search_pass(three * 3 + (base + 1 + more), False)
                sum_up(1, base + BITS - 1)
                for g in range(2):
                    for j in range(2):
                        counts(g, j, base + BITS)
                for g in range(2):
                    sum_up(g, base + BITS)
            pe.wait_ge(ties_counted, NT)
            tv = ties[:].rearrange("p (b t) -> p b t", t=TT)
            pe.matmul(pref[:], const["below"][:], tv, start=True, stop=False)
            for s in range(1, TT):
                mm = pe.matmul(pref[:, :, s:TT], const["ones32"][:], tv[:, :, 0:TT - s], start=False, stop=(s == TT - 1))
            mm.then_inc(pref_ready, 1)

        @block.vector
        def _(dve):
            n_dv = [0]

            def step(ins):
                ins.then_inc(dv, 1)
                n_dv[0] += 1
                dve.wait_ge(dv, n_dv[0])

            for k in range(17):
                dve.memset(digit[:, k:k + 1], float(1 << (15 - k)) if k < 16 else 0.0)
            dve.memset(want[:], float(TOPK))
            dve.memset(cand[:], 0.0)
            dve.memset(zeros[:], 0.0)
            dve.wait_ge(x_loaded, 16)
            dve.tensor_reduce(nmax[:], X[:], AX.X, ALU.max, negate=True).then_inc(max_ready, 1)
            dve.wait_ge(exp_done, NT)
            step(dve.reciprocal(rinv[:], rsum[:]))
            dve.wait_ge(side_loaded, 32)
            step(dve.scalar_tensor_tensor(out=rscale[:], in0=rinv[:], scalar=float(D) ** -0.5, in1=fs[:],
                                          op0=ALU.mult, op1=ALU.mult))
            with dve.Fori(0, B) as b:
                for t in range(TT):
                    a = adj[:, at(b * TT + t), :].rearrange("p o d -> p (o d)")
                    dve.scalar_tensor_tensor(out=a, in0=a, scalar=rscale[:, at(b * TT + t)],
                                             in1=embt[:, at(b), :].rearrange("p o d -> p (o d)"),
                                             op0=ALU.mult, op1=ALU.mult).then_inc(adj_done, 1)
            dve.wait_ge(diag_done, TT)
            bits = adj[:].bitcast(I32)
            step(dve.tensor_scalar(key[:], bits, 31, 0x7FFFFFFF, ALU.arith_shift_right, ALU.bitwise_and))
            step(dve.tensor_tensor(key[:], key[:], bits, ALU.bitwise_xor))
            k16 = key[:].rearrange("p n d -> p (n d)").bitcast(I16).rearrange("p (e two) -> p e two", two=2)
            dve.tensor_copy(hi[:].rearrange("p b e -> p (b e)"), k16[:, :, 1])
            step(dve.tensor_copy(lo[:].rearrange("p b e -> p (b e)"), k16[:, :, 0].bitcast(U16)))

            for half, src in enumerate((hi, lo)):
                base, decided = half * (BITS + 1), half * BITS

                def let_in(g, j):
                    b = g * 2 + j
                    dve.tensor_scalar(mask[:, b, :], src[:, b, :], cand[:, b:b + 1], None, ALU.is_ge)\
                       .then_inc(mask_ready[g], 1)

                def copy_part(g, k):
                    dve.wait_ge(part_ready[g], k + (base + 1))
                    dve.tensor_copy(part16[:, pair_of[g]], part[g][:]).then_inc(part_copied[g], 1)

                def decide(g, k):
                    p = pair_of[g]
                    after, gain = ((digit[:, k + 1:k + 2], digit[:, k:k + 1]) if isinstance(k, int)
                                   else (digit[:, at(k + 1)], digit[:, at(k)]))
                    dve.tensor_scalar(low[:, p], cand[:, p], after, None, ALU.subtract).then_inc(low_ready[g], 1)
                    dve.wait_ge(total_ready[g], k + (base + 1))
                    dve.tensor_tensor(ge[:, p], total[g][:], want[:, p], ALU.is_ge).then_inc(ge_ready[g], 1)
                    dve.wait_ge(low_ready[g], k + (decided + 1))
                    dve.wait_ge(ge_ready[g], k + (decided + 1))
                    dve.scalar_tensor_tensor(out=cand[:, p], in0=ge[:, p], scalar=gain, in1=low[:, p],
                                             op0=ALU.mult, op1=ALU.add).then_inc(cand_ready[g], 1)
                    dve.wait_ge(cand_ready[g], k + (decided + 1))

                def search_pass(k, first):
                    let_in(0, 0)
                    if not first:
                        copy_part(1, k - 1)
                    let_in(0, 1)
                    if not first:
                        decide(1, k - 1)
                    let_in(1, 0)
                    copy_part(0, k)
                    let_in(1, 1)
                    decide(0, k)

                search_pass(0, True)
                with dve.Fori(0, (BITS - 1) // 3) as three:
                    for more in range(3):
                        search_pass(three * 3 + (1 + more), False)
                copy_part(1, BITS - 1)
                decide(1, BITS - 1)
                for g in range(2):
                    for j in range(2):
                        let_in(g, j)
                step(dve.tensor_scalar(found[:, half, :], cand[:], 1.0, None, ALU.subtract))
                for g in range(2):
                    copy_part(g, BITS)
                for g in range(2):
                    dve.wait_ge(total_ready[g], BITS + (base + 1))
                    step(dve.tensor_tensor(want[:, pair_of[g]], want[:, pair_of[g]], total[g][:], ALU.subtract))
                if half == 0:
                    dve.memset(cand[:], 32768.0)
                    for b in range(B):
                        ins = dve.scalar_tensor_tensor(out=lo[:, b, :], in0=hi[:, b, :], scalar=found[:, 0, b:b + 1],
                                                       in1=lo[:, b, :], op0=ALU.is_equal, op1=ALU.mult)
                    step(ins)

            step(dve.tensor_copy(halves[:], found[:]))
            step(dve.tensor_scalar(halves[:, 0, :], halves[:, 0, :], 16, None, ALU.logical_shift_left))
            step(dve.tensor_tensor(tkey[:], halves[:, 0, :], halves[:, 1, :], ALU.bitwise_or))
            step(dve.tensor_scalar(tsign[:], tkey[:], 31, 0x7FFFFFFF, ALU.arith_shift_right, ALU.bitwise_and))
            step(dve.tensor_tensor(thr[:], tkey[:], tsign[:], ALU.bitwise_xor))
            thrf = thr[:].bitcast(F32)
            eq = key[:].bitcast(F32)
            with dve.Fori(0, B) as b:
                for t in range(TT):
                    n = b * TT + t
                    dve.tensor_scalar(eq[:, at(n), :], adj[:, at(n), :], thrf[:, at(b)], None,
                                      ALU.is_equal, ALU.add, accum_out=ties[:, at(n)]).then_inc(ties_counted, 1)
            dve.wait_ge(pref_ready, 1)
            step(dve.tensor_copy(before[:].rearrange("p (b t) -> p b t", t=TT), pref[:]))
            base = n_dv[0]
            with dve.Fori(0, B) as b:
                for t in range(TT):
                    n = b * TT + t
                    c = n * 3 + base
                    r = rank[:, t % 2, :]
                    flat = lambda v: v.rearrange("p o d -> p (o d)")
                    xs, es = flat(X[:, at(n), :]), flat(eq[:, at(n), :])
                    dve.tensor_tensor_scan(r, es, zeros[:], before[:, at(n)], ALU.add, ALU.add).then_inc(dv, 1)
                    dve.scalar_tensor_tensor(out=xs, in0=flat(adj[:, at(n), :]), scalar=thrf[:, at(b)], in1=xs,
                                             op0=ALU.is_gt, op1=ALU.add)
                    dve.wait_ge(dv, c + 1)
                    dve.scalar_tensor_tensor(out=r, in0=r, scalar=want[:, at(b)], in1=es,
                                             op0=ALU.is_le, op1=ALU.mult).then_inc(dv, 1)
                    dve.wait_ge(dv, c + 2)
                    dve.tensor_tensor(xs, xs, r, ALU.add).then_inc(dv, 1)
            n_dv[0] += 3 * NT


XS = 8.0
WS = 32.0
UNSCALE = 1.0 / (XS * WS)


def flat(v):
    return v.rearrange("p o d -> p (o d)")


def products(pe, out, left, right, start, stop):
    (lh, ll), (rh, rl) = left, right
    pe.matmul(out, lh, rh, start=start, stop=False)
    pe.matmul(out, lh, rl, start=False, stop=False)
    return pe.matmul(out, ll, rh, start=False, stop=stop)


def split_weights(nc, name, jobs):
    WIDE = 2048
    pieces = []
    for src, hi, lo, scale in jobs:
        n = src.shape[2]
        for a in range(src.shape[1]):
            for c in range(0, n, WIDE):
                w = min(WIDE, n - c)
                pieces.append((src[:, a, c:c + w], hi[:, a, c:c + w], lo[:, a, c:c + w], w, scale))
    SLOTS = 3
    with ExitStack() as ctx:
        m = Mem(nc, ctx, name)
        stage = m.sb("w_stage", [P, SLOTS, WIDE])
        loaded = [m.sem(f"w_loaded_{s}") for s in range(SLOTS)]
        hi_done, lo_done = m.sem("w_hi_done"), m.sem("w_lo_done")
        block = ctx.enter_context(nc.Block())

        @block.sync
        def _(sp):
            for j, (src, _, _, w, _) in enumerate(pieces):
                if j >= SLOTS:
                    sp.wait_ge(lo_done, j - SLOTS + 1)
                sp.dma_start(stage[:, j % SLOTS, 0:w], src).then_inc(loaded[j % SLOTS], 16)

        @block.scalar
        def _(act):
            for j, (_, hi, _, w, scale) in enumerate(pieces):
                act.wait_ge(loaded[j % SLOTS], 16 * (j // SLOTS + 1))
                act.activation(hi, stage[:, j % SLOTS, 0:w], ACT.Copy, scale=scale).then_inc(hi_done, 1)

        @block.vector
        def _(dve):
            for j, (_, hi, lo, w, scale) in enumerate(pieces):
                dve.wait_ge(hi_done, j + 1)
                dve.scalar_tensor_tensor(out=lo, in0=stage[:, j % SLOTS, 0:w], scalar=scale, in1=hi, op0=ALU.mult,
                                         op1=ALU.subtract).then_inc(lo_done, 1)


class Heads:

    CREDIT = 2

    def __init__(self, m, S, PT, O, ident, scores, values, out, scale, lag=2):
        self.S, self.PT, self.O, self.ident = S, PT, O, ident
        self.scores, self.values, self.out, self.scale = scores, values, out, scale
        self.lag, self.slots = lag, 2 if lag == 2 else 4
        self.prob = m.sb("prob", [P, 2, D])
        self.turned = m.sb("turned", [P, self.slots, 2, TT, P], F16)
        self.nmax = m.sb("head_nmax", [P, TT])
        self.nbias = m.sb("head_nbias", [P, TT])
        self.rsum = m.sb("head_rsum", [P, TT])
        self.rinv = m.sb("head_rinv", [P, TT])
        self.scores_ready = m.sem("scores_ready")
        self.max_raw = m.sem("max_raw")
        self.max_ready = m.sem("max_ready")
        self.exp_done = m.sem("exp_done")
        self.turn_ready = m.sem("turn_ready")
        self.copied_a = m.sem("copied_by_act")
        self.copied_v = m.sem("copied_by_dve")
        self.pv_ready = m.sem("pv_ready")
        self.rinv_ready = m.sem("rinv_ready")
        self.out_copied = m.sem("out_copied")

    def credits(self, pool):
        for s in (self.exp_done, self.turn_ready, self.copied_a, self.copied_v, self.out_copied):
            pool.sem_inc(s, self.CREDIT)
        pool.sem_inc(self.pv_ready, self.slots)

    def pe_scores(self, pe, h, t, u):
        pe.wait_ge(self.exp_done, u + 1)
        self.scores(pe, self.S[t % 2], h, t).then_inc(self.scores_ready, 1)

    def pe_wait_copy(self, pe, u, ahead):
        pe.wait_ge(self.copied_a, u + 1 + ahead)
        pe.wait_ge(self.copied_v, u + 1 + ahead)

    def pe_turn(self, pe, t, u):
        pe.wait_ge(self.exp_done, u + 1 + self.CREDIT)
        self.pe_wait_copy(pe, u, 0)
        for s in range(TT):
            mm = pe.transpose(self.PT[t % 2][:, s * P:(s + 1) * P], self.prob[:, t % 2, s * P:(s + 1) * P],
                              self.ident)
        mm.then_inc(self.turn_ready, 1)

    def pe_values(self, pe, h, t, u):
        self.pe_wait_copy(pe, u, self.CREDIT)
        pe.wait_ge(self.out_copied, u + 1)
        for s in range(TT):
            slot = self.turned[:, t % self.slots]
            mm = products(pe, self.O[t % 2], (slot[:, 0, s, :], slot[:, 1, s, :]), self.values(h, s),
                          s == 0, s == TT - 1)
        mm.then_inc(self.pv_ready, 1)

    def act_exp(self, act, t, u):
        act.wait_ge(self.max_ready, u + 1)
        act.wait_ge(self.turn_ready, u + 1)
        bias = self.nmax if self.scale == 1.0 else self.nbias
        act.activation(self.prob[:, t % 2, :], self.S[t % 2], ACT.Exp, bias=bias[:, t:t + 1], scale=self.scale,
                       accum_out=self.rsum[:, t:t + 1]).then_inc(self.exp_done, 1)

    def act_copy(self, act, t, u):
        act.wait_ge(self.turn_ready, u + 1 + self.CREDIT)
        act.wait_ge(self.pv_ready, u + 1)
        act.activation(self.turned[:, t % self.slots, 0].rearrange("p s q -> p (s q)"), self.PT[t % 2], ACT.Copy)\
           .then_inc(self.copied_a, 1)

    def dve_max(self, dve, t, u):
        dve.wait_ge(self.scores_ready, u + 1)
        ins = dve.tensor_reduce(self.nmax[:, t:t + 1], self.S[t % 2], AX.X, ALU.max, negate=True)
        if self.scale == 1.0:
            ins.then_inc(self.max_ready, 1)
        else:
            ins.then_inc(self.max_raw, 1)
            dve.wait_ge(self.max_raw, u + 1)
            dve.tensor_scalar(self.nbias[:, t:t + 1], self.nmax[:, t:t + 1], self.scale, None, ALU.mult)\
               .then_inc(self.max_ready, 1)

    def dve_copy(self, dve, t, u):
        dve.wait_ge(self.exp_done, u + 1 + self.CREDIT)
        dve.reciprocal(self.rinv[:, t:t + 1], self.rsum[:, t:t + 1]).then_inc(self.rinv_ready, 1)
        dve.wait_ge(self.copied_a, u + 1 + self.CREDIT)
        slot = self.turned[:, t % self.slots]
        dve.tensor_tensor(slot[:, 1].rearrange("p s q -> p (s q)"), self.PT[t % 2],
                          slot[:, 0].rearrange("p s q -> p (s q)"), ALU.subtract).then_inc(self.copied_v, 1)

    def dve_out(self, dve, h, t, u):
        dve.wait_ge(self.pv_ready, u + 1 + self.slots)
        dve.wait_ge(self.rinv_ready, u + 1)
        dve.tensor_scalar(self.out(h, t), self.O[t % 2], self.rinv[:, t:t + 1], None, ALU.mult)\
           .then_inc(self.out_copied, 1)

    def run(self, eng, heads, first_unit, current, turn, done, beside=None, turn_lag=1, done_lag=None):
        stages = ((turn, turn_lag), (done, done_lag or self.lag))

        def head(h, first, last):
            u0 = first_unit + h * TT
            for t in range(TT):
                current(h, t, u0 + t)
                if beside is not None:
                    beside(h, t, last)
                for stage, lag in stages:
                    if not (first and t < lag):
                        stage(h if t >= lag else h - 1, (t - lag) % TT, u0 + (t - lag))

        self.parity, self.nth = 0, 1
        head(0, True, False)
        with eng.Fori(0, (heads - 2) // 2) as pair:
            for self.parity in (1, 0):
                self.nth = pair + 2
                head(pair * 2 + (2 - self.parity), False, False)
        self.parity = 1
        head(heads - 1, False, True)
        end = first_unit + heads * TT
        for more in range(self.lag):
            for stage, lag in stages:
                if more < lag:
                    stage(heads - 1, TT + more - lag, end + more - lag)


def small_attention_phase(nc, X, const, a, W, Wo):
    H, DH = 16, 32
    EPS = 1e-6
    w_qkv, w_out = W, Wo
    with ExitStack() as ctx:
        m = Mem(nc, ctx, "small_")
        c_T = m.sb("cond_T", [P, KD, B])
        b_emb = m.sb("b_emb", [P, 2 * KD])
        g_norm = m.sb("g_norm", [P, KD])
        g_qk = m.sb("g_qk", [P, 2, DH])
        gg = m.sb("gg", [P, 1, DH])
        mod = m.sb("mod", [P, 2 * KD, B])
        ss = m.sb("ss", [P, NT])
        rstd = m.sb("rstd", [P, NT])
        tmp = m.sb("tmp", [P, 2, D])
        xn = m.sb("xn", [P, TT, D])
        y32 = m.sb("y32", [P, KD, T])
        yh, yl = m.sb("yh", [P, KD, T], F16), m.sb("yl", [P, KD, T], F16)
        raw = m.sb("raw", [P, TT, 2, D])
        w_emb = raw[:].rearrange("p t a d -> p t (a d)")
        vh, vl = m.sb("vh", [P, TT, D], F16), m.sb("vl", [P, TT, D], F16)
        ssq = m.sb("ssq", [P, TT, 2 * H])
        rq = m.sb("rq", [P, TT, 2 * H])
        q4, k4 = m.sb("q4", [P, TT, H, 4, DH], F16), m.sb("k4", [P, TT, H, 4, DH], F16)
        qT, kT = m.sb("qT", [P, H, T], F16), m.sb("kT", [P, H, T], F16)
        O = y32
        oh, ol = yh, yl
        bank = [m.ps(f"bank{i}", [P, D]) for i in range(6)]
        q_bank = [m.ps(f"qbank{i}", [P, T], F16) for i in range(2)]

        cond_loaded = m.sem("cond_loaded")
        mod_sum = m.sem("mod_sum")
        mod_ready = m.sem("mod_ready")
        sq_done = m.sem("sq_done")
        ms_ready = m.sem("ms_ready")
        root_done = m.sem("root_done")
        rstd_ready = m.sem("rstd_ready")
        gg_ready = m.sem("gg_ready")
        xn_ready = m.sem("xn_ready")
        xT_ready = m.sem("xT_ready")
        y_ready = m.sem("y_ready")
        yh_ready = m.sem("yh_ready")
        yl_ready = m.sem("yl_ready")
        qkv_ready = m.sem("qkv_ready")
        square_ready = m.sem("square_ready")
        ssq_ready = m.sem("ssq_ready")
        hms_ready = m.sem("hms_ready")
        hroot_done = m.sem("hroot_done")
        rq_ready = m.sem("rq_ready")
        normed = m.sem("normed")
        q_gained = m.sem("q_gained")
        hi4_done = m.sem("hi4_done")
        lo4_done = m.sem("lo4_done")
        qk_turned = m.sem("qk_turned")
        q_copied = m.sem("q_copied")
        k_copied = m.sem("k_copied")
        o_turned = m.sem("o_turned")
        oh_ready = m.sem("oh_ready")
        ol_ready = m.sem("ol_ready")
        y_out = m.sem("y_out")
        y_added = m.sem("y_added")
        x_added = m.sem("x_added")
        bank_free = m.sem("bank_free")
        vl_ready = m.sem("vl_ready")

        hs = Heads(
            m, S=[bank[0][:], bank[1][:]], PT=[bank[2][:], bank[3][:]], O=[bank[4][:, 0:DH], bank[5][:, 0:DH]],
            ident=const["ident"][:],
            scores=lambda pe, s, h, t: pe.matmul(s, flat(qT[:, at(h), t * P:(t + 1) * P]), flat(kT[:, at(h), :]),
                                                 start=True, stop=True),
            values=lambda h, s: (vh[:, s, at(h * DH, DH)], vl[:, s, at(h * DH, DH)]),
            out=lambda h, t: O[:, t, at(h * DH, DH)],
            scale=1.0, lag=3)
        qkv_bank = bank[4:6]

        block = ctx.enter_context(nc.Block())

        @block.sync
        def _(sp):
            sp.dma_start(c_T[:], a["cond_columns"]).then_inc(cond_loaded, 16)
            sp.dma_start(w_emb, a["L1_cond_W_emb"].rearrange("(k p) n -> p k n", p=P)).then_inc(cond_loaded, 16)
            sp.dma_start(b_emb[:], a["b_emb_columns"]).then_inc(cond_loaded, 16)
            sp.dma_start(g_norm[:], a["g_norm_columns"]).then_inc(cond_loaded, 16)
            for j, g in enumerate(("L1_cond_g_q", "L1_cond_g_k")):
                sp.dma_start(g_qk[:, j, :], a[g].rearrange("(o d) -> o d", o=1).broadcast_to([P, DH]))\
                  .then_inc(cond_loaded, 16)

        @block.gpsimd
        def _(pool):
            hs.credits(pool)
            pool.sem_inc(xT_ready, 1)
            pool.wait_ge(rstd_ready, 1)
            with pool.Fori(0, B) as b:
                for t in range(TT):
                    if t == 0:
                        pool.wait_ge(xT_ready, b * KD + 1)
                    pool.tensor_tensor(xn[:, t, :], flat(X[:, at(b * TT + t), :]),
                                       rstd[:, at(b * TT + t)].broadcast_to([P, D]), ALU.mult).then_inc(xn_ready, 1)
                for t in range(TT):
                    pool.wait_ge(bank_free, b * 12 + t * 3 + 2 + 2)
                    pool.wait_ge(ssq_ready, b * TT + t + 1)
                    pool.tensor_tensor(tmp[:].rearrange("p a d -> p (a d)"), raw[:, t].rearrange("p a d -> p (a d)"),
                                       raw[:, t].rearrange("p a d -> p (a d)"), ALU.mult).then_inc(square_ready, 1)

        @block.tensor
        def _(pe):
            pe.wait_ge(cond_loaded, 96)
            for f in range(2 * KD):
                for k in range(KD):
                    mm = pe.matmul(bank[0][:, f * B:(f + 1) * B], w_emb[:, k, f * P:(f + 1) * P], c_T[:, k, :],
                                   start=(k == 0), stop=(k == KD - 1))
            mm.then_inc(mod_sum, 1)
            pe.wait_ge(mod_ready, 3)
            with pe.Fori(0, B) as b:
                pe.wait_ge(xn_ready, (b + 1) * TT)
                for k in range(KD):
                    for t in range(TT):
                        mm = pe.transpose(bank[k][:, t * P:(t + 1) * P], xn[:, t, k * P:(k + 1) * P],
                                          const["ident"][:])
                    mm.then_inc(xT_ready, 1)
                for t in range(TT):
                    for j in range(3):
                        n = t * 3 + j
                        if n == 0:
                            pe.wait_ge(yl_ready, (b + 1) * KD)
                        pe.wait_ge(bank_free, b * 12 + n + 1)
                        if j == 1:
                            pe.wait_ge(vl_ready, b * TT + t + 1)
                        for k in range(KD):
                            mm = products(pe, qkv_bank[n % 2][:],
                                          (yh[:, k, t * P:(t + 1) * P], yl[:, k, t * P:(t + 1) * P]),
                                          (w_qkv[0][:, k, j * D:(j + 1) * D], w_qkv[1][:, k, j * D:(j + 1) * D]),
                                          k == 0, k == KD - 1)
                        mm.then_inc(qkv_ready, 1)
                hs_first = b * (H * TT)

                def turn_qk(h):
                    pe.wait_ge(q_copied, b * H + h + 1)
                    pe.wait_ge(k_copied, b * H + h + 1)
                    for i, src in enumerate((q4, k4)):
                        for t in range(TT):
                            mm = pe.transpose(q_bank[i][:, t * P:(t + 1) * P],
                                              src[:, t, at(h), :, :].rearrange("p o f d -> p (o f d)"),
                                              const["ident16"][:])
                    mm.then_inc(qk_turned, 1)

                pe.wait_ge(vl_ready, (b + 1) * TT + 1)
                pe.wait_ge(lo4_done, (b + 1) * TT * 2)
                turn_qk(0)

                def current(h, t, u):
                    if t == 0:
                        pe.wait_ge(q_copied, b * H + h + 2)
                        pe.wait_ge(k_copied, b * H + h + 2)
                    hs.pe_scores(pe, h, t, u)

                def beside(h, t, last):
                    if t == 1 and not last:
                        turn_qk(h + 1)

                hs.run(pe, H, hs_first, current, lambda h, t, u: hs.pe_turn(pe, t, u),
                       lambda h, t, u: hs.pe_values(pe, h, t, u), beside)
                pe.wait_ge(hs.out_copied, (b + 1) * (H * TT) + hs.CREDIT)
                for k in range(KD):
                    for t in range(TT):
                        mm = pe.transpose(bank[k][:, t * P:(t + 1) * P], O[:, t, k * P:(k + 1) * P],
                                          const["ident"][:])
                    mm.then_inc(o_turned, 1)
                pe.wait_ge(ol_ready, (b + 1) * KD)
                for t in range(TT):
                    pe.wait_ge(y_added, b * TT + t + 1)
                    for k in range(KD):
                        mm = products(pe, qkv_bank[t % 2][:],
                                      (oh[:, k, t * P:(t + 1) * P], ol[:, k, t * P:(t + 1) * P]),
                                      (w_out[0][:, k, :], w_out[1][:, k, :]), k == 0, k == KD - 1)
                    mm.then_inc(y_out, 1)

        @block.scalar
        def _(act):
            with act.Fori(0, NT) as n:
                act.wait_ge(sq_done, n)
                act.activation(flat(tmp[:, 0:1, :]), flat(X[:, at(n), :]), ACT.Square, accum_out=ss[:, at(n)])\
                   .then_inc(sq_done, 1)
            act.wait_ge(ms_ready, 1)
            act.activation(rstd[:], ss[:], ACT.Sqrt).then_inc(root_done, 1)
            with act.Fori(0, B) as b:
                for k in range(KD):
                    act.wait_ge(y_ready, b * KD + k + 1)
                    act.activation(yh[:, k, :], y32[:, k, :], ACT.Copy).then_inc(yh_ready, 1)
                def root(t):
                    act.wait_ge(hms_ready, b * TT + t + 1)
                    act.activation(rq[:, t, :], ssq[:, t, :], ACT.Sqrt).then_inc(hroot_done, 1)

                def high_parts(t):
                    for j, dst in enumerate((q4, k4)):
                        act.wait_ge(q_gained, b * TT * 2 + t * 2 + j + 1)
                        src = raw[:, t, j, :].rearrange("p (h d) -> p h d", h=H)
                        for e in range(2):
                            slot = e if j == 0 else 2 * e
                            ins = act.activation(dst[:, t, :, slot, :], src, ACT.Copy)
                        ins.then_inc(hi4_done, 1)

                for t in range(TT):
                    for j in range(3):
                        n = t * 3 + j
                        act.wait_ge(qkv_ready, b * 12 + n + 1)
                        dst, scale = (raw[:, t, j, :], UNSCALE) if j < 2 else (vh[:, t, :], XS * UNSCALE)
                        act.activation(dst, qkv_bank[n % 2][:], ACT.Copy, scale=scale).then_inc(bank_free, 1)
                        if t >= 1 and j < 2:
                            (root, high_parts)[j](t - 1)
                root(TT - 1)
                act.preload_act_table(ACT.Exp)
                high_parts(TT - 1)

                def copy_q(h):
                    act.wait_ge(qk_turned, b * H + h + 1)
                    act.activation(flat(qT[:, at(h), :]), q_bank[0][:], ACT.Copy).then_inc(q_copied, 1)

                copy_q(0)

                def beside(h, t, last):
                    if t == 1 and not last:
                        copy_q(h + 1)

                hs.run(act, H, b * (H * TT), lambda h, t, u: hs.act_exp(act, t, u),
                       lambda h, t, u: hs.act_copy(act, t, u), lambda h, t, u: None, beside)
                for k in range(KD):
                    act.wait_ge(o_turned, b * KD + k + 1)
                    act.activation(oh[:, k, :], bank[k][:], ACT.Copy).then_inc(oh_ready, 1)

        @block.vector
        def _(dve):
            dve.wait_ge(cond_loaded, 96)
            dve.tensor_tensor(gg[:, 0, :], g_qk[:, 0, :], g_qk[:, 1, :], ALU.mult).then_inc(gg_ready, 1)
            dve.wait_ge(gg_ready, 1)
            dve.tensor_scalar(gg[:], gg[:], float(DH) ** -0.5, None, ALU.mult).then_inc(gg_ready, 1)
            dve.wait_ge(sq_done, NT)
            dve.tensor_scalar(ss[:], ss[:], 1.0 / D, EPS, ALU.mult, ALU.add).then_inc(ms_ready, 1)
            dve.wait_ge(root_done, 1)
            dve.reciprocal(rstd[:], rstd[:]).then_inc(rstd_ready, 1)
            dve.wait_ge(mod_sum, 1)
            for f in range(2 * KD):
                dve.tensor_scalar(mod[:, f, :], bank[0][:, f * B:(f + 1) * B], b_emb[:, f:f + 1],
                                  1.0 if f < KD else 0.0, ALU.add, ALU.add)
            dve.engine_nop().then_inc(mod_ready, 1)
            dve.wait_ge(mod_ready, 1)
            for f in range(KD):
                dve.tensor_scalar(mod[:, f, :], mod[:, f, :], g_norm[:, f:f + 1], XS, ALU.mult, ALU.mult)
            dve.tensor_scalar(mod[:, KD:2 * KD, :], mod[:, KD:2 * KD, :], XS, None, ALU.mult).then_inc(mod_ready, 1)
            dve.wait_ge(mod_ready, 2)
            dve.engine_nop().then_inc(mod_ready, 1)
            dve.sem_inc(bank_free, 2)
            dve.sem_inc(y_added, 2)
            dve.sem_inc(q_copied, 1)
            dve.sem_inc(k_copied, 1)
            dve.sem_inc(ssq_ready, 1)
            dve.sem_inc(vl_ready, 1)
            with dve.Fori(0, B) as b:
                for k in range(KD):
                    dve.wait_ge(xT_ready, b * KD + k + 2)
                    dve.tensor_scalar(y32[:, k, :], bank[k][:], mod[:, k, at(b)], mod[:, KD + k, at(b)], ALU.mult,
                                      ALU.add).then_inc(y_ready, 1)
                for k in range(KD):
                    dve.wait_ge(yh_ready, b * KD + k + 1)
                    dve.tensor_tensor(yl[:, k, :], y32[:, k, :], yh[:, k, :], ALU.subtract).then_inc(yl_ready, 1)
                for t in range(TT):
                    dve.wait_ge(bank_free, b * 12 + t * 3 + 3 + 2)
                    dve.scalar_tensor_tensor(out=vl[:, t, :], in0=qkv_bank[(t * 3 + 2) % 2][:], scalar=XS * UNSCALE,
                                             in1=vh[:, t, :], op0=ALU.mult, op1=ALU.subtract).then_inc(vl_ready, 1)
                    dve.wait_ge(square_ready, b * TT + t + 1)
                    dve.tensor_reduce(ssq[:, t, :], tmp[:].rearrange("p a (h d) -> p (a h) d", d=DH), AX.X, ALU.add)\
                       .then_inc(ssq_ready, 1)
                    dve.wait_ge(ssq_ready, b * TT + t + 2)
                    dve.tensor_scalar(ssq[:, t, :], ssq[:, t, :], 1.0 / DH, EPS, ALU.mult, ALU.add)\
                       .then_inc(hms_ready, 1)
                    dve.wait_ge(hroot_done, b * TT + t + 1)
                    dve.reciprocal(rq[:, t, :], rq[:, t, :]).then_inc(rq_ready, 1)
                    dve.wait_ge(rq_ready, b * TT + t + 1)
                    for j in range(2):
                        v = raw[:, t, j, :].rearrange("p (h d) -> p h d", h=H)
                        r = rq[:, t, j * H:(j + 1) * H].rearrange("p (h o) -> p h o", o=1).broadcast_to([P, H, DH])
                        if j == 0:
                            dve.tensor_tensor(v, v, r, ALU.mult).then_inc(normed, 1)
                            dve.wait_ge(normed, b * TT + t + 1)
                            dve.tensor_tensor(v, v, gg[:].broadcast_to([P, H, DH]), ALU.mult).then_inc(q_gained, 1)
                        else:
                            dve.tensor_tensor(v, v, r, ALU.mult).then_inc(q_gained, 1)
                    for j, dst in enumerate((q4, k4)):
                        src = raw[:, t, j, :].rearrange("p (h d) -> p h d", h=H)
                        dve.wait_ge(hi4_done, b * TT * 2 + t * 2 + j + 1)
                        for e in range(2):
                            slot = 2 + e if j == 0 else 1 + 2 * e
                            ins = dve.tensor_tensor(dst[:, t, :, slot, :], src, dst[:, t, :, 0, :], ALU.subtract)
                        ins.then_inc(lo4_done, 1)

                def copy_k(h):
                    dve.wait_ge(qk_turned, b * H + h + 1)
                    dve.tensor_copy(flat(kT[:, at(h), :]), q_bank[1][:]).then_inc(k_copied, 1)

                copy_k(0)

                def beside(h, t, last):
                    if t == 1 and not last:
                        copy_k(h + 1)

                hs.run(dve, H, b * (H * TT), lambda h, t, u: hs.dve_max(dve, t, u),
                       lambda h, t, u: hs.dve_copy(dve, t, u), lambda h, t, u: hs.dve_out(dve, h, t, u), beside,
                       turn_lag=2)
                for k in range(KD):
                    dve.wait_ge(oh_ready, b * KD + k + 1)
                    dve.tensor_tensor(ol[:, k, :], bank[k][:], oh[:, k, :], ALU.subtract).then_inc(ol_ready, 1)
                for t in range(TT):
                    xs = flat(X[:, at(b * TT + t), :])
                    dve.wait_ge(y_out, b * TT + t + 1)
                    dve.scalar_tensor_tensor(out=xs, in0=O[:, t, :], scalar=1.0 / XS, in1=xs,
                                             op0=ALU.mult, op1=ALU.add).then_inc(x_added, 1)
                    dve.wait_ge(x_added, b * TT + t + 1)
                    dve.scalar_tensor_tensor(out=xs, in0=qkv_bank[t % 2][:], scalar=UNSCALE, in1=xs,
                                             op0=ALU.mult, op1=ALU.add).then_inc(y_added, 1)


HS = 64.0
RS = 256.0
GS = HS * RS
GIS = 64.0


def gate_input_phase(nc, X, const, a, w_ih, gi):
    G = 3 * KD
    with ExitStack() as ctx:
        m = Mem(nc, ctx, "gatein_")
        bias = m.sb("gate_bias", [P, 2 * G])
        col = m.sb("gate_col", [P, G])
        x32 = m.sb("gi_x32", [P, TT, D])
        xh, xl = m.sb("gi_xh", [P, KD, T], F16), m.sb("gi_xl", [P, KD, T], F16)
        bank = [m.ps(f"gbank{i}", [P, D]) for i in range(8)]
        bias_loaded, col_ready = m.sem("bias_loaded"), m.sem("col_ready")
        x_copied, x_turned = m.sem("gx_copied"), m.sem("gx_turned")
        xh_ready, xl_ready = m.sem("gxh_ready"), m.sem("gxl_ready")
        full = m.sb("gi_full", [P, 2, T])
        sum_ready, out_taken = m.sem("gate_sum"), m.sem("gate_out_taken")
        hi_done, lo_done = m.sem("gi_hi_done"), m.sem("gi_lo_done")
        block = ctx.enter_context(nc.Block())
        out_bank = bank[4:8]
        place = lambda g: g if g < KD else g + KD if g < 2 * KD else g - KD

        @block.sync
        def _(sp):
            sp.dma_start(bias[:, 0:G], a["b_ih_columns"]).then_inc(bias_loaded, 16)
            sp.dma_start(bias[:, G:2 * G], a["b_hh_columns"]).then_inc(bias_loaded, 16)

        @block.gpsimd
        def _(pool):
            with pool.Fori(0, B) as b:
                for t in range(TT):
                    pool.wait_ge(x_turned, b * KD)
                    pool.tensor_copy(x32[:, t, :], flat(X[:, at(b * TT + t), :])).then_inc(x_copied, 1)

        @block.tensor
        def _(pe):
            with pe.Fori(0, B) as b:
                pe.wait_ge(x_copied, (b + 1) * TT)
                pe.wait_ge(xl_ready, b * KD)
                for k in range(KD):
                    for t in range(TT):
                        mm = pe.transpose(bank[k][:, t * P:(t + 1) * P], x32[:, t, k * P:(k + 1) * P],
                                          const["ident"][:])
                    mm.then_inc(x_turned, 1)
                pe.wait_ge(xl_ready, (b + 1) * KD)
                for g in range(G):
                    pe.wait_ge(out_taken, b * G + g + 1)
                    for k in range(KD):
                        mm = products(pe, out_bank[g % 4][:],
                                      (w_ih[0][:, k, g * P:(g + 1) * P], w_ih[1][:, k, g * P:(g + 1) * P]),
                                      (xh[:, k, :], xl[:, k, :]), k == 0, k == KD - 1)
                    mm.then_inc(sum_ready, 1)

        @block.scalar
        def _(act):
            act.wait_ge(col_ready, 2)
            act.sem_inc(out_taken, 4)
            with act.Fori(0, B) as b:
                for k in range(KD):
                    act.wait_ge(x_turned, b * KD + k + 1)
                    act.wait_ge(sum_ready, b * G)
                    act.activation(xh[:, k, :], bank[k][:], ACT.Copy, scale=XS).then_inc(xh_ready, 1)
                for g in range(G):
                    act.wait_ge(sum_ready, b * G + g + 1)
                    act.wait_ge(lo_done, b * G + g + 1)
                    act.activation(full[:, g % 2, :], out_bank[g % 4][:], ACT.Identity,
                                   bias=col[:, g:g + 1], scale=GIS * UNSCALE).then_inc(out_taken, 1)
                    act.wait_ge(out_taken, b * G + g + 5)
                    act.activation(flat(gi[:, 0, place(g), at(b), :]), full[:, g % 2, :], ACT.Copy).then_inc(hi_done, 1)

        @block.vector
        def _(dve):
            dve.wait_ge(bias_loaded, 32)
            dve.tensor_tensor(col[:, 0:2 * KD], bias[:, 0:2 * KD], bias[:, G:G + 2 * KD], ALU.add)
            dve.tensor_copy(col[:, 2 * KD:G], bias[:, 2 * KD:G]).then_inc(col_ready, 1)
            dve.wait_ge(col_ready, 1)
            dve.tensor_scalar(col[:], col[:], GIS, None, ALU.mult).then_inc(col_ready, 1)
            dve.sem_inc(lo_done, 2)
            with dve.Fori(0, B) as b:
                for k in range(KD):
                    dve.wait_ge(xh_ready, b * KD + k + 1)
                    dve.scalar_tensor_tensor(out=xl[:, k, :], in0=bank[k][:], scalar=XS, in1=xh[:, k, :],
                                             op0=ALU.mult, op1=ALU.subtract).then_inc(xl_ready, 1)
                for g in range(G):
                    dve.wait_ge(hi_done, b * G + g + 1)
                    dve.tensor_tensor(flat(gi[:, 1, place(g), at(b), :]), full[:, g % 2, :], flat(gi[:, 0, place(g), at(b), :]),
                                      ALU.subtract).then_inc(lo_done, 1)


class WeightStore:

    WIDE = 1024
    SLOTS = 2

    def __init__(self, nc, a):
        def scratch(name, shape):
            return nc.dram_tensor(name, shape, F16, kind="Internal").ap()

        self.qk = scratch("w_qk_parts", (P, DIT_H, 2, 2, KD, DIT_DH))
        self.v = scratch("w_v_parts", (P, 2, KD, INNER))
        self.out = scratch("w_out_parts", (P, 2, INNER // P, D))
        self.w1 = scratch("w_1_parts", (P, 2, KD, MLP))
        self.w2 = scratch("w_2_parts", (P, 2, MLP // P, D))
        rows = lambda w: w.rearrange("(k p) n -> p k n", p=P)
        qkv = rows(a["L3_cond_qkv_w"])
        W = self.WIDE
        self.pieces = []
        wide = W // (KD * DIT_DH)
        for h in range(0, DIT_H, wide):
            for i in range(2):
                c = i * INNER + h * DIT_DH
                self.pieces.append((qkv[:, :, c:c + wide * DIT_DH], self.qk[:, h:h + wide, i], True))
        for src, dst in ((qkv[:, :, 2 * INNER:3 * INNER], self.v), (rows(a["L3_cond_out_w"]), self.out),
                         (rows(a["L3_cond_ffn_w1"]), self.w1), (rows(a["L3_cond_ffn_w2"]), self.w2)):
            n = src.shape[2]
            if n >= W:
                for q in range(src.shape[1]):
                    for c in range(0, n, W):
                        self.pieces.append((src[:, q, c:c + W], dst[:, :, q, c:c + W], False))
            else:
                for q in range(0, src.shape[1], W // n):
                    self.pieces.append((src[:, q:q + W // n, :],
                                        dst[:, :, q:q + W // n, :].rearrange("p e k n -> p e (k n)"), False))

    def place(self, m):
        self.given = m.sb("given_w", [P, self.SLOTS, self.WIDE])
        self.parts = m.sb("parts_w", [P, self.SLOTS, 2 * self.WIDE], F16)
        self.loaded = [m.sem(f"piece_loaded_{s}") for s in range(self.SLOTS)]
        self.stored = [m.sem(f"piece_stored_{s}") for s in range(self.SLOTS)]
        self.scaled, self.hi_done, self.lo_done = m.sem("piece_scaled"), m.sem("piece_hi"), m.sem("piece_lo")

    def load(self, sp, j):
        src, s = self.pieces[j][0], j % self.SLOTS
        dst = self.given[:, s, :]
        if len(src.shape) == 3:
            dst = dst.rearrange("p (k n) -> p k n", k=src.shape[1])
        sp.dma_start(dst, src).then_inc(self.loaded[s], 16)

    def sync(self, sp):
        S = self.SLOTS
        for j in range(S):
            self.load(sp, j)
        for j, (_, dst, by_head) in enumerate(self.pieces):
            s = j % S
            sp.wait_ge(self.lo_done, j + 1)
            out = self.parts[:, s, :]
            out = (out.rearrange("p (h e k n) -> p h e k n", e=2, k=KD, n=DIT_DH) if by_head
                   else out.rearrange("p (e n) -> p e n", e=2))
            sp.dma_start(dst, out).then_inc(self.stored[s], 16)
            if j + S < len(self.pieces):
                self.load(sp, j + S)
        for s in range(S):
            sp.wait_ge(self.stored[s], 16 * len(self.pieces[s::S]))

    def pool(self, pool):
        S = self.SLOTS
        parts_begun = 0
        for j, (_, _, by_head) in enumerate(self.pieces):
            s = j % S
            w = self.given[:, s, :]
            pool.wait_ge(self.loaded[s], 16 * (j // S + 1))
            pool.tensor_scalar(w, w, WS, None, ALU.mult).then_inc(self.scaled, 1)
            pool.wait_ge(self.scaled, j + 1)
            if j >= S:
                pool.wait_ge(self.stored[s], 16 * (j // S))
            out = self.parts[:, s, :]
            if by_head:
                v = out.rearrange("p (h e k n) -> p h e k n", e=2, k=KD, n=DIT_DH)
                g = w.rearrange("p (k h n) -> p k h n", k=KD, n=DIT_DH)
                pairs = [(v[:, h, 0], v[:, h, 1], g[:, :, h, :]) for h in range(g.shape[2])]
            else:
                pairs = [(out[:, 0:self.WIDE], out[:, self.WIDE:2 * self.WIDE], w)]
            for n, (hi, lo, src) in enumerate(pairs):
                pool.tensor_copy(hi, src).then_inc(self.hi_done, 1)
            parts_begun += len(pairs)
            pool.wait_ge(self.hi_done, parts_begun)
            for n, (hi, lo, src) in enumerate(pairs):
                ins = pool.tensor_tensor(lo, src, hi, ALU.subtract)
            ins.then_inc(self.lo_done, 1)


def gru_phase(nc, X, const, a, w_hh, gi, x_out, store):
    G = 3 * KD
    HALF = KD // 2
    A, Z = slice(0, HALF), slice(HALF, KD)
    every, first, second = range(KD), range(HALF), range(HALF, KD)
    with ExitStack() as ctx:
        m = Mem(nc, ctx, "gru_")
        store.place(m)
        hist = m.sb("hist", [P, KD, B, T + 1])
        h0 = m.sb("h0", [P, KD, B])
        b_hh = m.sb("b_hh", [P, G])
        ones = m.sb("gru_ones", [P, B])
        scaled_ident = m.sb("scaled_ident", [P, P], F16)
        bn32 = m.sb("bn32", [P, KD, B])
        bn = m.sb("bn", [P, 2, KD, B], F16)
        state = m.sb("state", [P, 2, KD, B])
        parts = m.sb("state_parts", [P, KD, 2 * B], F16)
        r_in, z_in, n_in = (m.sb(f"{g}_in", [P, KD, B]) for g in "rzn")
        r, keep, n = (m.sb(f"{g}_gate", [P, KD, B]) for g in ("r", "new", "n"))
        u, v, d, e = (m.sb(s, [P, KD, B]) for s in "uvde")
        r_bank, na_bank, nb_bank, za_bank, zb_bank, turned_0, turned_1 = \
            (m.ps(s, [P, 4 * P]) for s in ("sum_r", "sum_na", "sum_nb", "sum_za", "sum_zb", "turned_0", "turned_1"))
        turned = [turned_0, turned_1]
        start_loaded, made = m.sem("start_loaded"), m.sem("gru_made")
        hi_a, hi_b, lo_a, lo_b = (m.sem(s) for s in ("hi_a", "hi_b", "lo_a", "lo_b"))
        state_a, state_b, kept = m.sem("state_a"), m.sem("state_b"), m.sem("history_kept")
        r_sum, na_sum, nb_sum, za_sum, zb_sum = (m.sem(s) for s in ("r_sum", "na_sum", "nb_sum", "za_sum", "zb_sum"))
        r_in_ready, r_ready = m.sem("r_in_ready"), m.sem("r_ready")
        ua, ub, va, vb = (m.sem(s) for s in ("ua_ready", "ub_ready", "va_ready", "vb_ready"))
        n_in_a, n_in_b, n_a, n_b = (m.sem(s) for s in ("n_in_a", "n_in_b", "n_a", "n_b"))
        za_in, zb_in, keep_a, keep_b = (m.sem(s) for s in ("za_in_ready", "zb_in_ready", "keep_a", "keep_b"))
        da, db, ea, eb = (m.sem(s) for s in ("da_ready", "db_ready", "ea_ready", "eb_ready"))
        back_turned, added, stored = m.sem("back_turned"), m.sem("added"), m.sem("gru_stored")
        block = ctx.enter_context(nc.Block())

        def column(bank, f):
            return bank[:, f * 2 * B:(f + 1) * 2 * B]

        def n_part(fs):
            columns = r_bank[:, (KD + fs[0]) * 2 * B:(KD + fs[-1] + 1) * 2 * B]
            return columns.rearrange("p (f c) -> p f c", c=2 * B)[:, :, 0:B]

        @block.sync
        def _(sp):
            sp.dma_start(h0[:], a["cond_columns"]).then_inc(start_loaded, 16)
            sp.dma_start(b_hh[:], a["b_hh_columns"]).then_inc(start_loaded, 16)
            store.sync(sp)
            xo = x_out.rearrange("b (t p) d -> p (b t) d", p=P)
            for b in range(B):
                sp.wait_ge(added, (b + 1) * TT)
                sp.dma_start(xo[:, b * TT:(b + 1) * TT, :], X[:, b * TT:(b + 1) * TT, :]).then_inc(stored, 16)
            sp.wait_ge(stored, 16 * B)

        @block.gpsimd
        def _(pool):
            store.pool(pool)

        @block.tensor
        def _(pe):
            def low(bank, gate, fs, ks):
                for f in fs:
                    for k in ks:
                        c = (gate * KD + f) * P
                        mm = pe.matmul(column(bank, f)[:, 0:B], w_hh[1][:, k, c:c + P], parts[:, k, 0:B],
                                       start=False, stop=False, skip_group_check=True)
                return mm

            def high(bank, gate, fs, ks):
                for f in fs:
                    for k in ks:
                        c = (gate * KD + f) * P
                        mm = pe.matmul(column(bank, f), w_hh[0][:, k, c:c + P], parts[:, k, :],
                                       start=False, stop=False, skip_group_check=True)
                return mm

            def bring(out, what, start=True):
                pe.matmul(out, scaled_ident[:], what, start=start, stop=False, skip_group_check=True)

            def columns(bank, fs):
                return bank[:, fs[0] * 2 * B:(fs[-1] + 1) * 2 * B]

            def step_in(e, g, n, i):
                return gi[:, e, g:g + n, :, at(i)].rearrange("p f b o -> p f (b o)")

            pe.wait_ge(made, KD + 6)
            with pe.Fori(0, T // 2) as pair:
                for par in range(2):
                    i = pair * 2 + par
                    pe.wait_ge(n_in_b, i + 1)
                    for bank, fs in ((na_bank, first), (nb_bank, second)):
                        bring(columns(bank, fs), bn[:, :, fs[0]:fs[-1] + 1, :].rearrange("p e f b -> p f e b"))
                    r_and_n = r_bank[:, 0:2 * KD * 2 * B].rearrange("p (f c) -> p f c", c=2 * B)[:, :, 0:B]
                    for e in range(2):
                        bring(r_and_n, step_in(e, 0, 2 * KD, i), start=e == 0)
                    pe.wait_ge(hi_a, i + 1)
                    low(r_bank, 0, every, first)
                    low(na_bank, 2, first, first)
                    pe.wait_ge(zb_in, i + 1)
                    for bank, fs in ((za_bank, first), (zb_bank, second)):
                        bring(columns(bank, fs), gi[:, :, 2 * KD + fs[0]:2 * KD + fs[-1] + 1, :, at(i)]
                              .rearrange("p e f b o -> p f e (b o)"))
                    low(nb_bank, 2, second, first)
                    pe.wait_ge(hi_b, i + 1)
                    low(r_bank, 0, every, second)
                    pe.wait_ge(lo_a, i + 1)
                    high(r_bank, 0, every, first)
                    pe.wait_ge(lo_b, i + 1)
                    high(r_bank, 0, every, second).then_inc(r_sum, 1)
                    low(na_bank, 2, first, second)
                    high(na_bank, 2, first, every).then_inc(na_sum, 1)
                    low(za_bank, 1, first, every)
                    high(za_bank, 1, first, every).then_inc(za_sum, 1)
                    low(nb_bank, 2, second, second)
                    high(nb_bank, 2, second, every).then_inc(nb_sum, 1)
                    low(zb_bank, 1, second, every)
                    high(zb_bank, 1, second, every).then_inc(zb_sum, 1)
            pe.wait_ge(kept, T + 1)
            for b in range(B):
                for t in range(TT):
                    w = b * TT + t
                    if w >= 2:
                        pe.wait_ge(added, w - 1)
                    for f in range(KD):
                        mm = pe.transpose(turned[w % 2][:, f * P:(f + 1) * P],
                                          hist[:, f, b, 1 + t * P:1 + (t + 1) * P], const["ident"][:])
                    mm.then_inc(back_turned, 1)

        step_of = lambda v, i: v[:, :, :, at(i)].rearrange("p f b o -> p f (b o)")

        @block.scalar
        def _(act):
            act.preload_act_table_set("sigmoid_and_others")
            with act.Fori(0, T // 2) as pair:
                for par in range(2):
                    i = pair * 2 + par
                    act.wait_ge(state_a, i + 1)
                    act.wait_ge(state_b, i + 1)
                    act.activation(step_of(hist, i), state[:, par], ACT.Copy).then_inc(kept, 1)
                    act.wait_ge(r_in_ready, i + 1)
                    act.activation(r[:], r_in[:], ACT.Sigmoid, scale=1.0 / GS).then_inc(r_ready, 1)
                    act.wait_ge(n_in_a, i + 1)
                    act.activation(n[:, A], n_in[:, A], ACT.Tanh, scale=1.0 / GS).then_inc(n_a, 1)
                    act.wait_ge(za_in, i + 1)
                    act.activation(keep[:, A], z_in[:, A], ACT.Sigmoid, scale=-1.0 / GS).then_inc(keep_a, 1)
                    act.wait_ge(n_in_b, i + 2)
                    act.activation(n[:, Z], n_in[:, Z], ACT.Tanh, scale=1.0 / GS).then_inc(n_b, 1)
                    act.wait_ge(zb_in, i + 2)
                    act.activation(keep[:, Z], z_in[:, Z], ACT.Sigmoid, scale=-1.0 / GS).then_inc(keep_b, 1)
            act.wait_ge(state_a, T + 1)
            act.wait_ge(state_b, T + 1)
            act.activation(hist[:, :, :, T], state[:, T % 2], ACT.Copy).then_inc(kept, 1)

        @block.vector
        def _(dve):
            dve.wait_ge(start_loaded, 32)
            dve.memset(ones[:], GIS).then_inc(made, 1)
            dve.tensor_scalar(scaled_ident[:], const["ident16"][:], GS / GIS, None, ALU.mult).then_inc(made, 1)
            dve.wait_ge(made, 2)
            for f in range(KD):
                dve.tensor_scalar(bn32[:, f, :], ones[:], b_hh[:, 2 * KD + f:2 * KD + f + 1], None, ALU.mult)\
                   .then_inc(made, 1)
            dve.wait_ge(made, KD + 2)
            dve.tensor_copy(bn[:, 0], bn32[:]).then_inc(made, 1)
            dve.wait_ge(made, KD + 3)
            dve.tensor_tensor(bn[:, 1], bn32[:], bn[:, 0], ALU.subtract).then_inc(made, 1)
            dve.tensor_scalar(state[:, 0], h0[:], HS, None, ALU.mult).then_inc(state_a, 1)
            dve.wait_ge(state_a, 1)
            dve.tensor_copy(parts[:, :, 0:B], state[:, 0]).then_inc(made, 1)
            dve.wait_ge(made, KD + 5)
            dve.tensor_tensor(parts[:, :, B:2 * B], state[:, 0], parts[:, :, 0:B], ALU.subtract).then_inc(made, 1)
            for s in (state_b, hi_a, hi_b, lo_a, lo_b, n_in_b, zb_in):
                dve.sem_inc(s, 1)

            def total(out, bank, fs):
                columns = bank[:, fs[0] * 2 * B:(fs[-1] + 1) * 2 * B]
                return dve.tensor_reduce(out, columns.rearrange("p (f e b) -> p f b e", e=2, b=B), AX.X, ALU.add)

            with dve.Fori(0, T // 2) as pair:
                for par in range(2):
                    i = pair * 2 + par
                    before, after = state[:, par], state[:, 1 - par]
                    dve.wait_ge(r_sum, i + 1)
                    total(r_in[:], r_bank, every).then_inc(r_in_ready, 1)
                    dve.wait_ge(na_sum, i + 1)
                    total(u[:, A], na_bank, first).then_inc(ua, 1)
                    dve.wait_ge(ua, i + 1)
                    dve.wait_ge(r_ready, i + 1)
                    dve.tensor_tensor(v[:, A], u[:, A], r[:, A], ALU.mult).then_inc(va, 1)
                    dve.wait_ge(va, i + 1)
                    dve.tensor_tensor(n_in[:, A], v[:, A], n_part(first), ALU.add).then_inc(n_in_a, 1)
                    dve.wait_ge(za_sum, i + 1)
                    total(z_in[:, A], za_bank, first).then_inc(za_in, 1)
                    dve.wait_ge(nb_sum, i + 1)
                    total(u[:, Z], nb_bank, second).then_inc(ub, 1)
                    dve.wait_ge(ub, i + 1)
                    dve.tensor_tensor(v[:, Z], u[:, Z], r[:, Z], ALU.mult).then_inc(vb, 1)
                    dve.wait_ge(n_a, i + 1)
                    dve.scalar_tensor_tensor(out=d[:, A], in0=n[:, A], scalar=HS, in1=before[:, A], op0=ALU.mult,
                                             op1=ALU.subtract).then_inc(da, 1)
                    dve.wait_ge(vb, i + 1)
                    dve.tensor_tensor(n_in[:, Z], v[:, Z], n_part(second), ALU.add).then_inc(n_in_b, 1)
                    dve.wait_ge(zb_sum, i + 1)
                    total(z_in[:, Z], zb_bank, second).then_inc(zb_in, 1)
                    dve.wait_ge(da, i + 1)
                    dve.wait_ge(keep_a, i + 1)
                    dve.tensor_tensor(e[:, A], d[:, A], keep[:, A], ALU.mult).then_inc(ea, 1)
                    dve.wait_ge(ea, i + 1)
                    dve.tensor_tensor(parts[:, A, 0:B], e[:, A], before[:, A], ALU.add).then_inc(hi_a, 1)
                    dve.wait_ge(n_b, i + 1)
                    dve.scalar_tensor_tensor(out=d[:, Z], in0=n[:, Z], scalar=HS, in1=before[:, Z], op0=ALU.mult,
                                             op1=ALU.subtract).then_inc(db, 1)
                    dve.tensor_tensor(after[:, A], e[:, A], before[:, A], ALU.add).then_inc(state_a, 1)
                    dve.wait_ge(db, i + 1)
                    dve.wait_ge(keep_b, i + 1)
                    dve.tensor_tensor(e[:, Z], d[:, Z], keep[:, Z], ALU.mult).then_inc(eb, 1)
                    dve.wait_ge(eb, i + 1)
                    dve.tensor_tensor(parts[:, Z, 0:B], e[:, Z], before[:, Z], ALU.add).then_inc(hi_b, 1)
                    dve.tensor_tensor(after[:, Z], e[:, Z], before[:, Z], ALU.add).then_inc(state_b, 1)
                    dve.wait_ge(hi_a, i + 2)
                    dve.wait_ge(state_a, i + 2)
                    dve.tensor_tensor(parts[:, A, B:2 * B], after[:, A], parts[:, A, 0:B], ALU.subtract)\
                       .then_inc(lo_a, 1)
                    dve.wait_ge(hi_b, i + 2)
                    dve.wait_ge(state_b, i + 2)
                    dve.tensor_tensor(parts[:, Z, B:2 * B], after[:, Z], parts[:, Z, 0:B], ALU.subtract)\
                       .then_inc(lo_b, 1)
            for w in range(NT):
                dve.wait_ge(back_turned, w + 1)
                dve.scalar_tensor_tensor(out=X[:, w, :], in0=turned[w % 2][:], scalar=1.0 / HS, in1=X[:, w, :],
                                         op0=ALU.mult, op1=ALU.add).then_inc(added, 1)


def dit_condition_phase(nc, const, a, store, mod, region, gates_dram, row_dram):
    with ExitStack() as ctx:
        m = Mem(nc, ctx, "ditcond_")
        w = m.sb("ada_w", [P, 6, KD, D])
        w_out = region[1][:].rearrange("p e (k n) -> p e k n", k=DIT_H)
        w_v = region[0][:].rearrange("p e (k n) -> p e k n", k=KD)
        c_T = m.sb("cond_T", [P, KD, B])
        b_row = m.sb("ada_b_row", [B, 6, D])
        row = m.sb("mod_row", [B, 6, D])
        bv = m.sb("bv", [P, 3 * DIT_H])
        bvh, bvl = m.sb("bv_hi", [P, DIT_H], F16), m.sb("bv_lo", [P, DIT_H], F16)
        ob = m.sb("ob", [1, D])
        col_sum = m.ps("col_sum", [P, 4, KD, B])
        row_sum = [m.ps(f"row_sum{i}", [P, D]) for i in range(7)]
        ada_loaded = [m.sem(f"ada_loaded_{i}") for i in range(6)]
        side_loaded, out_loaded, v_loaded = m.sem("side_loaded"), m.sem("out_loaded"), m.sem("v_loaded")
        cols_ready, rows_ready, bv_ready, mapped = (m.sem(s) for s in ("cols", "rows", "bv_ready", "mapped"))
        bvh_ready, row_ready, ob_ready, stored = (m.sem(s) for s in ("bvh_ready", "row_ready", "ob_ready", "stored"))
        block = ctx.enter_context(nc.Block())
        chunks = (1, 0, 4, 3, 2, 5)

        @block.sync
        def _(sp):
            sp.dma_start(c_T[:], a["cond_columns"]).then_inc(side_loaded, 16)
            rows = a["L3_cond_ada_b"].rearrange("(o j d) -> o j d", o=1, d=D).broadcast_to([B, 6, D])
            sp.dma_start(b_row[:], rows).then_inc(side_loaded, 16)
            sp.dma_start(bv[:], a["qkv_b_columns"]).then_inc(side_loaded, 16)
            sp.dma_start(ob[:], a["L3_cond_out_b"].rearrange("(o d) -> o d", o=1)).then_inc(side_loaded, 16)
            for i, j in enumerate(chunks):
                sp.dma_start(w[:, i], a["L3_cond_ada_w"].rearrange("(k p) n -> p k n", p=P)[:, :, j * D:(j + 1) * D])\
                  .then_inc(ada_loaded[i], 16)
            sp.dma_start(w_out, store.out).then_inc(out_loaded, 16)
            sp.dma_start(w_v, store.v).then_inc(v_loaded, 16)
            sp.wait_ge(row_ready, 6)
            sp.dma_start(gates_dram, row[:, 4:6, :]).then_inc(stored, 16)
            sp.wait_ge(ob_ready, 1)
            sp.dma_start(row_dram, ob[:]).then_inc(stored, 16)
            sp.wait_ge(stored, 32)
            sp.wait_ge(v_loaded, 16)

        @block.tensor
        def _(pe):
            pe.wait_ge(side_loaded, 64)
            for i in range(6):
                pe.wait_ge(ada_loaded[i], 16)
                for k in range(KD):
                    mm = pe.matmul(row_sum[i][0:B, :], c_T[:, k, :], w[:, i, k, :], start=(k == 0), stop=(k == KD - 1))
                mm.then_inc(rows_ready, 1)
            for i in range(4):
                pe.wait_ge(row_ready, i + 1)
                for f in range(KD):
                    mm = pe.transpose(col_sum[:, i, f, :], row[:, i, f * P:(f + 1) * P], const["ident"][0:B, 0:B])
            mm.then_inc(cols_ready, 1)
            pe.wait_ge(bv_ready, 1)
            pe.wait_ge(out_loaded, 16)
            for h in range(DIT_H):
                mm = products(pe, row_sum[6][0:1, :], (bvh[:, h:h + 1], bvl[:, h:h + 1]),
                              (w_out[:, 0, h, :], w_out[:, 1, h, :]), h == 0, h == DIT_H - 1)
            mm.then_inc(mapped, 1)

        @block.vector
        def _(dve):
            dve.wait_ge(side_loaded, 64)
            v = bv[:, 2 * DIT_H:3 * DIT_H]
            dve.tensor_scalar(bvh[:], v, XS, None, ALU.mult).then_inc(bvh_ready, 1)
            dve.wait_ge(bvh_ready, 1)
            dve.scalar_tensor_tensor(out=bvl[:], in0=v, scalar=XS, in1=bvh[:], op0=ALU.mult, op1=ALU.subtract)\
               .then_inc(bv_ready, 1)
            for i, j in enumerate(chunks):
                dve.wait_ge(rows_ready, i + 1)
                dve.tensor_tensor(row[:, i, :], row_sum[i][0:B, :], b_row[:, j, :], ALU.add).then_inc(row_ready, 1)
            dve.wait_ge(cols_ready, 1)
            for i in range(4):
                dve.tensor_scalar(mod[:, i], col_sum[:, i], 1.0 if i in (SCALE1, SCALE2) else 0.0, XS, ALU.add,
                                  ALU.mult)
            dve.wait_ge(mapped, 1)
            dve.scalar_tensor_tensor(out=ob[:], in0=row_sum[6][0:1, :], scalar=UNSCALE, in1=ob[:], op0=ALU.mult,
                                     op1=ALU.add).then_inc(ob_ready, 1)


def dit_phase(nc, const, a, store, mod, region, gates_dram, row_dram, x_in, out):
    H, DH = DIT_H, DIT_DH
    FT = MLP // P
    C = INNER // D
    with ExitStack() as ctx:
        m = Mem(nc, ctx, "dit_")
        X = m.sb("X", [P, TT, D])
        yh, yl = m.sb("yh", [P, KD, T], F16), m.sb("yl", [P, KD, T], F16)
        big = m.sb("big", [P, TT, INNER])
        O = big
        A = big[:, :, 0:D]
        xn = big[:, :, D:2 * D]
        y32 = big[:, :, 2 * D:3 * D]
        V = m.sb("V", [P, 2, TT, INNER], F16)
        hid = V[:].rearrange("p e t n -> p e (t n)").rearrange("p e (f t) -> p e f t", f=FT)
        qk = m.sb("qk", [P, 2, 2, 2, T], F16)
        oT = [[yh[:].rearrange("p k t -> p (k t)").rearrange("p (h q) -> p h q", h=H),
               yl[:].rearrange("p k t -> p (k t)").rearrange("p (h q) -> p h q", h=H)],
              [qk[:, 0].rearrange("p a e t -> p (a e t)").rearrange("p (h q) -> p h q", h=H),
               qk[:, 1].rearrange("p a e t -> p (a e t)").rearrange("p (h q) -> p h q", h=H)]]
        cut = lambda r, k: r[:].rearrange("p e (k n) -> p e k n", k=k)
        w_v, w_1 = cut(region[0], KD), cut(region[0], KD)
        w_out, w_2 = cut(region[1], H), cut(region[1], FT)
        w_qk = m.sb("w_qk", [P, 2, 2, 2, KD, DH], F16)
        gates = m.sb("gates", [P, 2, D])
        rows = m.sb("bias_rows", [P, 2, D])
        gb = m.sb("gated_bias", [P, 2, D])
        qk_b = m.sb("qk_b", [P, 3 * H])
        b_1 = m.sb("b_1", [P, FT])
        stats = m.sb("stats", [P, TT, 6])
        mv = m.sb("mv", [P, TT, 2])
        rstd = m.sb("rstd", [P, TT])
        bank = [m.ps(f"bank{i}", [P, D]) for i in range(8)]
        work = bank[4:8]

        wv_loaded, w1_loaded, wo_loaded, w2_loaded = (m.sem(s) for s in "wv_loaded w1_loaded wo_loaded w2_loaded".split())
        wqk_loaded = [m.sem(f"wqk_loaded_{i}") for i in range(2)]
        (stats_taken, params_loaded, x_loaded, gates_loaded, b_scaled, gated, a_begun, stats_ready, mv_ready, var_ready,
         root_done, rstd_ready, xn_ready, rows_turned, y_ready, yh_ready, yl_ready, v_sum, vh_ready, vl_ready,
         qk_sum, qk_hi, qk_lo, o_turned, oh_ready, ol_ready, att_sum, att_gated, a_ready, x_again, hid_sum, hid_ready,
         hh_ready, hl_ready, mlp_sum, mlp_gated, out_ready, stored) = (m.sem(s) for s in (
             "stats_taken params_loaded x_loaded gates_loaded b_scaled gated a_begun stats_ready mv_ready var_ready root_done "
             "rstd_ready xn_ready rows_turned y_ready yh_ready yl_ready v_sum vh_ready vl_ready qk_sum qk_hi qk_lo "
             "o_turned oh_ready ol_ready att_sum att_gated a_ready x_again hid_sum hid_ready hh_ready hl_ready "
             "mlp_sum mlp_gated out_ready stored").split())

        def scores(pe, s, h, t):
            for (qe, ke) in ((0, 0), (0, 1), (1, 0)):
                mm = pe.matmul(s, qk[:, hs.parity, 0, qe, t * P:(t + 1) * P], qk[:, hs.parity, 1, ke, :],
                               start=(qe + ke == 0), stop=(qe == 1))
            return mm

        hs = Heads(
            m, S=[bank[0][:], bank[1][:]], PT=[bank[2][:], bank[3][:]], O=[bank[4][:, 0:DH], bank[5][:, 0:DH]],
            ident=const["ident"][:], scores=scores,
            values=lambda h, s: (V[:, 0, s, at(h * DH, DH)], V[:, 1, s, at(h * DH, DH)]),
            out=lambda h, t: O[:, t, at(h * DH, DH)],
            scale=UNSCALE * UNSCALE * float(DH) ** -0.5, lag=3)
        gelu = hs.prob

        x_rows = x_in.rearrange("b (t p) d -> p b t d", p=P)
        o_rows = out.rearrange("b (t p) d -> p b t d", p=P)
        flat_head = lambda v: v.rearrange("p o a e k n -> p (o a) e k n")
        block = ctx.enter_context(nc.Block())

        @block.sync
        def _(sp):
            sp.dma_start(qk_b[:], a["qkv_b_columns"]).then_inc(params_loaded, 16)
            sp.dma_start(b_1[:], a["ffn_b1_columns"]).then_inc(params_loaded, 16)
            sp.dma_start(rows[:, 0, :], row_dram.broadcast_to([P, D])).then_inc(params_loaded, 16)
            sp.dma_start(rows[:, 1, :], a["L3_cond_ffn_b2"].rearrange("(o d) -> o d", o=1).broadcast_to([P, D]))\
              .then_inc(params_loaded, 16)
            sp.sem_inc(wv_loaded, 16)
            with sp.Fori(0, B) as b:
                def load_qk(h, parity):
                    sp.dma_start(w_qk[:, parity], flat_head(store.qk[:, at(h)])).then_inc(wqk_loaded[parity], 16)

                sp.wait_ge(stored, b * (16 * TT))
                sp.dma_start(X[:], x_rows[:, at(b), :, :].rearrange("p o t d -> p (o t) d")).then_inc(x_loaded, 16)
                sp.dma_start(gates[:], gates_dram[at(b), :, :].broadcast_to([P, 2, D])).then_inc(gates_loaded, 16)
                sp.wait_ge(qk_sum, b * (2 * H))
                load_qk(0, 0)
                load_qk(1, 1)
                sp.wait_ge(mlp_sum, b * TT)
                sp.dma_start(w_out, store.out).then_inc(wo_loaded, 16)
                sp.wait_ge(v_sum, (b + 1) * (TT * C))
                sp.dma_start(w_1, store.w1).then_inc(w1_loaded, 16)
                with sp.Fori(0, (H - 2) // 2) as pair:
                    for parity in range(2):
                        sp.wait_ge(qk_sum, b * (2 * H) + pair * 4 + (parity * 2 + 2))
                        load_qk(pair * 2 + (2 + parity), parity)
                sp.wait_ge(att_sum, (b + 1) * TT)
                sp.dma_start(w_2, store.w2).then_inc(w2_loaded, 16)
                sp.wait_ge(hid_sum, (b + 1) * FT)
                sp.dma_start(w_v, store.v).then_inc(wv_loaded, 16)
                for t in range(TT):
                    sp.wait_ge(out_ready, b * TT + t + 1)
                    sp.dma_start(o_rows[:, at(b), t, :], X[:, t, :]).then_inc(stored, 16)
            sp.wait_ge(wv_loaded, (B + 1) * 16)
            sp.wait_ge(stored, B * TT * 16)

        @block.gpsimd
        def _(pool):
            hs.credits(pool)
            pool.sem_inc(att_gated, 2)
            pool.sem_inc(mlp_gated, 2)
            pool.sem_inc(hl_ready, 2)
            pool.sem_inc(vl_ready, C)
            pool.wait_ge(params_loaded, 64)
            with pool.Fori(0, B) as b:
                pool.wait_ge(gates_loaded, (b + 1) * 16)
                pool.tensor_tensor(gb[:], gates[:], rows[:], ALU.mult).then_inc(gated, 1)
                pool.wait_ge(gated, b + 1)
                for t in range(TT):
                    pool.wait_ge(att_gated, b * TT + t + 3)
                    pool.tensor_tensor(A[:, t, :], A[:, t, :], gb[:, 0, :], ALU.add).then_inc(a_begun, 1)
                    pool.wait_ge(a_begun, b * TT + t + 1)
                    pool.tensor_tensor(A[:, t, :], A[:, t, :], X[:, t, :], ALU.add).then_inc(a_ready, 1)
                for t in range(TT):
                    pool.wait_ge(a_ready, b * TT + t + 1)
                    pool.tensor_tensor(X[:, t, :], A[:, t, :], X[:, t, :], ALU.add).then_inc(x_again, 1)
                    pool.wait_ge(x_again, (b * TT + t) * 2 + 1)
                    pool.tensor_tensor(X[:, t, :], X[:, t, :], gb[:, 1, :], ALU.add).then_inc(x_again, 1)

        @block.tensor
        def _(pe):
            pe.wait_ge(b_scaled, 1)
            with pe.Fori(0, B) as b:
                def turn_rows(n):
                    pe.wait_ge(xn_ready, n * TT + TT)
                    for k in range(KD):
                        for t in range(TT):
                            mm = pe.transpose(bank[k][:, t * P:(t + 1) * P], xn[:, t, k * P:(k + 1) * P],
                                              const["ident"][:])
                        mm.then_inc(rows_turned, 1)

                pe.wait_ge(wv_loaded, (b + 1) * 16)
                turn_rows(b * 2)
                with pe.Fori(0, TT) as t:
                    pe.wait_ge(yl_ready, b * (2 * KD) + KD)
                    for c in range(C):
                        pe.wait_ge(vl_ready, b * (TT * C) + t * C + (c + 1))
                        for k in range(KD):
                            w = lambda e: w_v[:, e, k, c * D:(c + 1) * D]
                            mm = products(pe, work[c][:], (yh[:, k, at(t * P, P)], yl[:, k, at(t * P, P)]),
                                          (w(0), w(1)), k == 0, k == KD - 1)
                        mm.then_inc(v_sum, 1)
                pe.wait_ge(vl_ready, (b + 1) * (TT * C) + C)

                def project(h, i, parity, nth):
                    if i == 0:
                        pe.wait_ge(wqk_loaded[parity], b * (16 * (H // 2)) + nth * 16)
                    for k in range(KD):
                        w = lambda e: w_qk[:, parity, i, e, k, :]
                        mm = products(pe, work[2 + i][:], (w(0), w(1)), (yh[:, k, :], yl[:, k, :]), k == 0,
                                      k == KD - 1)
                    mm.then_inc(qk_sum, 1)

                project(0, 0, 0, 1)
                project(0, 1, 0, 1)

                def current(h, t, u):
                    if t == 0:
                        pe.wait_ge(qk_lo, b * (2 * H) + h * 2 + 2)
                    hs.pe_scores(pe, h, t, u)

                def beside(h, t, last):
                    if t in (1, 2) and not last:
                        project(h + 1, t - 1, 1 - hs.parity, hs.nth)

                hs.run(pe, H, b * (H * TT), current, lambda h, t, u: hs.pe_turn(pe, t, u),
                       lambda h, t, u: hs.pe_values(pe, h, t, u), beside)

                def project_out(t):
                    pe.wait_ge(ol_ready, b * (4 * TT) + 4 * t + 4)
                    pe.wait_ge(att_gated, b * TT + t + 1)
                    for h in range(H):
                        mm = products(pe, work[t % 2][:], (oT[t % 2][0][:, h, :], oT[t % 2][1][:, h, :]),
                                      (w_out[:, 0, h, :], w_out[:, 1, h, :]), h == 0, h == H - 1)
                    mm.then_inc(att_sum, 1)

                pe.wait_ge(hs.out_copied, (b + 1) * (H * TT) + hs.CREDIT)
                pe.wait_ge(wo_loaded, (b + 1) * 16)
                for t in range(TT):
                    for q in range(4):
                        if t >= 1:
                            pe.wait_ge(ol_ready, b * (4 * TT) + 4 * (t - 1) + q + 1)
                        for h in range(4):
                            mm = pe.transpose(bank[q][:, h * P:(h + 1) * P],
                                              O[:, t, (4 * q + h) * P:(4 * q + h + 1) * P], const["ident"][:])
                        mm.then_inc(o_turned, 1)
                    if t >= 1:
                        project_out(t - 1)
                project_out(TT - 1)
                pe.wait_ge(w1_loaded, (b + 1) * 16)
                turn_rows(b * 2 + 1)
                with pe.Fori(0, FT // 4) as g:
                    pe.wait_ge(yl_ready, (b + 1) * (2 * KD))
                    for j in range(4):
                        pe.wait_ge(hid_ready, b * FT + g * 4 + (j + 1))
                        for k in range(KD):
                            w = lambda e: w_1[:, e, k, at(g * (4 * P) + j * P, P)]
                            mm = products(pe, work[j][:], (w(0), w(1)), (yh[:, k, :], yl[:, k, :]), k == 0,
                                          k == KD - 1)
                        mm.then_inc(hid_sum, 1)
                with pe.Fori(0, TT // 2) as g:
                    pe.wait_ge(hl_ready, (b + 1) * FT + 2)
                    pe.wait_ge(w2_loaded, (b + 1) * 16)
                    for j in range(2):
                        pe.wait_ge(mlp_gated, b * TT + g * 2 + (j + 1))
                        for f in range(FT):
                            left = lambda e: hid[:, e, f, at(g * (2 * P) + j * P, P)]
                            mm = products(pe, work[j][:], (left(0), left(1)), (w_2[:, 0, f, :], w_2[:, 1, f, :]),
                                          f == 0, f == FT - 1)
                        mm.then_inc(mlp_sum, 1)

        @block.scalar
        def _(act):
            act.wait_ge(b_scaled, 1)
            act.sem_inc(hid_ready, 4)
            with act.Fori(0, B) as b:
                def parts_of_rows(n):
                    act.wait_ge(var_ready, n + 1)
                    act.activation(rstd[:], mv[:, :, 1], ACT.Sqrt).then_inc(root_done, 1)
                    for k in range(KD):
                        act.wait_ge(y_ready, n * KD + k + 1)
                        act.activation(yh[:, k, :], y32[:, k, :], ACT.Copy).then_inc(yh_ready, 1)

                parts_of_rows(b * 2)
                with act.Fori(0, TT) as t:
                    for c in range(C):
                        act.wait_ge(v_sum, b * (TT * C) + t * C + (c + 1))
                        act.activation(V[:, 0, at(t), c * D:(c + 1) * D].rearrange("p o n -> p (o n)"), work[c][:],
                                       ACT.Copy).then_inc(vh_ready, 1)
                act.preload_act_table(ACT.Exp)

                def take(h, i, parity):
                    act.wait_ge(qk_sum, b * (2 * H) + h * 2 + (i + 1))
                    act.activation(qk[:, parity, i, 0, :], work[2 + i][:], ACT.Identity,
                                   bias=qk_b[:, at(h + i * H)]).then_inc(qk_hi, 1)

                take(0, 0, 0)
                take(0, 1, 0)

                def beside(h, t, last):
                    if t in (2, 3) and not last:
                        take(h + 1, t - 2, 1 - hs.parity)

                hs.run(act, H, b * (H * TT), lambda h, t, u: hs.act_exp(act, t, u),
                       lambda h, t, u: hs.act_copy(act, t, u), lambda h, t, u: None, beside)
                for t in range(TT):
                    for q in range(4):
                        act.wait_ge(o_turned, b * (4 * TT) + 4 * t + q + 1)
                        if t >= 2:
                            act.wait_ge(att_sum, b * TT + t - 1)
                        act.activation(oT[t % 2][0][:, 4 * q:4 * q + 4, :].rearrange("p h q -> p (h q)"),
                                       bank[q][:], ACT.Copy, scale=XS * UNSCALE).then_inc(oh_ready, 1)
                parts_of_rows(b * 2 + 1)
                act.preload_act_table(ACT.Gelu)
                with act.Fori(0, FT // 4) as g:
                    for j in range(4):
                        n = b * FT + g * 4 + j
                        act.wait_ge(hid_sum, n + 1)
                        act.wait_ge(hl_ready, n + 1)
                        act.activation(gelu[:, j % 2, :], work[j][:], ACT.Gelu, bias=b_1[:, at(g * 4 + j)],
                                       scale=UNSCALE).then_inc(hid_ready, 1)
                        act.wait_ge(hid_ready, n + 5)
                        act.activation(flat(hid[:, 0, at(g * 4 + j), :]), gelu[:, j % 2, :], ACT.Copy, scale=XS)\
                           .then_inc(hh_ready, 1)

        @block.vector
        def _(dve):
            dve.wait_ge(params_loaded, 64)
            dve.tensor_scalar(qk_b[:], qk_b[:], XS * WS, None, ALU.mult).then_inc(b_scaled, 1)
            dve.wait_ge(b_scaled, 1)
            with dve.Fori(0, B) as b:
                def norm(n, src, ready, scale, shift):
                    for t in range(TT):
                        ready(t)
                        dve.bn_stats(stats[:, t, :], src[:, t, :]).then_inc(stats_ready, 1)
                    dve.wait_ge(stats_ready, (n + 1) * TT)
                    dve.sem_inc(stats_taken, 1)
                    for t in range(TT):
                        dve.bn_aggr(mv[:, t, :], stats[:, t, :]).then_inc(mv_ready, 1)
                    dve.wait_ge(mv_ready, (n + 1) * TT)
                    dve.tensor_scalar(mv[:, :, 1], mv[:, :, 1], DIT_EPS, None, ALU.add).then_inc(var_ready, 1)
                    dve.wait_ge(root_done, n + 1)
                    dve.reciprocal(rstd[:], rstd[:]).then_inc(rstd_ready, 1)
                    dve.wait_ge(rstd_ready, n + 1)
                    for t in range(TT):
                        dve.tensor_scalar(xn[:, t, :], src[:, t, :], mv[:, t, 0:1], rstd[:, t:t + 1], ALU.subtract,
                                          ALU.mult).then_inc(xn_ready, 1)
                    for k in range(KD):
                        dve.wait_ge(rows_turned, n * KD + k + 1)
                        dve.tensor_scalar(y32[:, k, :], bank[k][:], mod[:, scale, k, at(b)], mod[:, shift, k, at(b)],
                                          ALU.mult, ALU.add).then_inc(y_ready, 1)
                    for k in range(KD):
                        dve.wait_ge(yh_ready, n * KD + k + 1)
                        dve.tensor_tensor(yl[:, k, :], y32[:, k, :], yh[:, k, :], ALU.subtract).then_inc(yl_ready, 1)

                norm(b * 2, X, lambda t: dve.wait_ge(x_loaded, (b + 1) * 16) if t == 0 else None, SCALE1, SHIFT1)
                with dve.Fori(0, TT) as t:
                    for c in range(C):
                        dve.wait_ge(vh_ready, b * (TT * C) + t * C + (c + 1))
                        cols = slice(c * D, (c + 1) * D)
                        dve.tensor_tensor(flat(V[:, 1, at(t), cols]), work[c][:], flat(V[:, 0, at(t), cols]),
                                          ALU.subtract).then_inc(vl_ready, 1)

                def take(h, i, parity):
                    dve.wait_ge(qk_hi, b * (2 * H) + h * 2 + (i + 1))
                    dve.scalar_tensor_tensor(out=qk[:, parity, i, 1, :], in0=work[2 + i][:],
                                             scalar=qk_b[:, at(h + i * H)], in1=qk[:, parity, i, 0, :],
                                             op0=ALU.add, op1=ALU.subtract).then_inc(qk_lo, 1)

                take(0, 0, 0)
                take(0, 1, 0)

                def beside(h, t, last):
                    if t in (2, 3) and not last:
                        take(h + 1, t - 2, 1 - hs.parity)

                hs.run(dve, H, b * (H * TT), lambda h, t, u: hs.dve_max(dve, t, u),
                       lambda h, t, u: hs.dve_copy(dve, t, u), lambda h, t, u: hs.dve_out(dve, h, t, u), beside,
                       turn_lag=2)

                def gate_attention(t):
                    dve.wait_ge(att_sum, b * TT + t + 1)
                    dve.wait_ge(gates_loaded, (b + 1) * 16)
                    dve.scalar_tensor_tensor(out=A[:, t, :], in0=work[t % 2][:], scalar=UNSCALE, in1=gates[:, 0, :],
                                             op0=ALU.mult, op1=ALU.mult).then_inc(att_gated, 1)

                for t in range(TT):
                    for q in range(4):
                        dve.wait_ge(oh_ready, b * (4 * TT) + 4 * t + q + 1)
                        part = lambda e: oT[t % 2][e][:, 4 * q:4 * q + 4, :].rearrange("p h q -> p (h q)")
                        dve.scalar_tensor_tensor(out=part(1), in0=bank[q][:], scalar=XS * UNSCALE, in1=part(0),
                                                 op0=ALU.mult, op1=ALU.subtract).then_inc(ol_ready, 1)
                    if t >= 1:
                        gate_attention(t - 1)
                gate_attention(TT - 1)
                norm(b * 2 + 1, A, lambda t: dve.wait_ge(a_ready, b * TT + t + 1), SCALE2, SHIFT2)
                with dve.Fori(0, FT // 4) as g:
                    for j in range(4):
                        n = b * FT + g * 4 + j
                        dve.wait_ge(hh_ready, n + 1)
                        dve.scalar_tensor_tensor(out=flat(hid[:, 1, at(g * 4 + j), :]), in0=gelu[:, j % 2, :],
                                                 scalar=XS, in1=flat(hid[:, 0, at(g * 4 + j), :]), op0=ALU.mult,
                                                 op1=ALU.subtract).then_inc(hl_ready, 1)
                for t in range(TT):
                    dve.wait_ge(mlp_sum, b * TT + t + 1)
                    if t >= 2:
                        dve.wait_ge(out_ready, b * TT + t - 1)
                    dve.scalar_tensor_tensor(out=gelu[:, t % 2, :], in0=work[t % 2][:], scalar=UNSCALE,
                                             in1=gates[:, 1, :], op0=ALU.mult, op1=ALU.mult).then_inc(mlp_gated, 1)
                    dve.wait_ge(mlp_gated, b * TT + t + 3)
                    dve.wait_ge(x_again, (b * TT + t) * 2 + 2)
                    dve.tensor_tensor(X[:, t, :], X[:, t, :], gelu[:, t % 2, :], ALU.add).then_inc(out_ready, 1)


def program(nc, a, out):
    rows = lambda w: w.rearrange("(k p) n -> p k n", p=P)
    x_gru = nc.dram_tensor("x_gru", (B, T, D), F32, kind="Internal").ap()
    store = WeightStore(nc, a)
    gates_dram = nc.dram_tensor("gates", (B, 2, D), F32, kind="Internal").ap()
    row_dram = nc.dram_tensor("out_bias_row", (1, D), F32, kind="Internal").ap()

    def parts(ctx, name, k, n):
        return [Mem(nc, ctx).sb(f"{name}_{e}", [P, k, n], F16) for e in ("hi", "lo")]

    with ExitStack() as ctx:
        m = Mem(nc, ctx)
        const = {
            "ones16": m.sb("ones16", [P, P], F16),
            "ones32": m.sb("ones32", [P, P]),
            "below": m.sb("below", [P, P]),
            "ident": m.sb("ident", [P, P]),
            "ident16": m.sb("ident16", [P, P], F16),
        }
        made = m.sem("const_made")
        with nc.Block() as block:
            @block.gpsimd
            def _(pool):
                pool.memset(const["ones16"][:], 1.0).then_inc(made, 1)
                pool.memset(const["ones32"][:], 1.0).then_inc(made, 1)
                pool.wait_ge(made, 2)
                pool.affine_select(out=const["below"][:], in_=const["ones32"][:], compare_op=ALU.is_gt, fill=0.0,
                                   base=0, pattern=[[1, P]], channel_multiplier=-1)
                pool.affine_select(out=const["ident"][:], in_=const["ones32"][:], compare_op=ALU.is_equal, fill=0.0,
                                   base=0, pattern=[[1, P]], channel_multiplier=-1)
                pool.affine_select(out=const["ident16"][:], in_=const["ones16"][:], compare_op=ALU.is_equal,
                                   fill=0.0, base=0, pattern=[[1, P]], channel_multiplier=-1)

        with ExitStack() as inner:
            X = Mem(nc, inner).sb("X", [P, NT, D])
            with ExitStack() as weights:
                w_qkv, w_out = parts(weights, "small_qkv", KD, 3 * D), parts(weights, "small_out", KD, D)
                topk_phase(nc, X, const, a["x"], a["side_columns"], a["cond_2048"],
                           [(rows(a["L1_cond_W_qkv"]), w_qkv[0][:], w_qkv[1][:], WS),
                            (rows(a["L1_cond_W_out"]), w_out[0][:], w_out[1][:], WS)])
                small_attention_phase(nc, X, const, a, w_qkv, w_out)
            with ExitStack() as weights:
                gi = Mem(nc, weights).sb("gi", [P, 2, 3 * KD, B, T], F16)
                w_hh = parts(weights, "w_hh", KD, 3 * D)
                with ExitStack() as deeper:
                    w_ih = parts(deeper, "w_ih", KD, 3 * D)
                    split_weights(nc, "gru_", [(rows(a["L2_cond_W_ih"]), w_ih[0][:], w_ih[1][:], WS),
                                               (rows(a["L2_cond_W_hh"]), w_hh[0][:], w_hh[1][:], RS)])
                    gate_input_phase(nc, X, const, a, w_ih, gi)
                gru_phase(nc, X, const, a, w_hh, gi, x_gru, store)

        mod = m.sb("dit_mod", [P, 4, KD, B])
        region = [m.sb(f"weights{i}", [P, 2, KD * INNER], F16) for i in range(2)]
        dit_condition_phase(nc, const, a, store, mod, region, gates_dram, row_dram)
        dit_phase(nc, const, a, store, mod, region, gates_dram, row_dram, x_gru, out)


def kernel(**inputs):
    import numpy as np
    import concourse.bacc as bacc
    from concourse.bass_utils import run_bass_kernel_spmd

    nc = bacc.Bacc("TRN2", target_bir_lowering=False, num_devices=1)
    given = {k: np.asarray(v) for k, v in inputs.items()}
    given["side_columns"] = given["fside_BxSx1_0"].reshape(NT, P).T
    columns = lambda v: v.reshape(-1, P).T
    given["cond_columns"] = given["cond_2048"].reshape(B, KD, P).transpose(2, 1, 0)
    given["b_emb_columns"] = columns(given["L1_cond_b_emb"])
    given["b_ih_columns"] = columns(given["L2_cond_b_ih"])
    given["b_hh_columns"] = columns(given["L2_cond_b_hh"])
    given["qkv_b_columns"] = columns(given["L3_cond_qkv_b"])
    given["ffn_b1_columns"] = columns(given["L3_cond_ffn_b1"])
    given["g_norm_columns"] = columns(given["L1_cond_g_norm"])
    arrays = {f"in_{k}": np.ascontiguousarray(v) for k, v in given.items()}
    args = {k: nc.dram_tensor(f"in_{k}", arrays[f"in_{k}"].shape, mybir.dt.from_np(arrays[f"in_{k}"].dtype),
                              kind="ExternalInput").ap() for k in given}
    out = nc.dram_tensor("out", (B, T, D), F32, kind="ExternalOutput").ap()
    program(nc, args, out)
    r = run_bass_kernel_spmd(nc, [arrays], core_ids=[0])
    return r.results[0]["out"]
```
